# Optimizing a Trainium2 kernel written in Bass

```python
import numpy as np
import jax
import jax.numpy as jnp

def _softmax(x, axis=-1):
    return jax.nn.softmax(x, axis=axis)

def _gelu(x):
    return jax.nn.gelu(x, approximate=True)

def _silu(x):
    return jax.nn.silu(x)

def _sigmoid(x):
    return jax.nn.sigmoid(x)

def _layernorm(x, axis=-1, eps=1e-05):
    m = jnp.mean(x, axis=axis, keepdims=True)
    v = jnp.var(x, axis=axis, keepdims=True)
    return (x - m) / jnp.sqrt(v + eps)

def _scatter_add(tgt, idx, src, axis=0):
    return tgt.at[idx].add(src)

def _segment_sum(src, seg, n):
    return jax.ops.segment_sum(src, seg, n)
kernel_name = 'mk_adaln_d2_jaxref_r8_d7e0b1'

def setup_inputs(seed: int=0):
    np.random.seed(seed)
    _w = jnp.asarray

    def _L0_attn_setup():
        import jax, jax.numpy as jnp
        import numpy as np
        D_MODEL = 128
        N_HEADS = 16
        HEAD_DIM = D_MODEL // N_HEADS
        KV_LATENT = 32
        LN_EPS = 1e-05

        def apply_rope(x):
            b, h, t, d = x.shape
            half = d // 2
            pos = jnp.arange(t, dtype=x.dtype)[:, None]
            inv_freq = 1.0 / 10000.0 ** (jnp.arange(half, dtype=x.dtype) / half)
            angles = pos * inv_freq[None, :]
            sin = jnp.sin(angles)[None, None]
            cos = jnp.cos(angles)[None, None]
            x1, x2 = (x[..., :half], x[..., half:])
            return jnp.concatenate([x1 * cos - x2 * sin, x1 * sin + x2 * cos], axis=-1)
        key = jax.random.key(seed)
        ks = jax.random.split(key, 6)
        d, L = (D_MODEL, KV_LATENT)
        s = 1.0 / np.sqrt(d)
        sl = 1.0 / np.sqrt(L)
        return {'x': jax.random.normal(ks[0], (2, 256, d), dtype=jnp.float32), 'W_q': jax.random.uniform(ks[1], (d, d), jnp.float32, -s, s), 'W_dkv': jax.random.uniform(ks[2], (d, L), jnp.float32, -s, s), 'W_uk': jax.random.uniform(ks[3], (L, d), jnp.float32, -sl, sl), 'W_uv': jax.random.uniform(ks[4], (L, d), jnp.float32, -sl, sl), 'W_o': jax.random.uniform(ks[5], (d, d), jnp.float32, -s, s), 'ln_gamma': jnp.ones((L,), jnp.float32), 'ln_beta': jnp.zeros((L,), jnp.float32)}
    _L0_attn_in = _L0_attn_setup()

    def _L0_ffn_setup():
        import jax, jax.numpy as jnp
        import numpy as np
        B, T, D, FF, E, TOP_K = (8, 256, 128, 512, 8, 2)
        key = jax.random.key(seed)
        kx, kr, k1, k2 = jax.random.split(key, 4)
        x = jax.random.normal(kx, (B, T, D), dtype=jnp.float32)
        Wr = jax.random.normal(kr, (E, D), dtype=jnp.float32) * 0.02
        W1 = jax.random.normal(k1, (E, D, FF), dtype=jnp.float32) * 0.02
        W2 = jax.random.normal(k2, (E, FF, D), dtype=jnp.float32) * 0.02
        return {'x': x, 'Wr': Wr, 'W1': W1, 'W2': W2}
    _L0_ffn_in = _L0_ffn_setup()
    _L0_c = _w((lambda *s: np.random.randn(*s).astype(np.float32) * 0.05)(1, 128))
    _L0_wmod = _w((lambda *s: np.random.randn(*s).astype(np.float32) * 0.05)(128, 6 * 128) * 128 ** (-0.5))

    def _L1_attn_setup():
        import jax, jax.numpy as jnp
        import numpy as np
        B, S, E, H = (4, 256, 128, 16)
        HD = E // H
        key = jax.random.key(seed)
        k_x, k_q, k_k, k_v, k_o = jax.random.split(key, 5)
        scale = 0.02
        x = jax.random.normal(k_x, (B, S, E), dtype=jnp.float32)
        Wq = jax.random.normal(k_q, (H, HD, HD), dtype=jnp.float32) * scale
        Wk = jax.random.normal(k_k, (H, HD, HD), dtype=jnp.float32) * scale
        Wv = jax.random.normal(k_v, (H, HD, HD), dtype=jnp.float32) * scale
        Wo = jax.random.normal(k_o, (E, E), dtype=jnp.float32) * scale
        return {'x': x, 'Wq': Wq, 'Wk': Wk, 'Wv': Wv, 'Wo': Wo}
    _L1_attn_in = _L1_attn_setup()

    def _L1_ffn_setup():
        import jax, jax.numpy as jnp
        import numpy as np
        TOP_K = 2

        def _ffn(x, gw, uw, dw):
            return jax.nn.silu(x @ gw.T) * (x @ uw.T) @ dw.T
        key = jax.random.key(seed)
        ks = jax.random.split(key, 8)
        w = lambda k, shape: jax.random.normal(k, shape, jnp.float32) * 0.02
        return dict(x=jax.random.normal(ks[0], (4, 256, 128), jnp.float32), gate_w=w(ks[1], (8, 128)), expert_gate=w(ks[2], (8, 352, 128)), expert_up=w(ks[3], (8, 352, 128)), expert_down=w(ks[4], (8, 128, 352)), shared_gate=w(ks[5], (352, 128)), shared_up=w(ks[6], (352, 128)), shared_down=w(ks[7], (128, 352)))
    _L1_ffn_in = _L1_ffn_setup()
    _L1_c = _w((lambda *s: np.random.randn(*s).astype(np.float32) * 0.05)(1, 128))
    _L1_wmod = _w((lambda *s: np.random.randn(*s).astype(np.float32) * 0.05)(128, 6 * 128) * 128 ** (-0.5))
    _d = {'L0_attn_x': _L0_attn_in['x'], 'L0_attn_W_q': _L0_attn_in['W_q'], 'L0_attn_W_dkv': _L0_attn_in['W_dkv'], 'L0_attn_W_uk': _L0_attn_in['W_uk'], 'L0_attn_W_uv': _L0_attn_in['W_uv'], 'L0_attn_W_o': _L0_attn_in['W_o'], 'L0_attn_ln_gamma': _L0_attn_in['ln_gamma'], 'L0_attn_ln_beta': _L0_attn_in['ln_beta'], 'L0_ffn_Wr': _L0_ffn_in['Wr'], 'L0_ffn_W1': _L0_ffn_in['W1'], 'L0_ffn_W2': _L0_ffn_in['W2'], 'L0_c': _L0_c, 'L0_wmod': _L0_wmod, 'L1_attn_Wq': _L1_attn_in['Wq'], 'L1_attn_Wk': _L1_attn_in['Wk'], 'L1_attn_Wv': _L1_attn_in['Wv'], 'L1_attn_Wo': _L1_attn_in['Wo'], 'L1_ffn_gate_w': _L1_ffn_in['gate_w'], 'L1_ffn_expert_gate': _L1_ffn_in['expert_gate'], 'L1_ffn_expert_up': _L1_ffn_in['expert_up'], 'L1_ffn_expert_down': _L1_ffn_in['expert_down'], 'L1_ffn_shared_gate': _L1_ffn_in['shared_gate'], 'L1_ffn_shared_up': _L1_ffn_in['shared_up'], 'L1_ffn_shared_down': _L1_ffn_in['shared_down'], 'L1_c': _L1_c, 'L1_wmod': _L1_wmod}
    _x0 = _d['L0_attn_x']
    _d['L0_attn_x'] = jax.random.normal(jax.random.fold_in(jax.random.key(seed), 1), (1, 2048, 128), dtype=_x0.dtype)
    del _x0
    return _d

def reference(L0_attn_x, L0_attn_W_q, L0_attn_W_dkv, L0_attn_W_uk, L0_attn_W_uv, L0_attn_W_o, L0_attn_ln_gamma, L0_attn_ln_beta, L0_ffn_Wr, L0_ffn_W1, L0_ffn_W2, L0_c, L0_wmod, L1_attn_Wq, L1_attn_Wk, L1_attn_Wv, L1_attn_Wo, L1_ffn_gate_w, L1_ffn_expert_gate, L1_ffn_expert_up, L1_ffn_expert_down, L1_ffn_shared_gate, L1_ffn_shared_up, L1_ffn_shared_down, L1_c, L1_wmod):

    def _L0_attn_ref(x, W_q, W_dkv, W_uk, W_uv, W_o, ln_gamma, ln_beta):
        import jax, jax.numpy as jnp
        import numpy as np
        D_MODEL = 128
        N_HEADS = 16
        HEAD_DIM = D_MODEL // N_HEADS
        KV_LATENT = 32
        LN_EPS = 1e-05

        def apply_rope(x):
            b, h, t, d = x.shape
            half = d // 2
            pos = jnp.arange(t, dtype=x.dtype)[:, None]
            inv_freq = 1.0 / 10000.0 ** (jnp.arange(half, dtype=x.dtype) / half)
            angles = pos * inv_freq[None, :]
            sin = jnp.sin(angles)[None, None]
            cos = jnp.cos(angles)[None, None]
            x1, x2 = (x[..., :half], x[..., half:])
            return jnp.concatenate([x1 * cos - x2 * sin, x1 * sin + x2 * cos], axis=-1)
        b, t, _ = x.shape
        q = (x @ W_q).reshape(b, t, N_HEADS, HEAD_DIM).transpose(0, 2, 1, 3)
        lat = x @ W_dkv
        mu = jnp.mean(lat, axis=-1, keepdims=True)
        var = jnp.mean(jnp.square(lat - mu), axis=-1, keepdims=True)
        lat = (lat - mu) * jax.lax.rsqrt(var + LN_EPS) * ln_gamma + ln_beta
        k = (lat @ W_uk).reshape(b, t, N_HEADS, HEAD_DIM).transpose(0, 2, 1, 3)
        v = (lat @ W_uv).reshape(b, t, N_HEADS, HEAD_DIM).transpose(0, 2, 1, 3)
        q = apply_rope(q)
        k = apply_rope(k)
        scores = jnp.einsum('bhqd,bhkd->bhqk', q, k) / jnp.sqrt(jnp.float32(HEAD_DIM))
        causal = jnp.tril(jnp.ones((t, t), dtype=bool))
        scores = jnp.where(causal[None, None], scores, -jnp.inf)
        attn = jax.nn.softmax(scores, axis=-1)
        out = jnp.einsum('bhqk,bhkd->bhqd', attn, v)
        out = out.transpose(0, 2, 1, 3).reshape(b, t, D_MODEL)
        return out @ W_o

    def _L0_ffn_ref(x, Wr, W1, W2):
        import jax, jax.numpy as jnp
        import numpy as np
        B, T, D, FF, E, TOP_K = (8, 256, 128, 512, 8, 2)
        Bs, Ts, Ds = x.shape
        Ne = Wr.shape[0]
        xf = x.reshape(-1, Ds)
        N = xf.shape[0]
        logits = xf @ Wr.T
        topk_vals, topk_idx = jax.lax.top_k(logits, TOP_K)
        w = jax.nn.softmax(topk_vals.astype(jnp.float32), axis=-1).astype(x.dtype)
        idx_flat = topk_idx.reshape(-1)
        w_flat = w.reshape(-1)
        sort_idx = jnp.argsort(idx_flat)
        rev = sort_idx // TOP_K
        sw = w_flat[sort_idx]
        perm = xf[rev]
        S = perm.shape[0]
        chunks = perm.reshape(Ne, S // Ne, Ds)
        h = jax.nn.gelu(jnp.einsum('ecd,edf->ecf', chunks, W1), approximate=False)
        eo = jnp.einsum('ecf,efd->ecd', h, W2).reshape(S, Ds)
        out = jnp.zeros((N, Ds), dtype=x.dtype).at[rev].add(eo * sw[:, None])
        return out.reshape(Bs, Ts, Ds)

    def _L1_attn_ref(x, Wq, Wk, Wv, Wo):
        import jax, jax.numpy as jnp
        import numpy as np
        B, S, E, H = (4, 256, 128, 16)
        HD = E // H
        b, s, e = x.shape
        xh = x.reshape(b, s, H, HD)
        q = jnp.einsum('bshd,hde->bshe', xh, Wq)
        k = jnp.einsum('bshd,hde->bshe', xh, Wk)
        v = jnp.einsum('bshd,hde->bshe', xh, Wv)
        scores = jnp.einsum('bqhd,bkhd->bhqk', q, k) / jnp.sqrt(jnp.float32(HD))
        causal = jnp.tril(jnp.ones((s, s), dtype=bool))
        scores = jnp.where(causal, scores, jnp.float32(-jnp.inf))
        attn = jax.nn.softmax(scores.astype(jnp.float32), axis=-1)
        out = jnp.einsum('bhqk,bkhd->bqhd', attn, v)
        out = out.reshape(b, s, e)
        return jnp.einsum('bse,ef->bsf', out, Wo)

    def _L1_ffn_ref(x, gate_w, expert_gate, expert_up, expert_down, shared_gate, shared_up, shared_down):
        import jax, jax.numpy as jnp
        import numpy as np
        TOP_K = 2

        def _ffn(x, gw, uw, dw):
            return jax.nn.silu(x @ gw.T) * (x @ uw.T) @ dw.T
        B, S, H = x.shape
        xf = x.reshape(-1, H)
        T = xf.shape[0]
        E = expert_gate.shape[0]
        shared = _ffn(xf, shared_gate, shared_up, shared_down)
        logits = xf @ gate_w.T
        probs = jax.nn.softmax(logits, axis=-1)
        topw, topi = jax.lax.top_k(probs, TOP_K)
        topw = topw / (topw.sum(-1, keepdims=True) + 1e-20)
        comb = jnp.zeros((T, E), xf.dtype).at[jnp.arange(T)[:, None], topi].add(topw)

        def body(acc, ws):
            gw, uw, dw, wcol = ws
            return (acc + _ffn(xf, gw, uw, dw) * wcol[:, None], None)
        routed, _ = jax.lax.scan(body, jnp.zeros_like(xf), (expert_gate, expert_up, expert_down, comb.T))
        return (shared + routed).reshape(B, S, H)
    x = L0_attn_x
    mod = (_silu(L0_c) @ L0_wmod).reshape(L0_c.shape[0], 6, 1, -1)
    sa, ca, ga, sb, cb, gb = (mod[:, 0], mod[:, 1], mod[:, 2], mod[:, 3], mod[:, 4], mod[:, 5])
    ga = (2 * (ga >= 0) - 1) * jnp.maximum(jnp.abs(ga), 0.25)
    gb = (2 * (gb >= 0) - 1) * jnp.maximum(jnp.abs(gb), 0.25)
    h = _layernorm(x, axis=-1) * (1 + ca) + sa
    x = x + ga * _L0_attn_ref(h, L0_attn_W_q, L0_attn_W_dkv, L0_attn_W_uk, L0_attn_W_uv, L0_attn_W_o, L0_attn_ln_gamma, L0_attn_ln_beta)
    h = _layernorm(x, axis=-1) * (1 + cb) + sb
    x = x + gb * _L0_ffn_ref(h, L0_ffn_Wr, L0_ffn_W1, L0_ffn_W2)
    mod = (_silu(L1_c) @ L1_wmod).reshape(L1_c.shape[0], 6, 1, -1)
    sa, ca, ga, sb, cb, gb = (mod[:, 0], mod[:, 1], mod[:, 2], mod[:, 3], mod[:, 4], mod[:, 5])
    ga = (2 * (ga >= 0) - 1) * jnp.maximum(jnp.abs(ga), 0.25)
    gb = (2 * (gb >= 0) - 1) * jnp.maximum(jnp.abs(gb), 0.25)
    h = _layernorm(x, axis=-1) * (1 + ca) + sa
    x = x + ga * _L1_attn_ref(h, L1_attn_Wq, L1_attn_Wk, L1_attn_Wv, L1_attn_Wo)
    h = _layernorm(x, axis=-1) * (1 + cb) + sb
    x = x + gb * _L1_ffn_ref(h, L1_ffn_gate_w, L1_ffn_expert_gate, L1_ffn_expert_up, L1_ffn_expert_down, L1_ffn_shared_gate, L1_ffn_shared_up, L1_ffn_shared_down)
    return x

_drawn_inputs = setup_inputs


def setup_inputs(seed=0):
    import zlib

    import numpy as np

    out = dict(_drawn_inputs(seed))
    spreads = {'L0_attn_ln_gamma': (1.0, 0.6), 'L0_attn_ln_beta': (0.0, 0.738)}
    factors = {'L0_attn_W_q': 8.0,
     'L0_attn_W_dkv': 8.0,
     'L0_attn_W_uk': 8.0,
     'L0_attn_W_uv': 4.885,
     'L0_attn_W_o': 4.904,
     'L0_ffn_Wr': 6.791,
     'L0_ffn_W1': 6.01,
     'L0_ffn_W2': 5.942,
     'L0_c': 3.477,
     'L0_wmod': 3.538,
     'L1_attn_Wq': 47.84,
     'L1_attn_Wk': 49.045,
     'L1_attn_Wv': 8.0,
     'L1_attn_Wo': 8.0,
     'L1_ffn_gate_w': 8.0,
     'L1_ffn_expert_gate': 8.0,
     'L1_ffn_expert_up': 8.0,
     'L1_ffn_expert_down': 8.0,
     'L1_ffn_shared_gate': 8.0,
     'L1_ffn_shared_up': 8.0,
     'L1_ffn_shared_down': 8.0,
     'L1_c': 8.0,
     'L1_wmod': 8.0}
    for name, (base, spread) in spreads.items():
        noise = np.random.default_rng([zlib.crc32(name.encode()), seed]).standard_normal(out[name].shape)
        drawn = base * np.exp(spread * noise) if base else spread * noise
        out[name] = jnp.asarray(drawn.astype(out[name].dtype))
    for name, factor in factors.items():
        out[name] = (out[name] * factor).astype(out[name].dtype)
    return out
```

```python
import numpy as np
import concourse.bass as bass
from concourse import mybir
from concourse.alu_op_type import AluOpType as ALU
from contextlib import ExitStack

F32 = mybir.dt.float32
BF = mybir.dt.bfloat16
U32 = mybir.dt.uint32
I32 = mybir.dt.int32
ACT = mybir.ActivationFunctionType
AX = mybir.AxisListType

P = 128
T = 2048
D = 128
H, HD = 16, 8
TILES = T // P
CH = 512
NC4 = T // CH
TPC = CH // P
LAT = 32
E8 = 8
FF0, FF1 = 512, 352
EPS = 1e-5
NEG = -1e30
SCALE = float(1 / np.sqrt(np.float32(HD)))
GH = 4
NG = H // GH
SHIFT0 = 96
MXBUF = 3

ROWS0 = 2 * T
RTILES1 = 2 * T // P + E8
ROWS1 = RTILES1 * P

C_ID, C_MN, C_MT, C_UP, C_BD, C_I8, C_IT, C_TH, C_W = 0, 128, 256, 384, 512, 640, 648, 688, 704

UNITS = [(g, Q if g % 2 == 0 else NC4 - 1 - Q) for g in range(NG) for Q in range(NC4)]
STEPS = [(g, Q, kb) for g, Q in UNITS for kb in range(TPC * (Q + 1))]
NU, NST = len(UNITS), len(STEPS)
UNIT = [UNITS.index(s[:2]) for s in STEPS]
FIRST = [UNIT.index(u) for u in range(NU)] + [NST]
LAST = [max(s for s, x in enumerate(STEPS) if x[0] == g) for g in range(NG)]
TURN_LAG = 3


def max_tiles(g, Q):
    return [(g, Q, j, qb, c) for qb in range(TPC) for j in range(GH) for c in range(Q + 1)]


def max_width(m):
    return CH if m[4] < m[1] else (m[3] + 1) * P


def step_off(s):
    return max(0, STEPS[s][2] * P - STEPS[s][1] * CH)


def schedule():
    base, due = [], []
    for u, (g, Q) in enumerate(UNITS):
        for m in max_tiles(g, Q):
            base.append(("max", m))
            if due and due[0][0] <= len(base):
                base.append(("turn", due.pop(0)[1]))
        due.append((len(base) + TURN_LAG, u))
    base += [("turn", u) for _, u in due]
    pe = dve = act = 0.0
    out, rot = [], []
    k = s = half = 0
    lat = 0.1
    ready = [1e9] * NU
    free = [0.0] * MXBUF
    last_max, exp_done = {}, [0.0, 0.0]
    loaded = [0.0, 0.0] + [1e9] * NG
    norms = []
    while k < len(base) or s < NST or norms:
        b = len(rot) % MXBUF
        if norms and norms[0][0] <= pe or (k == len(base) and s == NST):
            pe = max(pe, free[b] + lat) + .4
            dve = max(dve, pe + lat) + .3
            free[b] = dve
            out.append(("rot", len(rot)))
            rot.append(("norm", norms.pop(0)[1]))
            continue
        t_step = max(pe, ready[UNIT[s]], exp_done[half] + lat) if s < NST and ready[UNIT[s]] < 1e8 else 1e9
        t_max = 1e9
        if k < len(base):
            kind, x = base[k]
            t_max = max(pe, free[b] + lat)
            if kind == "max":
                t_max = max(t_max, loaded[x[0]])
            else:
                t_max = max(t_max, last_max[x] + .6)
        if t_max <= t_step + .05 and k < len(base):
            pe = t_max
            if kind == "max":
                w = max_width(x)
                pe += w / 2400 + .003
                dve = max(dve, pe + lat + .1) + .075 + w * .00104
                last_max[UNITS.index(x[:2])] = dve
            else:
                pe += .22
                dve = max(dve, pe + lat) + .6
                ready[x] = dve + 2.4
            free[b] = dve
            out.append(("rot", len(rot)))
            rot.append((kind, x))
            k += 1
        else:
            pe = t_step
            w = CH - step_off(s)
            pe += 2 * w / 2400 + (.11 if STEPS[s][2] >= TPC * STEPS[s][1] else 0)
            act = max(act, pe + lat + .1) + .19 + 2 * w * .000833
            exp_done[half] = act
            out.append(("scores", s, half))
            if half == 1:
                if s:
                    out.append(("av", s - 1))
                    pe += 4 * (CH - step_off(s - 1)) / 2400
                    if s - 1 in LAST:
                        loaded[LAST.index(s - 1) + 2] = pe + 9
                    if s in FIRST:
                        norms.append((pe + 3, UNIT[s] - 1))
                s += 1
                if s == NST:
                    out.append(("av", NST - 1))
                    norms.append((pe + 3, NU - 1))
            half ^= 1
    return out, rot


ORDER, ROT = schedule()
NROT = len(ROT)
NORM_AT = {x: k for k, (kind, x) in enumerate(ROT) if kind == "norm"}


class Count:

    def __init__(self, sem):
        self.sem, self.value = sem, 0

    def next(self, n=1):
        self.value += n
        return self.value


def setup(nc, m, w, dram):
    with ExitStack() as ctx:
        sb = lambda n, s, d=F32: ctx.enter_context(nc.sbuf_tensor(n, s, d))
        wmod = [sb(f"wmod{l}", [P, 6 * D]) for l in range(2)]
        ccol, scol, sbc = sb("ccol", [P, 2]), sb("scol", [P, 2]), sb("sbc", [P, 2, P])
        gate, sign = sb("gate", [P, 4, D]), sb("sign", [P, 4, D])
        loads = m.sem("setup_loads")
        silu_done, bc_done, cols_ready, rows_ready, memset_done = (m.sem(n) for n in (
            "silu_done", "bc_done", "cols_ready", "rows_ready", "memset_done"))
        gates, weights_ready = Count(m.sem("gates_chain")), m.sem("weights_ready")
        small = [(m.consts[:], dram["consts"])] + [
            (m.x[:, 4 * z:4 * z + 4], dram["x"].rearrange("(b p) d -> p b d", p=P)[:, 4 * z:4 * z + 4]) for z in range(4)]
        for l in range(2):
            small += [(wmod[l][:], dram[f"wmod{l}"]), (ccol[:, l:l + 1], dram[f"c{l}"].rearrange("o d -> d o")),
                      (m.wo[l][:], dram[f"wo{l}"]), (m.wr[l][:], dram[f"wr{l}"])]
        small += [(m.wq[:], dram["wq0"]), (m.wdkv[:], dram["wdkv"]), (m.wuk[:], dram["wuk"]), (m.wuv[:], dram["wuv"]),
                  (m.lngb[:, 0:1], dram["ln_gamma"]), (m.lngb[:, 1:2], dram["ln_beta"])]
        small += [(m.w1small[:, i], dram[n]) for i, n in enumerate(("wq1", "wk1", "wv1"))]

        with nc.Block() as block:
            @block.sync
            def _(sp):
                for dst, src in small:
                    sp.dma_start(dst, src).then_inc(loads, 16)
                sp.wait_ge(memset_done, 4)
                for p in range(2):
                    for j in range(GH):
                        sp.dma_start(m.KS[p][SHIFT0:SHIFT0 + 2 * GH, j, :], dram["zo"][j]).then_inc(loads, 16)
                sp.wait_ge(memset_done, 5)
                sp.dma_start(dram["perm1"].rearrange("(b p) d -> p b d", p=P)[:, 0:20], m.xn[:, 0:1].to_broadcast([P, 20, D])).then_inc(loads, 16)
                sp.dma_start(dram["perm1"].rearrange("(b p) d -> p b d", p=P)[:, 20:40], m.xn[:, 0:1].to_broadcast([P, 20, D])).then_inc(loads, 16)
                sp.wait_ge(loads, 16 * (len(small) + 10))

            @block.scalar
            def _(act):
                act.wait_ge(loads, 16 * (len(small) + 10))
                act.activation(scol[:], ccol[:], ACT.Silu).then_inc(silu_done, 1)

            @block.tensor
            def _(pe):
                pe.wait_ge(bc_done, 2)
                for l in range(2):
                    for i, part in enumerate((0, 1, 3, 4)):
                        mm = pe.matmul(m.bank[0][:, 4 * l + i:4 * l + i + 1], wmod[l][:, part * D:(part + 1) * D],
                                       scol[:, l:l + 1], start=True, stop=True)
                mm.then_inc(cols_ready, 1)
                for l in range(2):
                    for i, part in enumerate((2, 5)):
                        mm = pe.matmul(m.bank[1][:, (2 * l + i) * D:(2 * l + i + 1) * D], sbc[:, l, :],
                                       wmod[l][:, part * D:(part + 1) * D], start=True, stop=True)
                mm.then_inc(rows_ready, 1)

            @block.vector
            def _(v):
                for p in range(2):
                    v.memset(m.KS[p][64:P], 0.).then_inc(memset_done, 1)
                    v.memset(m.QS[p][64:P], 0.).then_inc(memset_done, 1)
                v.memset(m.xn[:, 0], 0.).then_inc(memset_done, 1)
                v.wait_ge(silu_done, 1)
                for l in range(2):
                    v.tensor_copy(sbc[:, l, :], scol[:, l:l + 1].to_broadcast([P, P])).then_inc(bc_done, 1)
                v.wait_ge(cols_ready, 1)
                v.tensor_copy(m.modc[:], m.bank[0][:, 0:8]).then_inc(gates.sem, 1)
                v.wait_ge(gates.sem, gates.next())
                for i in (1, 3, 5, 7):
                    v.tensor_scalar(m.modc[:, i:i + 1], m.modc[:, i:i + 1], 1.0, None, ALU.add).then_inc(gates.sem, 1)
                v.wait_ge(rows_ready, 1)
                g2, s2 = gate[:].rearrange("p a d -> p (a d)"), sign[:].rearrange("p a d -> p (a d)")
                v.tensor_scalar(s2, m.bank[1][:], 0., 2., ALU.is_ge, ALU.mult).then_inc(gates.sem, 1)
                v.tensor_copy(g2, m.bank[1][:]).then_inc(gates.sem, 1)
                v.wait_ge(gates.sem, gates.next(6))
                v.tensor_scalar(s2, s2, -1., None, ALU.add).then_inc(gates.sem, 1)
                v.wait_ge(gates.sem, gates.next())
                v.tensor_tensor(g2, g2, s2, ALU.mult).then_inc(gates.sem, 1)
                v.wait_ge(gates.sem, gates.next())
                v.tensor_scalar(g2, g2, .25, None, ALU.max).then_inc(gates.sem, 1)
                v.wait_ge(gates.sem, gates.next())
                v.tensor_tensor(m.gates[:].rearrange("p a d -> p (a d)"), g2, s2, ALU.mult).then_inc(gates.sem, 1)
                v.wait_ge(gates.sem, gates.next())
                for l in range(2):
                    v.tensor_tensor(m.wo[l][:], m.wo[l][:], m.gates[:, 2 * l], ALU.mult).then_inc(weights_ready, 1)
                for src, dst, n in ((m.wq, m.wqr, P), (m.wuk, m.wukr, LAT)):
                    a = src[:].rearrange("p (h u d) -> p h u d", u=2, d=HD // 2)
                    b = dst[:].rearrange("p (h u d) -> p h u d", u=2, d=HD // 2)
                    v.tensor_scalar(b[:, :, 0], a[:, :, 1], -1., None, ALU.mult).then_inc(weights_ready, 1)
                    v.tensor_copy(b[:, :, 1], a[:, :, 0]).then_inc(weights_ready, 1)
                for i in range(3):
                    v.tensor_tensor(m.w1bd[:, i].rearrange("p (h e) -> p h e", e=HD),
                                    m.consts[:, C_BD:C_BD + P].rearrange("p (h e) -> p h e", e=HD),
                                    m.w1small[:, i:i + 1, :].to_broadcast([P, H, HD]), ALU.mult).then_inc(weights_ready, 1)
                v.tensor_copy(m.identb[:], m.consts[:, C_ID:C_ID + P]).then_inc(weights_ready, 1)
                v.tensor_copy(m.maskTb[:], m.consts[:, C_MT:C_MT + P]).then_inc(weights_ready, 1)
                v.memset(m.maskN[:, 0:CH - P], 0.).then_inc(weights_ready, 1)
                v.tensor_copy(m.maskN[:, CH - P:], m.consts[:, C_MN:C_MN + P]).then_inc(weights_ready, 1)


def reciprocal_root(v, act_done, count, a, root, y, t):
    v.wait_ge(act_done[0], act_done[1])
    v.reciprocal(y, root).then_inc(count.sem, 1)
    v.wait_ge(count.sem, count.next())
    v.tensor_tensor(t, y, y, ALU.mult).then_inc(count.sem, 1)
    v.wait_ge(count.sem, count.next())
    v.tensor_tensor(t, t, a, ALU.mult).then_inc(count.sem, 1)
    v.wait_ge(count.sem, count.next())
    v.tensor_scalar(t, t, -.5, 1.5, ALU.mult, ALU.add).then_inc(count.sem, 1)
    v.wait_ge(count.sem, count.next())
    v.tensor_tensor(y, y, t, ALU.mult).then_inc(count.sem, 1)
    v.wait_ge(count.sem, count.next())


def layer_norm(nc, m, n):
    with ExitStack() as ctx:
        sb = lambda name, s, d=F32: ctx.enter_context(nc.sbuf_tensor(f"{name}_ln{n}", s, d))
        st, mv = sb("st", [P, TILES, 6]), sb("mv", [P, TILES, 2])
        a, root, y, t = (sb(k, [P, TILES]) for k in "a root y t".split())
        chain, var_ready, root_done, rstd_ready = m.ln_chain, m.sem("ln_var"), m.sem("ln_root"), m.sem("ln_rstd")
        xn_done = m.sem("ln_out")
        with nc.Block() as block:
            @block.vector
            def _(v):
                for b in range(TILES):
                    v.bn_stats(st[:, b], m.x[:, b]).then_inc(chain.sem, 1)
                v.wait_ge(chain.sem, chain.next(TILES))
                for b in range(TILES):
                    v.bn_aggr(mv[:, b], st[:, b]).then_inc(chain.sem, 1)
                v.wait_ge(chain.sem, chain.next(TILES))
                v.tensor_scalar(a[:], mv[:, :, 1], EPS, None, ALU.add).then_inc(var_ready, 1)
                v.wait_ge(var_ready, n + 1)
                reciprocal_root(v, (root_done, n + 1), chain, a[:], root[:], y[:], t[:])
                v.sem_inc(rstd_ready, 1)
                for b in range(0, TILES, 2):
                    v.tensor_scalar(m.xn[:, b], m.x[:, b], mv[:, b, 0:1], y[:, b:b + 1], ALU.subtract, ALU.mult).then_inc(xn_done, 1)

            @block.scalar
            def _(act):
                act.wait_ge(var_ready, n + 1)
                act.activation(root[:], a[:], ACT.Sqrt).then_inc(root_done, 1)

            @block.gpsimd
            def _(g):
                g.wait_ge(rstd_ready, n + 1)
                for b in range(1, TILES, 2):
                    g.tensor_scalar(m.xn[:, b], m.x[:, b], mv[:, b, 0:1], y[:, b:b + 1], ALU.subtract, ALU.mult).then_inc(xn_done, 1)


def project(nc, m, L, dram):
    with ExitStack() as ctx:
        sb = lambda name, s, d=F32: ctx.enter_context(nc.sbuf_tensor(f"{name}_pj{L}", s, d))
        hT = sb("hT", [P, T])
        qf, res = [sb(f"qf{i}", [P, CH]) for i in range(2)], [sb(f"res{i}", [P, CH]) for i in range(2)]
        parts = [[sb(f"part{i}{a}", [P, T], BF) for a in range(3)] for i in range(2)]
        tmp = [sb(f"tmp{i}", [P, CH]) for i in range(2)]
        if L == 0:
            cosT, sinT = sb("cosT", [P, T]), sb("sinT", [P, T])
            cen, sq, latn = (sb(k, [P, TILES, LAT]) for k in ("cen", "sq", "latn"))
            latT = sb("latT", [LAT, T])
            mean, a, root, y, t = (sb(k, [P, TILES]) for k in ("mean", "a", "root", "y", "t"))
        names = "turned ht_ready lat_ready lat_var lat_root latn_ready latT_turned latT_ready v_ready v_out proj_ready proj_used qf_ready hi_done r_done mid_done lo_done stored tables".split()
        (turned, ht_ready, lat_ready, lat_var, lat_root, latn_ready, latT_turned, latT_ready, v_ready, v_out, proj_ready,
         proj_used, qf_ready, hi_done, r_done, mid_done, lo_done, stored, tables) = (m.sem("pj_" + k) for k in names)
        chain = m.pj_chain
        bank = m.bank
        PA = (bank[5], bank[7])
        PB = (bank[6], bank[0])
        s8 = 2 * NC4 * L
        s4 = NC4 * L
        ident = m.consts[:, C_ID:C_ID + P]

        with nc.Block() as block:
            @block.sync
            def _(sp):
                if L == 0:
                    for dst, key in ((cosT, "cos"), (sinT, "sin")):
                        for g in range(2 * H):
                            sp.dma_start(dst[4 * g:4 * g + 4, :], dram[key]).then_inc(tables, 16)
                for i, key in enumerate(("q_parts", "k_parts")):
                    sp.wait_ge(lo_done, s8 + NC4 * (i + 1))
                    for a3 in range(3):
                        dst = bass.AP(dram[f"{key}{L}"].tensor, a3 * HD * T, [[3 * HD * T, H], [T, HD], [1, T]])
                        sp.dma_start(dst, parts[i][a3][:]).then_inc(stored, 16)
                sp.wait_ge(stored, 96 * (L + 1))

            @block.tensor
            def _(pe):
                for c in range(NC4):
                    for t4 in range(TPC):
                        mm = pe.transpose(bank[c][:, t4 * P:(t4 + 1) * P], m.xn[:, c * TPC + t4], ident)
                    mm.then_inc(turned, 1)
                for c in range(NC4):
                    pe.wait_ge(ht_ready, s4 + c + 1)
                    if L == 0:
                        for b in range(c * TPC, (c + 1) * TPC):
                            mm = pe.matmul(bank[4][:, b * LAT:(b + 1) * LAT], hT[:, b * P:(b + 1) * P], m.wdkv[:], start=True, stop=True)
                        mm.then_inc(lat_ready, 1)

                def heads(s):
                    i, c = divmod(s, NC4)
                    rhs = (hT if i == 0 or L else latT)[:, c * CH:(c + 1) * CH]
                    if s >= 2:
                        pe.wait_ge(proj_used, s8 + s - 1)
                    if L == 0:
                        pe.matmul(PB[s % 2][:], (m.wqr, m.wukr)[i][:], rhs, start=True, stop=True)
                    mm = pe.matmul(PA[s % 2][:], ((m.wq, m.wuk)[i][:] if L == 0 else m.w1bd[:, i]), rhs, start=True, stop=True)
                    mm.then_inc(proj_ready, 1)

                for s in range(NC4):
                    heads(s)
                if L == 0:
                    pe.wait_ge(latn_ready, 1)
                    for c in range(NC4):
                        for t4 in range(TPC):
                            mm = pe.transpose(bank[1 + c][0:LAT, t4 * P:(t4 + 1) * P], latn[:, c * TPC + t4], ident)
                        mm.then_inc(latT_turned, 1)
                for c in range(NC4):
                    if L == 0:
                        pe.wait_ge(latT_ready, c + 1)
                    for t4 in range(TPC):
                        b = c * TPC + t4
                        mm = pe.matmul(bank[1 + c][:, t4 * P:(t4 + 1) * P], (latT if L == 0 else hT)[:, b * P:(b + 1) * P],
                                       m.wuv[:] if L == 0 else m.w1bd[:, 2], start=True, stop=True)
                    mm.then_inc(v_ready, 1)
                for s in range(NC4, 2 * NC4):
                    heads(s)

            @block.scalar
            def _(act):
                for c in range(NC4):
                    act.wait_ge(turned, s4 + c + 1)
                    act.activation(hT[:, c * CH:(c + 1) * CH], bank[c][:], ACT.Identity, bias=m.modc[:, 4 * L:4 * L + 1],
                                   scale=m.modc[:, 4 * L + 1:4 * L + 2]).then_inc(ht_ready, 1)
                if L == 0:
                    act.wait_ge(lat_var, 1)
                    act.activation(root[:], a[:], ACT.Sqrt).then_inc(lat_root, 1)

                def hi(s):
                    i, c = divmod(s, NC4)
                    act.wait_ge(qf_ready, s8 + s + 1)
                    act.copy(parts[i][0][:, c * CH:(c + 1) * CH], qf[s % 2][:]).then_inc(hi_done, 1)

                def mid(s):
                    i, c = divmod(s, NC4)
                    act.wait_ge(r_done, s8 + s + 1)
                    act.copy(parts[i][1][:, c * CH:(c + 1) * CH], res[s % 2][:]).then_inc(mid_done, 1)

                for s in range(NC4):
                    hi(s)
                    if s:
                        mid(s - 1)
                mid(NC4 - 1)
                if L == 0:
                    for c in range(NC4):
                        act.wait_ge(latT_turned, c + 1)
                        act.activation(latT[:, c * CH:(c + 1) * CH], bank[1 + c][0:LAT], ACT.Identity, bias=m.lngb[:, 1:2],
                                       scale=m.lngb[:, 0:1]).then_inc(latT_ready, 1)
                for c in range(NC4):
                    act.wait_ge(v_ready, s4 + c + 1)
                    act.copy(m.vall[:, c * TPC:(c + 1) * TPC], bank[1 + c][:].rearrange("p (b d) -> p b d", d=D)).then_inc(v_out, 1)
                for s in range(NC4, 2 * NC4):
                    hi(s)
                    if s > NC4:
                        mid(s - 1)
                mid(2 * NC4 - 1)

            @block.vector
            def _(v):
                if L == 0:
                    lat = bank[4][:].rearrange("p (b l) -> p b l", l=LAT)
                    v.wait_ge(lat_ready, NC4)
                    v.tensor_reduce(mean[:], lat, AX.X, ALU.add).then_inc(chain.sem, 1)
                    v.wait_ge(chain.sem, chain.next())
                    v.tensor_scalar(mean[:], mean[:], 1 / LAT, None, ALU.mult).then_inc(chain.sem, 1)
                    v.wait_ge(chain.sem, chain.next())
                    v.tensor_tensor(cen[:], lat, mean[:].unsqueeze(2).to_broadcast([P, TILES, LAT]), ALU.subtract).then_inc(chain.sem, 1)
                    v.wait_ge(chain.sem, chain.next())
                    v.tensor_tensor(sq[:], cen[:], cen[:], ALU.mult).then_inc(chain.sem, 1)
                    v.wait_ge(chain.sem, chain.next())
                    v.tensor_reduce(a[:], sq[:], AX.X, ALU.add).then_inc(chain.sem, 1)
                    v.wait_ge(chain.sem, chain.next())
                    v.tensor_scalar(a[:], a[:], 1 / LAT, EPS, ALU.mult, ALU.add).then_inc(lat_var, 1)
                    v.wait_ge(lat_var, 1)
                    reciprocal_root(v, (lat_root, 1), chain, a[:], root[:], y[:], t[:])
                    v.tensor_tensor(latn[:], cen[:], y[:].unsqueeze(2).to_broadcast([P, TILES, LAT]), ALU.mult).then_inc(latn_ready, 1)
                    v.wait_ge(tables, 16 * 4 * H)
                for s in range(2 * NC4):
                    c = s % NC4
                    cs = slice(c * CH, (c + 1) * CH)
                    if s >= 2:
                        v.wait_ge(r_done, s8 + s - 1)
                        v.wait_ge(hi_done, s8 + s - 1)
                    v.wait_ge(proj_ready, s8 + s + 1)
                    if L == 0:
                        v.tensor_tensor(tmp[0][:], PA[s % 2][:], cosT[:, cs], ALU.mult).then_inc(chain.sem, 1)
                        v.tensor_tensor(tmp[1][:], PB[s % 2][:], sinT[:, cs], ALU.mult).then_inc(proj_used, 1)
                        v.wait_ge(chain.sem, chain.next())
                        v.wait_ge(proj_used, s8 + s + 1)
                        v.tensor_tensor(qf[s % 2][:], tmp[0][:], tmp[1][:], ALU.add).then_inc(qf_ready, 1)
                        v.wait_ge(qf_ready, s8 + s + 1)
                    else:
                        v.tensor_copy(qf[s % 2][:], PA[s % 2][:]).then_inc(qf_ready, 1)
                        v.wait_ge(qf_ready, s8 + s + 1)
                        v.sem_inc(proj_used, 1)

            @block.gpsimd
            def _(g):
                def low(s):
                    i, c = divmod(s, NC4)
                    g.wait_ge(mid_done, s8 + s + 1)
                    g.tensor_tensor(parts[i][2][:, c * CH:(c + 1) * CH], res[s % 2][:], parts[i][1][:, c * CH:(c + 1) * CH],
                                    ALU.subtract).then_inc(lo_done, 1)

                for s in range(2 * NC4):
                    i, c = divmod(s, NC4)
                    g.wait_ge(hi_done, s8 + s + 1)
                    if s >= 2:
                        g.wait_ge(lo_done, s8 + s - 1)
                    g.tensor_tensor(res[s % 2][:], qf[s % 2][:], parts[i][0][:, c * CH:(c + 1) * CH], ALU.subtract).then_inc(r_done, 1)
                    if s:
                        low(s - 1)
                low(2 * NC4 - 1)


def attention(nc, m, L, dram, weight_loads):
    with ExitStack() as ctx:
        sb = lambda name, s, d=F32: ctx.enter_context(nc.sbuf_tensor(f"{name}_at{L}", s, d))
        QS, KS = m.QS, m.KS
        VS = [sb(f"vs{p}", [P, TILES, GH, 32]) for p in range(2)]
        probs = sb("probs", [P, 2, GH, CH])
        avs = sb("avs", [P, 2, CH])
        mxp = sb("mxp", [P, 4, GH * TPC, NC4])
        mx = sb("mx", [P, 4, GH * TPC])
        nsh = sb("nsh", [P, 4, TPC, 2 * GH], BF)
        shrow = sb("shrow", [2 * GH, 4, CH], BF)
        junk = sb("junk", [P, MXBUF, CH])
        st, mxb, avb = m.st, m.mxb, m.avb
        s_ = m.sem
        q_d, k_d = dram[f"q_parts{L}"], dram[f"k_parts{L}"]
        vs_filled, weights_in = s_("vs_filled"), s_("weights_in")
        kq_loaded = [s_(f"kq_loaded{p}") for p in range(2)]
        v_copied = [s_(f"v_copied{p}") for p in range(2)]
        rows_zeroed = [s_(f"rows_zeroed{p}") for p in range(2)]
        st_ready = [s_(f"st_ready{i}") for i in range(2)]
        exp_done = [s_(f"exp_done{i}") for i in range(2)]
        shift_set = [s_(f"shift_set{u}") for u in range(4)]
        (av_done, av_free, max_final, hi_split, mx_ready, mx_free, shift_split, shift_row) = (s_(n) for n in (
            "av_done", "av_free", "max_final", "hi_split", "mx_ready", "mx_free", "shift_split", "shift_row"))
        RB, SB, UB = L * NROT, L * NST, L * NU
        GB = L * NG // 2

        with nc.Block() as block:
            @block.sync
            def _(sp):
                def load_group(g):
                    p = g % 2
                    for j in range(GH):
                        base = (g * GH + j) * 3 * HD * T
                        for a in range(3):
                            sp.dma_start(QS[p][24 * a:24 * a + 24, j, :],
                                         bass.AP(q_d.tensor, base + a * HD * T, [[0, 3], [T, HD], [1, T]])).then_inc(kq_loaded[p], 16)
                        sp.dma_start(KS[p][0:72, j, :], bass.AP(k_d.tensor, base, [[0, 3], [T, 3 * HD], [1, T]])).then_inc(kq_loaded[p], 16)

                load_group(0)
                load_group(1)
                for dst, src in weight_loads:
                    sp.dma_start(dst, src).then_inc(weights_in, 16)
                for item in ORDER:
                    if item[0] == "rot" and ROT[item[1]][0] == "turn":
                        u = ROT[item[1]][1]
                        g, Q = UNITS[u]
                        sp.wait_ge(shift_row, UB + u + 1)
                        sp.dma_start(QS[g % 2][SHIFT0:SHIFT0 + 2 * GH, :, Q * CH:(Q + 1) * CH],
                                     shrow[:, u % 4, :].unsqueeze(1).to_broadcast([2 * GH, GH, CH])).then_inc(shift_set[u % 4], 16)
                    if item[0] == "av" and item[1] in LAST[:NG - 2]:
                        sp.wait_ge(av_done, 2 + SB + item[1] + 1)
                        load_group(LAST.index(item[1]) + 2)
                sp.wait_ge(weights_in, 16 * m.weights_total)

            @block.gpsimd
            def _(g):
                for p in range(2):
                    g.memset(VS[p][:], 0.).then_inc(vs_filled, 1)
                g.wait_ge(vs_filled, 4 * L + 2)
                for p in range(2):
                    g.memset(VS[p][:, :, :, HD:HD + 1], 1.).then_inc(vs_filled, 1)
                g.wait_ge(vs_filled, 4 * L + 4)
                for gg in range(NG):
                    p, i = gg % 2, gg // 2
                    if i:
                        g.wait_ge(av_done, 2 + SB + LAST[gg - 2] + 1)
                    g.memset(QS[p][SHIFT0:SHIFT0 + 32], 0.).then_inc(rows_zeroed[p], 1)
                    g.wait_ge(rows_zeroed[p], GB + i + 1)
                    g.tensor_copy(VS[p][:, :, :, 0:HD], m.vall[:, :, gg * GH * HD:(gg + 1) * GH * HD].rearrange(
                        "p b (h d) -> p b h d", d=HD)).then_inc(v_copied[p], 1)
                    g.wait_ge(v_copied[p], GB + i + 1)

            @block.tensor
            def _(pe):
                if L == 0:
                    pe.sem_inc(av_done, 2)
                pe.wait_ge(vs_filled, 4 * L + 4)

                def rotate(k):
                    kind, x = ROT[k]
                    buf = mxb[k % MXBUF]
                    pe.wait_ge(mx_free, RB + k + 1)
                    if kind == "max":
                        gg, Q, j, qb, c = x
                        p, w = gg % 2, max_width(x)
                        if (qb, j, c) == (0, 0, 0) and UNITS.index((gg, Q)) % NC4 == 0:
                            pe.wait_ge(kq_loaded[p], (GB + gg // 2 + 1) * 16 * 4 * GH)
                            pe.wait_ge(rows_zeroed[p], GB + gg // 2 + 1)
                        pe.matmul(buf[:, 0:w], QS[p][:, j, (4 * Q + qb) * P:(4 * Q + qb + 1) * P],
                                  KS[p][:, j, c * CH:c * CH + w], start=True, stop=True).then_inc(mx_ready, 1)
                    elif kind == "turn":
                        pe.wait_ge(shift_split, UB + x + 1)
                        for qb in range(TPC):
                            mm = pe.transpose(buf[:].bitcast(BF)[0:2 * GH, qb * P:(qb + 1) * P], nsh[:, x % 4, qb, :], m.identb[:])
                        mm.then_inc(mx_ready, 1)
                    else:
                        pe.wait_ge(av_free, UB + x + 1)
                        for qb in range(TPC):
                            mm = pe.transpose(buf[:, qb * P:(qb + 1) * P], avs[:, x % 2, qb * P:(qb + 1) * P], m.consts[:, C_ID:C_ID + P])
                        mm.then_inc(mx_ready, 1)

                def scores(s, half):
                    gg, Q, kb = STEPS[s]
                    p, off, diag = gg % 2, step_off(s), kb >= TPC * Q
                    if s:
                        pe.wait_ge(exp_done[half], SB + s)
                    for y in range(2):
                        j = 2 * half + y
                        mm = pe.matmul(st[half][:, y, off:CH], KS[p][:, j, kb * P:(kb + 1) * P], QS[p][:, j, Q * CH + off:(Q + 1) * CH],
                                       start=True, stop=True, skip_group_check=diag)
                        if diag:
                            mm = pe.matmul(st[half][:, y, off:off + P], m.identb[:], m.maskTb[:], start=False, stop=True, skip_group_check=True)
                    mm.then_inc(st_ready[half], 1)

                def values(s):
                    gg, Q, kb = STEPS[s]
                    u, p, off = UNIT[s], gg % 2, step_off(s)
                    if kb == 0:
                        pe.wait_ge(v_copied[p], GB + gg // 2 + 1)
                        if u:
                            pe.wait_ge(av_free, UB + u)
                    for half in range(2):
                        pe.wait_ge(exp_done[half], SB + s + 1)
                    for j in range(GH):
                        mm = pe.matmul(avb[32 * j:32 * j + 32, off:CH], VS[p][:, kb, j, :], probs[:, s % 2, j, off:CH],
                                       start=kb == 0, stop=kb == TPC * Q + 3, tile_position=(0, 32 * j), skip_group_check=True)
                    mm.then_inc(av_done, 1)

                for item in ORDER:
                    if item[0] == "rot":
                        rotate(item[1])
                    elif item[0] == "av":
                        values(item[1])
                    else:
                        _, s, half = item
                        if STEPS[s][2] == 0 and half == 0:
                            u = UNIT[s]
                            pe.wait_ge(shift_set[u % 4], 16 * (L * (NU // 4) + u // 4 + 1))
                        scores(s, half)

            @block.scalar
            def _(act):
                def evacuate(u):
                    act.wait_ge(av_done, 2 + SB + FIRST[u + 1])
                    if u >= 2:
                        act.wait_ge(mx_ready, RB + NORM_AT[u - 2] + 1)
                    act.copy(avs[:, u % 2, :], avb[:]).then_inc(av_free, 1)

                for s, (g, Q, kb) in enumerate(STEPS):
                    off = step_off(s)
                    act.wait_ge(av_done, SB + s + 1)
                    for half in range(2):
                        act.wait_ge(st_ready[half], SB + s + 1)
                        act.activation(probs[:, s % 2, 2 * half:2 * half + 2, off:CH], st[half][:, :, off:CH], ACT.Exp,
                                       scale=SCALE).then_inc(exp_done[half], 1)
                    if kb == 0 and s:
                        evacuate(UNIT[s] - 1)
                evacuate(NU - 1)

            @block.vector
            def _(v):
                if L == 0:
                    v.sem_inc(mx_free, MXBUF)
                for k, (kind, x) in enumerate(ROT):
                    buf = mxb[k % MXBUF]
                    v.wait_ge(mx_ready, RB + k + 1)
                    if kind == "max":
                        g, Q, j, qb, c = x
                        u, w = UNITS.index((g, Q)), max_width(x)
                        dst = mxp[:, u % 4, qb * GH + j, c:c + 1]
                        if c < Q:
                            ins = v.tensor_reduce(dst, buf[:, 0:w], AX.X, ALU.max)
                        else:
                            ins = v.tensor_tensor_reduce(junk[:, k % MXBUF, 0:w], buf[:, 0:w], m.maskN[:, CH - w:], 1.0, -3e38,
                                                         ALU.add, ALU.max, dst)
                        ins.then_inc(mx_free, 1)
                        if (j, qb, c) == (GH - 1, TPC - 1, Q):
                            v.wait_ge(mx_free, RB + k + 1 + MXBUF)
                            v.tensor_reduce(mx[:, u % 4, :], mxp[:, u % 4, :, 0:Q + 1], AX.X, ALU.max, negate=True).then_inc(max_final, 1)
                            v.wait_ge(max_final, UB + u + 1)
                            ns = nsh[:, u % 4].rearrange("p q (j s) -> p (q j) s", s=2)
                            v.tensor_copy(ns[:, :, 0], mx[:, u % 4, :]).then_inc(hi_split, 1)
                            v.wait_ge(hi_split, UB + u + 1)
                            v.tensor_tensor(ns[:, :, 1], mx[:, u % 4, :], ns[:, :, 0], ALU.subtract).then_inc(shift_split, 1)
                    elif kind == "turn":
                        if x >= 4:
                            v.wait_ge(shift_set[x % 4], 16 * (L * (NU // 4) + x // 4))
                        v.tensor_copy(shrow[:, x % 4, :], buf[:].bitcast(BF)[0:2 * GH, 0:CH]).then_inc(shift_row, 1)
                        v.wait_ge(shift_row, UB + x + 1)
                        v.sem_inc(mx_free, 1)
                    else:
                        g, Q = UNITS[x]
                        v.tensor_copy(m.araw[:, TPC * Q:TPC * Q + TPC, GH * g:GH * g + GH, :],
                                      buf[:].rearrange("p (q j c) -> p q j c", j=GH, c=32)[:, :, :, 0:HD + 1]).then_inc(mx_free, 1)


def output_projection(nc, m, L):
    with ExitStack() as ctx:
        sb = lambda name, s, d=F32: ctx.enter_context(nc.sbuf_tensor(f"{name}_op{L}", s, d))
        rec = sb("rec", [P, TILES, H])
        att, attT = sb("att", [P, TILES, D]), sb("attT", [P, T])
        inv_done, att_ready, turned, attT_ready, o_ready, x_done = (m.sem("op_" + n) for n in "inv att turned attT o x".split())
        s4 = L * NC4
        with nc.Block() as block:
            @block.vector
            def _(v):
                v.reciprocal(rec[:], m.araw[:, :, :, HD]).then_inc(inv_done, 1)
                v.wait_ge(inv_done, L + 1)
                for c in range(NC4):
                    for b in range(c * TPC, (c + 1) * TPC):
                        v.tensor_tensor(att[:, b].rearrange("p (h d) -> p h d", d=HD), m.araw[:, b, :, 0:HD],
                                        rec[:, b].unsqueeze(2).to_broadcast([P, H, HD]), ALU.mult).then_inc(att_ready, 1)
                for c in range(NC4):
                    v.wait_ge(o_ready, s4 + c + 1)
                    xs = m.x[:, c * TPC:(c + 1) * TPC].rearrange("p b d -> p (b d)")
                    v.tensor_tensor(xs, xs, m.bank[4 + c][:], ALU.add).then_inc(x_done, 1)

            @block.tensor
            def _(pe):
                for c in range(NC4):
                    pe.wait_ge(att_ready, TPC * (s4 + c + 1))
                    for t4 in range(TPC):
                        mm = pe.transpose(m.bank[c][:, t4 * P:(t4 + 1) * P], att[:, c * TPC + t4], m.consts[:, C_ID:C_ID + P])
                    mm.then_inc(turned, 1)
                for c in range(NC4):
                    pe.wait_ge(attT_ready, s4 + c + 1)
                    for t4 in range(TPC):
                        b = c * TPC + t4
                        mm = pe.matmul(m.bank[4 + c][:, t4 * P:(t4 + 1) * P], attT[:, b * P:(b + 1) * P], m.wo[L][:], start=True, stop=True)
                    mm.then_inc(o_ready, 1)

            @block.scalar
            def _(act):
                for c in range(NC4):
                    act.wait_ge(turned, s4 + c + 1)
                    act.copy(attT[:, c * CH:(c + 1) * CH], m.bank[c][:]).then_inc(attT_ready, 1)


def route(nc, m, L, dram):
    with ExitStack() as ctx:
        sb = lambda name, s, d=F32: ctx.enter_context(nc.sbuf_tensor(f"{name}_rt{L}", s, d))
        hT = m.hT
        S3 = [P, TILES, E8]
        val, eq, cand, sel2, oh1, oh2, both = (sb(k, S3) for k in "val eq cand sel2 oh1 oh2 both".split())
        m1, m2, ix, sm, dif, ex, pf = (sb(k, [P, TILES]) for k in "m1 m2 ix sm dif ex pf".split())
        tot, run = sb("tot", [P, E8, TILES]), sb("run", [P, E8, TILES])
        rank = sb("rank", S3)
        npad, cmp, endt, texp = sb("npad", [P, E8]), sb("cmp", [P, E8, TILES]), sb("endt", [P, E8]), sb("texp", [P, 40])
        zero8, ones = sb("zero8", [P, P]), sb("ones", [P, P])
        grid = sb("grid", [P, 40, E8])
        turned, ht_ready, logits_ready, counted = (m.sem("rt_" + n) for n in "turned ht logits counted".split())
        both_ready, exp_in, exp_out, pos_ready, scattered = (m.sem("rt_" + n) for n in "both exp_in exp_out pos scattered".split())
        k = m.rt_chain
        s4 = L * NC4
        C = m.consts
        iota = C[:, C_I8:C_I8 + E8].unsqueeze(1).to_broadcast(S3)
        bc = lambda a: a.unsqueeze(2).to_broadcast(S3)
        f2 = lambda a: a.rearrange("p b e -> p (b e)")
        with nc.Block() as block:
            @block.tensor
            def _(pe):
                for c in range(NC4):
                    for t4 in range(TPC):
                        mm = pe.transpose(m.bank[c][:, t4 * P:(t4 + 1) * P], m.xn[:, c * TPC + t4], C[:, C_ID:C_ID + P])
                    mm.then_inc(turned, 1)
                for c in range(NC4):
                    pe.wait_ge(ht_ready, s4 + c + 1)
                    for b in range(c * TPC, (c + 1) * TPC):
                        mm = pe.matmul(m.bank[4][:, b * E8:(b + 1) * E8], hT[:, b * P:(b + 1) * P], m.wr[L][:], start=True, stop=True)
                mm.then_inc(logits_ready, 1)
                pe.wait_ge(both_ready, 2 * L + 2)
                pe.matmul(m.bank[5][:, 0:P], C[:, C_UP:C_UP + P], f2(both[:]), start=True, stop=True)
                pe.matmul(m.bank[6][:, 0:P], ones[:], f2(both[:]), start=True, stop=True).then_inc(counted, 1)

            @block.scalar
            def _(act):
                for c in range(NC4):
                    act.wait_ge(turned, s4 + c + 1)
                    act.activation(hT[:, c * CH:(c + 1) * CH], m.bank[c][:], ACT.Identity, bias=m.modc[:, 4 * L + 2:4 * L + 3],
                                   scale=m.modc[:, 4 * L + 3:4 * L + 4]).then_inc(ht_ready, 1)
                act.wait_ge(exp_in, L + 1)
                if L == 0:
                    act.activation(ex[:], dif[:], ACT.Exp).then_inc(exp_out, 1)
                else:
                    act.activation(f2(val[:]), f2(val[:]), ACT.Exp).then_inc(exp_out, 1)

            @block.vector
            def _(v):
                v.memset(ones[:], 1.).then_inc(both_ready, 1)
                v.memset(zero8[:], 0.).then_inc(k.sem, 1)
                v.wait_ge(logits_ready, L + 1)
                v.tensor_copy(f2(val[:]), m.bank[4][:, 0:P]).then_inc(k.sem, 1)
                v.wait_ge(k.sem, k.next(2))
                if L == 1:
                    v.tensor_reduce(m1[:], val[:], AX.X, ALU.max).then_inc(k.sem, 1)
                    v.wait_ge(k.sem, k.next())
                    v.tensor_tensor(val[:], val[:], bc(m1[:]), ALU.subtract).then_inc(exp_in, 2 - L)
                    v.wait_ge(exp_out, L + 1)
                    v.tensor_reduce(sm[:], val[:], AX.X, ALU.add).then_inc(k.sem, 1)
                    v.wait_ge(k.sem, k.next())
                    v.reciprocal(sm[:], sm[:]).then_inc(k.sem, 1)
                    v.wait_ge(k.sem, k.next())
                    v.tensor_tensor(val[:], val[:], bc(sm[:]), ALU.mult).then_inc(k.sem, 1)
                    v.wait_ge(k.sem, k.next())

                for src, top, oh in ((val, m1, oh1), (sel2, m2, oh2)):
                    v.tensor_reduce(top[:], src[:], AX.X, ALU.max).then_inc(k.sem, 1)
                    v.wait_ge(k.sem, k.next())
                    v.tensor_tensor(eq[:], src[:], bc(top[:]), ALU.is_ge).then_inc(k.sem, 1)
                    v.wait_ge(k.sem, k.next())
                    v.tensor_tensor(cand[:], eq[:], iota, ALU.mult).then_inc(k.sem, 1)
                    v.wait_ge(k.sem, k.next())
                    v.tensor_reduce(ix[:], cand[:], AX.X, ALU.min).then_inc(k.sem, 1)
                    v.wait_ge(k.sem, k.next())
                    v.tensor_tensor(oh[:], iota, bc(ix[:]), ALU.is_equal).then_inc(k.sem, 1)
                    v.wait_ge(k.sem, k.next())
                    if src is val:
                        v.scalar_tensor_tensor(f2(sel2[:]), f2(oh1[:]), NEG, f2(val[:]), ALU.mult, ALU.add).then_inc(k.sem, 1)
                        v.wait_ge(k.sem, k.next())
                v.tensor_tensor(both[:], oh1[:], oh2[:], ALU.add).then_inc(both_ready, 1)
                if L == 0:
                    v.tensor_tensor(dif[:], m2[:], m1[:], ALU.subtract).then_inc(exp_in, 1)
                    v.wait_ge(exp_out, 1)
                    v.tensor_scalar(sm[:], ex[:], 1., None, ALU.add).then_inc(k.sem, 1)
                    v.wait_ge(k.sem, k.next())
                    v.reciprocal(m.wt[:, 0], sm[:]).then_inc(k.sem, 1)
                    v.wait_ge(k.sem, k.next())
                    v.tensor_tensor(m.wt[:, 1], ex[:], m.wt[:, 0], ALU.mult).then_inc(k.sem, 1)
                else:
                    v.tensor_tensor(sm[:], m1[:], m2[:], ALU.add).then_inc(k.sem, 1)
                    v.wait_ge(k.sem, k.next())
                    v.tensor_scalar(sm[:], sm[:], 1e-20, None, ALU.add).then_inc(k.sem, 1)
                    v.wait_ge(k.sem, k.next())
                    v.reciprocal(sm[:], sm[:]).then_inc(k.sem, 1)
                    v.wait_ge(k.sem, k.next())
                    v.tensor_tensor(m.wt[:, 0], m1[:], sm[:], ALU.mult).then_inc(k.sem, 1)
                    v.wait_ge(k.sem, k.next())
                    v.tensor_tensor(m.wt[:, 1], m2[:], sm[:], ALU.mult).then_inc(k.sem, 1)
                v.wait_ge(k.sem, k.next())
                v.wait_ge(counted, L + 1)
                v.tensor_copy(tot[:], m.bank[6][:, 0:P].rearrange("p (b e) -> p e b", e=E8)).then_inc(k.sem, 1)
                v.wait_ge(k.sem, k.next())
                v.tensor_tensor_scan(f2(run[:]), f2(tot[:]), zero8[:], 0., ALU.add, ALU.add).then_inc(k.sem, 1)
                v.wait_ge(k.sem, k.next())
                if L == 1:
                    v.tensor_reduce(npad[:], tot[:], AX.X, ALU.add).then_inc(k.sem, 1)
                    v.wait_ge(k.sem, k.next())
                    v.tensor_tensor(cmp[:], npad[:].unsqueeze(2).to_broadcast([P, E8, TILES]),
                                    C[:, C_TH:C_TH + TILES].unsqueeze(1).to_broadcast([P, E8, TILES]), ALU.is_gt).then_inc(k.sem, 1)
                    v.wait_ge(k.sem, k.next())
                    v.tensor_reduce(endt[:], cmp[:], AX.X, ALU.add).then_inc(k.sem, 1)
                    v.wait_ge(k.sem, k.next())
                    v.tensor_tensor_scan(texp[:, 0:E8], endt[:], zero8[:, 0:E8], 0., ALU.add, ALU.add).then_inc(k.sem, 1)
                    v.wait_ge(k.sem, k.next())
                    v.tensor_tensor(npad[:], texp[:, 0:E8], endt[:], ALU.subtract).then_inc(k.sem, 1)
                    v.tensor_tensor(grid[:], C[:, C_IT:C_IT + 40].unsqueeze(2).to_broadcast([P, 40, E8]),
                                    texp[:, 0:E8].unsqueeze(1).to_broadcast([P, 40, E8]), ALU.is_ge).then_inc(k.sem, 1)
                    v.wait_ge(k.sem, k.next(2))
                    v.tensor_scalar(npad[:], npad[:], float(P), None, ALU.mult).then_inc(k.sem, 1)
                    v.tensor_reduce(texp[:], grid[:], AX.X, ALU.add).then_inc(k.sem, 1)
                    v.wait_ge(k.sem, k.next(2))
                    v.tensor_scalar(m.tile_expert[:], texp[:], float(E8 - 1), None, ALU.min).then_inc(k.sem, 1)
                    v.tensor_tensor(endt[:], run[:, :, 0], tot[:, :, 0], ALU.subtract).then_inc(k.sem, 1)
                    v.wait_ge(k.sem, k.next(2))
                    v.tensor_tensor(npad[:], npad[:], endt[:], ALU.subtract).then_inc(k.sem, 1)
                    v.wait_ge(k.sem, k.next())
                    v.tensor_tensor(run[:], run[:], npad[:].unsqueeze(2).to_broadcast([P, E8, TILES]), ALU.add).then_inc(k.sem, 1)
                    v.wait_ge(k.sem, k.next())
                v.tensor_tensor(run[:], run[:], tot[:], ALU.subtract).then_inc(k.sem, 1)
                v.wait_ge(k.sem, k.next())
                v.tensor_tensor(rank[:], run[:].rearrange("p e b -> p b e"), m.bank[5][:, 0:P].rearrange("p (b e) -> p b e", e=E8),
                                ALU.add).then_inc(k.sem, 1)
                v.wait_ge(k.sem, k.next())
                for i, oh in enumerate((oh1, oh2)):
                    v.tensor_tensor(cand[:], oh[:], rank[:], ALU.mult).then_inc(k.sem, 1)
                    v.wait_ge(k.sem, k.next())
                    v.tensor_reduce(pf[:], cand[:], AX.X, ALU.add).then_inc(k.sem, 1)
                    v.wait_ge(k.sem, k.next())
                    v.tensor_copy(m.pos[:, i], pf[:]).then_inc(pos_ready, 1)
                    v.wait_ge(pos_ready, 2 * L + i + 1)

            @block.gpsimd
            def _(g):
                for i in range(2):
                    g.wait_ge(pos_ready, 2 * L + i + 1)
                    for b in range(TILES):
                        g.indirect_dma_start(out=dram[f"perm{L}"], out_offset=bass.IndirectOffsetOnAxis(ap=m.pos[:, i, b:b + 1], axis=0),
                                             in_=m.xn[:, b], in_offset=None).then_inc(scattered, 16)
                g.wait_ge(scattered, (L + 1) * 32 * 16)


def experts0(nc, m, dram, w1, w2):
    with ExitStack() as ctx:
        sb = lambda name, s, d=F32: ctx.enter_context(nc.sbuf_tensor(f"{name}_f0", s, d))
        rows = [sb(f"rows{i}", [P, TPC, D]) for i in range(3)]
        hT = [sb(f"hTf{i}", [P, CH]) for i in range(2)]
        hid = [sb(f"hid{i}", [P, TPC, CH]) for i in range(2)]
        eo = [sb(f"eo{i}", [P, TPC, D]) for i in range(2)]
        loaded, stored = [m.sem(f"f0_loaded{i}") for i in range(3)], [m.sem(f"f0_stored{i}") for i in range(2)]
        turned, ht_ready, up_ready, hid_ready, down_ready, eo_ready = (m.sem("f0_" + n) for n in "turned ht up hid down eo".split())
        FB = FF0 // P
        bank = m.bank
        view = lambda t, e: t.rearrange("(b p) d -> p b d", p=P)[:, e * TPC:(e + 1) * TPC]
        with nc.Block() as block:
            @block.sync
            def _(sp):
                for e in range(E8 + 2):
                    if e < E8:
                        if e >= 3:
                            sp.wait_ge(turned, e - 2)
                        sp.dma_start(rows[e % 3][:], view(dram["perm0"], e)).then_inc(loaded[e % 3], 16)
                    if e >= 2:
                        sp.wait_ge(eo_ready, e - 1)
                        sp.dma_start(view(dram["eo0"], e - 2), eo[e % 2][:]).then_inc(stored[e % 2], 16)
                for i in range(2):
                    sp.wait_ge(stored[i], 16 * E8 // 2)

            @block.tensor
            def _(pe):
                def turn(e):
                    pe.wait_ge(loaded[e % 3], 16 * (e // 3 + 1))
                    for t4 in range(TPC):
                        mm = pe.transpose(bank[e % 2][:, t4 * P:(t4 + 1) * P], rows[e % 3][:, t4], m.consts[:, C_ID:C_ID + P])
                    mm.then_inc(turned, 1)

                turn(0)
                for e in range(E8):
                    pe.wait_ge(ht_ready, e + 1)
                    for f in range(FB):
                        if e:
                            pe.wait_ge(hid_ready, (e - 1) * FB + f + 1)
                        pe.matmul(bank[2 + f][:], w1[:, e, f * P:(f + 1) * P], hT[e % 2][:], start=True, stop=True).then_inc(up_ready, 1)
                    if e + 1 < E8:
                        turn(e + 1)
                    if e >= 2:
                        pe.wait_ge(eo_ready, e - 1)
                    for t4 in range(TPC):
                        for f in range(FB):
                            if t4 == 0:
                                pe.wait_ge(hid_ready, e * FB + f + 1)
                            mm = pe.matmul(bank[6 + e % 2][:, t4 * P:(t4 + 1) * P], hid[e % 2][:, f, t4 * P:(t4 + 1) * P], w2[:, e * FB + f],
                                           start=f == 0, stop=f == FB - 1)
                    mm.then_inc(down_ready, 1)

            @block.scalar
            def _(act):
                def modulate(e):
                    act.wait_ge(turned, e + 1)
                    act.activation(hT[e % 2][:], bank[e % 2][:], ACT.Identity, bias=m.modc[:, 2:3], scale=m.modc[:, 3:4]).then_inc(ht_ready, 1)

                modulate(0)
                for e in range(E8):
                    for f in range(FB):
                        if e >= 2 and f == 0:
                            act.wait_ge(down_ready, e - 1)
                        act.wait_ge(up_ready, e * FB + f + 1)
                        act.activation(hid[e % 2][:, f], bank[2 + f][:], ACT.Gelu).then_inc(hid_ready, 1)
                    if e + 1 < E8:
                        modulate(e + 1)

            @block.vector
            def _(v):
                for e in range(E8):
                    if e >= 2:
                        v.wait_ge(stored[e % 2], 16 * (e // 2))
                    v.wait_ge(down_ready, e + 1)
                    v.tensor_tensor(eo[e % 2][:], bank[6 + e % 2][:].rearrange("p (b d) -> p b d", d=D),
                                    m.gates[:, 1:2, :].to_broadcast([P, TPC, D]), ALU.mult).then_inc(eo_ready, 1)


BLOCKS1 = [(0, P), (P, P), (2 * P, FF1 - 2 * P)]


def shared_expert(nc, m, gw, uw, dw):
    with ExitStack() as ctx:
        sb = lambda name, s, d=F32: ctx.enter_context(nc.sbuf_tensor(f"{name}_sh", s, d))
        sg = [sb(f"sg{i}", [P, CH]) for i in range(2)]
        hid = [sb(f"hid{i}", [P, 3, CH]) for i in range(2)]
        tmp = [sb(f"tmp{i}", [P, TPC, D]) for i in range(2)]
        gu_ready, silu_done, hid_ready, down_ready, tmp_ready, x_done = (m.sem("sh_" + n) for n in "gu silu hid down tmp x".split())
        bank, S = m.bank, E8
        with nc.Block() as block:
            @block.tensor
            def _(pe):
                def down(c):
                    if c >= 2:
                        pe.wait_ge(tmp_ready, c - 1)
                    pe.wait_ge(hid_ready, 3 * c + 3)
                    for t4 in range(TPC):
                        for f, (o, w) in enumerate(BLOCKS1):
                            mm = pe.matmul(bank[4 + c % 2][:, t4 * P:(t4 + 1) * P], hid[c % 2][0:w, f, t4 * P:(t4 + 1) * P],
                                           dw[0:w, S, f], start=f == 0, stop=f == 2)
                    mm.then_inc(down_ready, 1)

                for c in range(NC4):
                    for f, (o, w) in enumerate(BLOCKS1):
                        n = 3 * c + f
                        if n >= 2:
                            pe.wait_ge(hid_ready, n - 1)
                        for z, wt in enumerate((gw, uw)):
                            mm = pe.matmul(bank[2 * (n % 2) + z][0:w], wt[:, S, o:o + w], m.hT[:, c * CH:(c + 1) * CH], start=True, stop=True)
                        mm.then_inc(gu_ready, 1)
                    if c:
                        down(c - 1)
                down(NC4 - 1)

            @block.scalar
            def _(act):
                for n in range(3 * NC4):
                    w = BLOCKS1[n % 3][1]
                    if n >= 2:
                        act.wait_ge(hid_ready, n - 1)
                    act.wait_ge(gu_ready, n + 1)
                    act.activation(sg[n % 2][0:w], bank[2 * (n % 2)][0:w], ACT.Silu).then_inc(silu_done, 1)

            @block.vector
            def _(v):
                def finish(c):
                    v.wait_ge(down_ready, c + 1)
                    v.tensor_tensor(tmp[c % 2][:], bank[4 + c % 2][:].rearrange("p (b d) -> p b d", d=D),
                                    m.gates[:, 3:4, :].to_broadcast([P, TPC, D]), ALU.mult).then_inc(tmp_ready, 1)
                    v.wait_ge(tmp_ready, c + 1)
                    xs = m.x[:, c * TPC:(c + 1) * TPC]
                    v.tensor_tensor(xs, xs, tmp[c % 2][:], ALU.add).then_inc(x_done, 1)
                    v.wait_ge(x_done, c + 1)

                for n in range(3 * NC4):
                    c, f = divmod(n, 3)
                    w = BLOCKS1[f][1]
                    if c >= 2 and f == 0:
                        v.wait_ge(down_ready, c - 1)
                    v.wait_ge(silu_done, n + 1)
                    v.tensor_tensor(hid[c % 2][0:w, f], bank[2 * (n % 2) + 1][0:w], sg[n % 2][0:w], ALU.mult).then_inc(hid_ready, 1)
                    if f == 2 and c:
                        finish(c - 1)
                finish(NC4 - 1)


def experts1(nc, m, dram, gw, uw, dw):
    with ExitStack() as ctx:
        sb = lambda name, s, d=F32: ctx.enter_context(nc.sbuf_tensor(f"{name}_f1", s, d))
        rows = [sb(f"rows{i}", [P, D]) for i in range(4)]
        hT = [sb(f"hTt{i}", [P, P]) for i in range(2)]
        sg = [sb(f"sg{i}", [P, FF1]) for i in range(2)]
        hid = [sb(f"hid{i}", [P, FF1]) for i in range(2)]
        hidT = [sb(f"hidT{i}", [P, 3, P]) for i in range(2)]
        eo = [sb(f"eo{i}", [P, D]) for i in range(4)]
        loaded, stored = [m.sem(f"f1_loaded{i}") for i in range(4)], [m.sem(f"f1_stored{i}") for i in range(4)]
        (turned, ht_ready, gu_ready, silu_done, hid_ready, hid_turned, hidT_ready, down_ready, eo_ready) = (
            m.sem("f1_" + n) for n in "turned ht gu silu hid hid_turned hidT down eo".split())
        G, U, X, O = m.bank[0:2], m.bank[2:4], m.bank[4:6], m.bank[6:8]
        N, ident = RTILES1, m.consts[:, C_ID:C_ID + P]
        with nc.Block() as block:
            @block.sync
            def _(sp):
                def load(n, z, q):
                    sp.dma_start(rows[z][:], dram["perm1"][bass.ds(n * P, P)]).then_inc(loaded[z], 16)

                def store(n, z):
                    sp.wait_ge(eo_ready, n + 1)
                    sp.dma_start(dram["eo1"][bass.ds(n * P, P)], eo[z][:]).then_inc(stored[z], 16)

                for n in range(4):
                    load(n, n, 0)
                with sp.Fori(0, N // 4 - 1) as i:
                    for z in range(4):
                        store(4 * i + z, z)
                        sp.wait_ge(turned, 4 * i + z + 1)
                        load(4 * i + 4 + z, z, i + 1)
                for n in range(N - 4, N):
                    store(n, n % 4)
                for z in range(4):
                    sp.wait_ge(stored[z], 16 * (N // 4))

            @block.tensor
            def _(pe):
                expert = lambda n: pe.value_load(m.tile_expert[0:1, bass.ds(n, 1)], min_val=0, max_val=E8 - 1)

                def turn(z, q):
                    pe.wait_ge(loaded[z], 16 * (q + 1))
                    pe.transpose(X[z % 2][:, 0:P], rows[z][:], ident).then_inc(turned, 1)

                def gate_up(n, z):
                    e = expert(n)
                    pe.wait_ge(ht_ready, n + 1)
                    pe.matmul(G[z % 2][:, 0:FF1], hT[z % 2][:], gw[:, bass.ds(e, 1), :], start=True, stop=True)
                    pe.matmul(U[z % 2][:, 0:FF1], hT[z % 2][:], uw[:, bass.ds(e, 1), :], start=True, stop=True).then_inc(gu_ready, 1)

                def down(n, z, reused=True, later=True):
                    e = expert(n)
                    pe.wait_ge(hid_ready, n + 1)
                    if later:
                        pe.wait_ge(ht_ready, n + 3)
                    for f, (o, w) in enumerate(BLOCKS1):
                        mm = pe.transpose(X[z % 2][0:w, (f + 1) * P:(f + 2) * P], hid[z % 2][:, o:o + w], ident)
                    mm.then_inc(hid_turned, 1)
                    if reused:
                        pe.wait_ge(eo_ready, n - 1)
                    pe.wait_ge(hidT_ready, n + 1)
                    for f, (o, w) in enumerate(BLOCKS1):
                        mm = pe.matmul(O[z % 2][:, 0:P], hidT[z % 2][0:w, f], dw[0:w, bass.ds(e, 1), f], start=f == 0, stop=f == 2)
                    mm.then_inc(down_ready, 1)

                turn(0, 0)
                turn(1, 0)
                gate_up(0, 0)
                for n in range(1, 5):
                    turn((n + 1) % 4, (n + 1) // 4)
                    gate_up(n, n % 4)
                    down(n - 1, (n - 1) % 4, n >= 3)
                with pe.Fori(1, N // 4 - 1) as i:
                    for z in range(1, 5):
                        turn((z + 1) % 4, i + (z + 1) // 4)
                        gate_up(4 * i + z, z % 4)
                        down(4 * i + z - 1, (z - 1) % 4)
                for n in range(N - 3, N):
                    if n + 1 < N:
                        turn((n + 1) % 4, (n + 1) // 4)
                    gate_up(n, n % 4)
                    down(n - 1, (n - 1) % 4, True, n + 1 < N)
                down(N - 1, 3, True, False)

            @block.scalar
            def _(act):
                def modulate(n, z):
                    act.wait_ge(turned, n + 1)
                    act.activation(hT[z % 2][:], X[z % 2][:, 0:P], ACT.Identity, bias=m.modc[:, 6:7], scale=m.modc[:, 7:8]).then_inc(ht_ready, 1)

                def silu(n, z, reused=True):
                    if reused:
                        act.wait_ge(hid_ready, n - 1)
                    act.wait_ge(gu_ready, n + 1)
                    act.activation(sg[z % 2][:], G[z % 2][:, 0:FF1], ACT.Silu).then_inc(silu_done, 1)

                modulate(0, 0)
                for n in range(4):
                    modulate(n + 1, n + 1)
                    silu(n, n, n >= 2)
                with act.Fori(1, N // 4 - 1) as i:
                    for z in range(4):
                        modulate(4 * i + z + 1, z + 1)
                        silu(4 * i + z, z)
                for n in range(N - 4, N):
                    if n + 1 < N:
                        modulate(n + 1, n + 1)
                    silu(n, n)

            @block.vector
            def _(v):
                def hidden(n, z):
                    v.wait_ge(silu_done, n + 1)
                    v.tensor_tensor(hid[z % 2][:], U[z % 2][:, 0:FF1], sg[z % 2][:], ALU.mult).then_inc(hid_ready, 1)

                def finish(n, z, q, reused=True):
                    v.wait_ge(hid_turned, n + 1)
                    v.tensor_copy(hidT[z % 2][:], X[z % 2][:, P:4 * P].rearrange("p (f t) -> p f t", t=P)).then_inc(hidT_ready, 1)
                    if reused:
                        v.wait_ge(stored[z % 4], 16 * q)
                    v.wait_ge(down_ready, n + 1)
                    v.tensor_tensor(eo[z % 4][:], O[z % 2][:, 0:P], m.gates[:, 3], ALU.mult).then_inc(eo_ready, 1)

                hidden(0, 0)
                for n in range(1, 5):
                    hidden(n, n)
                    finish(n - 1, n - 1, 0, False)
                with v.Fori(1, N // 4 - 1) as i:
                    for z in range(1, 5):
                        hidden(4 * i + z, z)
                        finish(4 * i + z - 1, z - 1, i)
                for n in range(N - 3, N):
                    hidden(n, n)
                    finish(n - 1, n - 1, (n - 1) // 4)
                finish(N - 1, 3, (N - 1) // 4)


def combine(nc, m, L, dram, out):
    with ExitStack() as ctx:
        sb = lambda name, s, d=F32: ctx.enter_context(nc.sbuf_tensor(f"{name}_cb{L}", s, d))
        got = sb("got", [P, 2, TILES, D])
        gathered, added, written = [m.sem(f"cb_gathered{c}") for c in range(NC4)], m.sem("cb_added"), m.sem("cb_written")
        with nc.Block() as block:
            @block.gpsimd
            def _(g):
                for c in range(NC4):
                    for b in range(c * TPC, (c + 1) * TPC):
                        for i in range(2):
                            g.indirect_dma_start(out=got[:, i, b], out_offset=None, in_=dram[f"eo{L}"],
                                                 in_offset=bass.IndirectOffsetOnAxis(ap=m.pos[:, i, b:b + 1], axis=0)).then_inc(gathered[c], 16)

            @block.vector
            def _(v):
                for c in range(NC4):
                    v.wait_ge(gathered[c], 128 * (L + 1))
                    for i in range(2):
                        for b in range(c * TPC, (c + 1) * TPC):
                            v.scalar_tensor_tensor(m.x[:, b], got[:, i, b], m.wt[:, i, b:b + 1], m.x[:, b], ALU.mult, ALU.add).then_inc(added, 1)
                        v.wait_ge(added, (L * NC4 + c) * 2 * TPC + (i + 1) * TPC)

            if L == 1:
                @block.sync
                def _(sp):
                    for c in range(NC4):
                        sp.wait_ge(added, (NC4 + c + 1) * 2 * TPC)
                        sp.dma_start(out[0].rearrange("(b p) d -> p b d", p=P)[:, c * TPC:(c + 1) * TPC], m.x[:, c * TPC:(c + 1) * TPC]).then_inc(written, 16)
                    sp.wait_ge(written, 16 * NC4)


class Memory:

    def __init__(self, nc, ctx):
        sb = lambda n, s, d=F32: ctx.enter_context(nc.sbuf_tensor(n, s, d))
        self.sems = {}
        self.new_sem = lambda n: ctx.enter_context(nc.semaphore(n))
        self.x, self.xn, self.vall = sb("x", [P, TILES, D]), sb("xn", [P, TILES, D]), sb("vall", [P, TILES, D])
        self.QS = [sb(f"qs{p}", [P, GH, T], BF) for p in range(2)]
        self.KS = [sb(f"ks{p}", [P, GH, T], BF) for p in range(2)]
        self.araw = sb("araw", [P, TILES, H, HD + 1])
        self.consts = sb("consts_sb", [P, C_W])
        self.identb, self.maskTb, self.maskN = sb("identb", [P, P], BF), sb("maskTb", [P, P], BF), sb("maskN", [P, CH])
        self.wo, self.wr = [sb(f"wo{l}", [P, D]) for l in range(2)], [sb(f"wr{l}", [P, E8]) for l in range(2)]
        self.wq, self.wqr, self.wdkv = sb("wq", [P, D]), sb("wqr", [P, D]), sb("wdkv", [P, LAT])
        self.wuk, self.wukr, self.wuv = sb("wuk", [LAT, D]), sb("wukr", [LAT, D]), sb("wuv", [LAT, D])
        self.w1small, self.w1bd = sb("w1small", [P, 3, HD]), sb("w1bd", [P, 3, D])
        self.lngb, self.modc, self.gates = sb("lngb", [LAT, 2]), sb("modc", [P, 8]), sb("gates", [P, 4, D])
        self.wt, self.pos = sb("wt", [P, 2, TILES]), sb("pos", [P, 2, TILES], U32)
        self.tile_expert = sb("tile_expert", [P, 40], I32)
        self.st = [ctx.enter_context(nc.psum_tensor(f"st{i}", [P, 2, CH], F32)) for i in range(2)]
        self.mxb = [ctx.enter_context(nc.psum_tensor(f"mx{i}", [P, CH], F32)) for i in range(MXBUF)]
        self.avb = ctx.enter_context(nc.psum_tensor("av", [P, CH], F32))
        self.bank = [self.st[0][:, 0], self.st[0][:, 1], self.st[1][:, 0], self.st[1][:, 1]] + [b[:] for b in self.mxb] + [self.avb[:]]
        self.ln_chain, self.pj_chain, self.rt_chain = (Count(self.sem(n)) for n in ("ln_chain", "pj_chain", "rt_chain"))
        self.weights_total = 0

    def sem(self, name):
        if name not in self.sems:
            self.sems[name] = self.new_sem(name)
        return self.sems[name]


def adaln_two_layers(nc, *aps):
    dram = dict(zip(INPUTS, aps))
    out = aps[-1]
    for L in range(2):
        for key in ("q_parts", "k_parts"):
            dram[f"{key}{L}"] = nc.dram_tensor(f"{key}{L}", [H * 3 * HD, T], BF).ap()
        for key, n in (("perm", (ROWS0, ROWS1)), ("eo", (ROWS0, ROWS1))):
            dram[f"{key}{L}"] = nc.dram_tensor(f"{key}{L}", [n[L], D], F32).ap()
    with ExitStack() as ctx:
        m = Memory(nc, ctx)
        setup(nc, m, None, dram)
        for L in range(2):
            layer_norm(nc, m, 2 * L)
            project(nc, m, L, dram)
            with ExitStack() as wctx:
                sb = lambda n, s: wctx.enter_context(nc.sbuf_tensor(n, s, F32))
                if L == 0:
                    w1, w2 = sb("w1_sb", [P, E8, FF0]), sb("w2_sb", [P, E8 * FF0 // P, D])
                    weight_loads = [(w1[:], dram["w1"].rearrange("e d f -> d e f"))] + [
                        (w2[:, 4 * e:4 * e + 4], dram["w2"][e].rearrange("(k p) d -> p k d", p=P)) for e in range(E8)]
                else:
                    gw, uw, dw = sb("gw_sb", [P, E8 + 1, FF1]), sb("uw_sb", [P, E8 + 1, FF1]), sb("dw_sb", [P, E8 + 1, 3, D])
                    weight_loads = [(gw[:], dram["gw"]), (uw[:], dram["uw"]), (dw[:], dram["dw"])]
                m.weights_total += len(weight_loads)
                attention(nc, m, L, dram, weight_loads)
                output_projection(nc, m, L)
                layer_norm(nc, m, 2 * L + 1)
                m.hT = wctx.enter_context(nc.sbuf_tensor(f"hT{L}", [P, T], F32))
                route(nc, m, L, dram)
                if L == 0:
                    experts0(nc, m, dram, w1, w2)
                else:
                    shared_expert(nc, m, gw, uw, dw)
                    experts1(nc, m, dram, gw, uw, dw)
            combine(nc, m, L, dram, out)


INPUTS = ["x", "consts", "cos", "sin", "zo", "c0", "wmod0", "c1", "wmod1", "wq0", "wdkv", "wuk", "wuv", "wo0", "ln_gamma",
          "ln_beta", "wr0", "w1", "w2", "wq1", "wk1", "wv1", "wo1", "wr1", "gw", "uw", "dw"]


def layout(i):
    a = {k: np.asarray(v) for k, v in i.items()}
    q = np.arange(P)
    consts = np.zeros((P, C_W), np.float32)
    consts[:, C_ID:C_ID + P] = np.eye(P)
    consts[:, C_MN:C_MN + P] = np.where(q[None, :] <= q[:, None], 0, NEG)
    consts[:, C_MT:C_MT + P] = np.where(q[:, None] <= q[None, :], 0, NEG)
    consts[:, C_UP:C_UP + P] = q[:, None] < q[None, :]
    consts[:, C_BD:C_BD + P] = q[:, None] // HD == q[None, :] // HD
    consts[:, C_I8:C_I8 + E8] = np.arange(E8) - E8
    consts[:, C_IT:C_IT + 40] = np.arange(40)
    consts[:, C_TH:C_TH + TILES] = P * np.arange(TILES)
    half = HD // 2
    inv = (np.float32(1.0) / np.float32(10000.0) ** (np.arange(half, dtype=np.float32) / np.float32(half))).astype(np.float32)
    ang = (np.arange(T, dtype=np.float32)[None, :] * inv[:, None]).astype(np.float32)
    ones = np.zeros((GH, 2 * GH, T), np.dtype("bfloat16"))
    for j in range(GH):
        ones[j, 2 * j:2 * j + 2] = 1
    dw = np.zeros((E8 + 1, 3 * P, D), np.float32)
    dw[:E8, :FF1] = a["L1_ffn_expert_down"].transpose(0, 2, 1)
    dw[E8, :FF1] = a["L1_ffn_shared_down"].T
    both = lambda e, s: np.concatenate([a[e], a[s][None]]).transpose(2, 0, 1)
    return {
        "x": a["L0_attn_x"][0], "consts": consts, "cos": np.cos(ang).astype(np.float32), "sin": np.sin(ang).astype(np.float32),
        "zo": ones, "c0": a["L0_c"], "wmod0": a["L0_wmod"], "c1": a["L1_c"], "wmod1": a["L1_wmod"], "wq0": a["L0_attn_W_q"],
        "wdkv": a["L0_attn_W_dkv"], "wuk": a["L0_attn_W_uk"], "wuv": a["L0_attn_W_uv"], "wo0": a["L0_attn_W_o"],
        "ln_gamma": a["L0_attn_ln_gamma"][:, None], "ln_beta": a["L0_attn_ln_beta"][:, None], "wr0": a["L0_ffn_Wr"].T,
        "w1": a["L0_ffn_W1"], "w2": a["L0_ffn_W2"], "wq1": a["L1_attn_Wq"].reshape(P, HD), "wk1": a["L1_attn_Wk"].reshape(P, HD),
        "wv1": a["L1_attn_Wv"].reshape(P, HD), "wo1": a["L1_attn_Wo"], "wr1": a["L1_ffn_gate_w"].T,
        "gw": both("L1_ffn_expert_gate", "L1_ffn_shared_gate"), "uw": both("L1_ffn_expert_up", "L1_ffn_shared_up"),
        "dw": dw.reshape(E8 + 1, 3, P, D).transpose(2, 0, 1, 3)}


def kernel(**inputs):
    import concourse.bacc as bacc
    from concourse.bass_utils import run_bass_kernel_spmd

    nc = bacc.Bacc("TRN2", target_bir_lowering=False, num_devices=1)
    arrays, args = {}, []
    laid = layout(inputs)
    for name in INPUTS:
        a = np.ascontiguousarray(laid[name])
        arrays[f"in_{name}_dram"] = a
        args.append(nc.dram_tensor(f"in_{name}_dram", a.shape, mybir.dt.from_np(a.dtype), kind="ExternalInput").ap())
    args.append(nc.dram_tensor("out_0_dram", (1, T, D), F32, kind="ExternalOutput").ap())
    adaln_two_layers(nc, *args)
    r = run_bass_kernel_spmd(nc, [arrays], core_ids=[0])
    return r.results[0]["out_0_dram"]
```

```python
import numpy as np
import concourse.bass as bass
from concourse import mybir
from concourse.alu_op_type import AluOpType as ALU
from contextlib import ExitStack

F32 = mybir.dt.float32
BF = mybir.dt.bfloat16
U32 = mybir.dt.uint32
I32 = mybir.dt.int32
ACT = mybir.ActivationFunctionType
AX = mybir.AxisListType

P = 128
T = 2048
D = 128
H, HD = 16, 8
TILES = T // P
CH = 512
NC4 = T // CH
TPC = CH // P
LAT = 32
E8 = 8
FF0, FF1 = 512, 352
EPS = 1e-5
NEG = -1e30
SCALE = float(1 / np.sqrt(np.float32(HD)))
GH = 4
NG = H // GH
SHIFT0 = 96
MXBUF = 3

ROWS0 = 2 * T
RTILES1 = 2 * T // P + E8
ROWS1 = RTILES1 * P

C_ID, C_MN, C_MT, C_UP, C_BD, C_I8, C_IT, C_TH, C_W = 0, 128, 256, 384, 512, 640, 648, 688, 704
PACK = [("consts", C_W), ("wq0", D), ("wdkv", LAT), ("wo0", D), ("wo1", D), ("wr0", E8), ("wr1", E8), ("w1small", 3 * HD)]
W_PACK = sum(w for _, w in PACK)
W_MOD = 2 + 12 * D

UNITS = [(0, 0), (0, 2), (0, 1), (1, 0), (0, 3), (1, 2), (1, 3), (1, 1),
         (2, 3), (2, 2), (3, 3), (2, 1), (3, 1), (2, 0), (3, 2), (3, 0)]
STEPS = [(g, Q, kb) for g, Q in UNITS for kb in range(TPC * (Q + 1))]
NU, NST = len(UNITS), len(STEPS)
UNIT = [UNITS.index(s[:2]) for s in STEPS]
FIRST = [UNIT.index(u) for u in range(NU)] + [NST]
FIRST_UNIT = [min(u for u, x in enumerate(UNITS) if x[0] == g) for g in range(NG)]
LAST = [max(s for s, x in enumerate(STEPS) if x[0] == g) for g in range(NG)]
TURN_LAG = 3


def max_tiles(g, Q):
    return [(g, Q, j, qb, c) for qb in range(TPC) for j in range(GH) for c in range(Q + 1)]


def max_width(m):
    return CH if m[4] < m[1] else (m[3] + 1) * P


def step_off(s):
    return max(0, STEPS[s][2] * P - STEPS[s][1] * CH)


def schedule():
    base, due = [], []
    for u, (g, Q) in enumerate(UNITS):
        for m in max_tiles(g, Q):
            base.append(("max", m))
            if due and due[0][0] <= len(base):
                base.append(("turn", due.pop(0)[1]))
        due.append((len(base) + TURN_LAG, u))
    base += [("turn", u) for _, u in due]
    pe = dve = act = 0.0
    out, rot = [], []
    k = s = half = 0
    lat = 0.1
    ready = [1e9] * NU
    free = [0.0] * MXBUF
    last_max, exp_done = {}, [0.0, 0.0]
    loaded = [0.0, 22.0] + [1e9] * NG
    norms = []
    while k < len(base) or s < NST or norms:
        b = len(rot) % MXBUF
        if norms and norms[0][0] <= pe or (k == len(base) and s == NST):
            pe = max(pe, free[b] + lat) + .4
            dve = max(dve, pe + lat) + .3
            free[b] = dve
            out.append(("rot", len(rot)))
            rot.append(("norm", norms.pop(0)[1]))
            continue
        t_step = max(pe, ready[UNIT[s]], exp_done[half] + lat) if s < NST and ready[UNIT[s]] < 1e8 else 1e9
        t_max = 1e9
        if k < len(base):
            kind, x = base[k]
            t_max = max(pe, free[b] + lat)
            if kind == "max":
                t_max = max(t_max, loaded[x[0]])
            else:
                t_max = max(t_max, last_max[x] + .6)
        if t_max <= t_step + 0.2 and k < len(base):
            pe = t_max
            if kind == "max":
                w = max_width(x)
                pe += w / 2400 + .003
                dve = max(dve, pe + lat + .1) + .075 + w * .00104
                last_max[UNITS.index(x[:2])] = dve
            else:
                pe += .22
                dve = max(dve, pe + lat) + .6
                ready[x] = dve + 2.4
            free[b] = dve
            out.append(("rot", len(rot)))
            rot.append((kind, x))
            k += 1
        else:
            pe = t_step
            w = CH - step_off(s)
            pe += 2 * w / 2400 + (.11 if STEPS[s][2] >= TPC * STEPS[s][1] else 0)
            act = max(act, pe + lat + .1) + .19 + 2 * w * .000833
            exp_done[half] = act
            out.append(("scores", s, half))
            if half == 1:
                if s:
                    out.append(("av", s - 1))
                    pe += 4 * (CH - step_off(s - 1)) / 2400
                    if s - 1 in LAST:
                        loaded[LAST.index(s - 1) + 2] = pe + 9
                    if s in FIRST:
                        norms.append((pe + 3, UNIT[s] - 1))
                s += 1
                if s == NST:
                    out.append(("av", NST - 1))
                    norms.append((pe + 3, NU - 1))
            half ^= 1
    return out, rot


ORDER, ROT = schedule()
NROT = len(ROT)
NORM_AT = {x: k for k, (kind, x) in enumerate(ROT) if kind == "norm"}


class Count:

    def __init__(self, sem):
        self.sem, self.value = sem, 0

    def next(self, n=1):
        self.value += n
        return self.value


def setup(nc, m, dram):
    with ExitStack() as ctx:
        sb = lambda n, s, d=F32: ctx.enter_context(nc.sbuf_tensor(n, s, d))
        mod = sb("mod", [P, W_MOD])
        scol, sbc = sb("scol", [P, 2]), sb("sbc", [P, 2, P])
        gate, sign = sb("gate", [P, 4, D]), sb("sign", [P, 4, D])
        wmod = lambda l, part: mod[:, 2 + (6 * l + part) * D:2 + (6 * l + part + 1) * D]
        mod_loaded, pack_loaded = m.sem("mod_loaded"), m.sem("pack_loaded")
        silu_done, bc_done, cols_ready, rows_ready = (m.sem(n) for n in ("silu_done", "bc_done", "cols_ready", "rows_ready"))
        gates, weights_ready, pool_set = Count(m.sem("gates_chain")), m.sem("weights_ready"), m.sem("pool_set")

        with nc.Block() as block:
            @block.sync
            def _(sp):
                sp.dma_start(mod[:], dram["mod"]).then_inc(mod_loaded, 16)
                for z in range(NC4):
                    sp.dma_start(m.x[:, 4 * z:4 * z + 4], dram["x"].rearrange("(b p) d -> p b d", p=P)[:, 4 * z:4 * z + 4]).then_inc(m.sem("x_loaded"), 16)
                sp.dma_start(m.pack[:], dram["pack"]).then_inc(pack_loaded, 16)
                sp.dma_start(m.lpack[:], dram["lpack"]).then_inc(pack_loaded, 16)
                for dst, key in ((m.cosT, "cos"), (m.sinT, "sin")):
                    sp.dma_start(dst[:], bass.AP(dram[key].tensor, 0, [[0, 2 * H], [T, HD // 2], [1, T]])).then_inc(m.sem("tables"), 16)
                sp.wait_ge(m.sem("x_loaded"), 16 * NC4)

            @block.scalar
            def _(act):
                act.wait_ge(mod_loaded, 16)
                act.activation(scol[:], mod[:, 0:2], ACT.Silu).then_inc(silu_done, 1)

            @block.tensor
            def _(pe):
                pe.wait_ge(bc_done, 2)
                for l in range(2):
                    for i, part in enumerate((0, 1, 3, 4)):
                        mm = pe.matmul(m.bank[0][:, 4 * l + i:4 * l + i + 1], wmod(l, part), scol[:, l:l + 1], start=True, stop=True)
                mm.then_inc(cols_ready, 1)
                for l in range(2):
                    for i, part in enumerate((2, 5)):
                        mm = pe.matmul(m.bank[1][:, (2 * l + i) * D:(2 * l + i + 1) * D], sbc[:, l, :], wmod(l, part), start=True, stop=True)
                mm.then_inc(rows_ready, 1)

            @block.gpsimd
            def _(g):
                for p in range(2):
                    g.memset(m.VS[p][:], 0.).then_inc(pool_set, 1)
                g.wait_ge(pool_set, 2)
                for p in range(2):
                    g.memset(m.VS[p][:, :, :, HD:HD + 1], 1.).then_inc(pool_set, 1)

            @block.vector
            def _(v):
                v.wait_ge(silu_done, 1)
                for l in range(2):
                    v.tensor_copy(sbc[:, l, :], scol[:, l:l + 1].to_broadcast([P, P])).then_inc(bc_done, 1)
                v.wait_ge(pack_loaded, 32)
                for src, dst in ((m.wq, m.wqr), (m.wuk, m.wukr)):
                    a = src.rearrange("p (h u d) -> p h u d", u=2, d=HD // 2)
                    b = dst[:].rearrange("p (h u d) -> p h u d", u=2, d=HD // 2)
                    v.tensor_scalar(b[:, :, 0], a[:, :, 1], -1., None, ALU.mult).then_inc(weights_ready, 1)
                    v.tensor_copy(b[:, :, 1], a[:, :, 0]).then_inc(weights_ready, 1)
                for i in range(3):
                    v.tensor_tensor(m.w1bd[:, i].rearrange("p (h e) -> p h e", e=HD),
                                    m.consts[:, C_BD:C_BD + P].rearrange("p (h e) -> p h e", e=HD),
                                    m.w1small[:, i:i + 1, :].to_broadcast([P, H, HD]), ALU.mult).then_inc(weights_ready, 1)
                v.tensor_copy(m.identb[:], m.consts[:, C_ID:C_ID + P]).then_inc(weights_ready, 1)
                v.tensor_copy(m.maskTb[:], m.consts[:, C_MT:C_MT + P]).then_inc(weights_ready, 1)
                v.memset(m.maskN[:, 0:CH - P], 0.).then_inc(weights_ready, 1)
                v.tensor_copy(m.maskN[:, CH - P:], m.consts[:, C_MN:C_MN + P]).then_inc(weights_ready, 1)
                v.wait_ge(cols_ready, 1)
                v.tensor_copy(m.modc[:], m.bank[0][:, 0:8]).then_inc(gates.sem, 1)
                v.wait_ge(gates.sem, gates.next())
                for i in (1, 3, 5, 7):
                    v.tensor_scalar(m.modc[:, i:i + 1], m.modc[:, i:i + 1], 1.0, None, ALU.add).then_inc(gates.sem, 1)
                v.wait_ge(rows_ready, 1)
                g2, s2 = gate[:].rearrange("p a d -> p (a d)"), sign[:].rearrange("p a d -> p (a d)")
                v.tensor_scalar(s2, m.bank[1][:], 0., 2., ALU.is_ge, ALU.mult).then_inc(gates.sem, 1)
                v.wait_ge(gates.sem, gates.next(5))
                v.tensor_scalar(s2, s2, -1., None, ALU.add).then_inc(gates.sem, 1)
                v.wait_ge(gates.sem, gates.next())
                v.tensor_tensor(g2, m.bank[1][:], s2, ALU.mult).then_inc(gates.sem, 1)
                v.wait_ge(gates.sem, gates.next())
                v.tensor_scalar(g2, g2, .25, None, ALU.max).then_inc(gates.sem, 1)
                v.wait_ge(gates.sem, gates.next())
                v.tensor_tensor(m.gates[:].rearrange("p a d -> p (a d)"), g2, s2, ALU.mult).then_inc(gates.sem, 1)
                v.wait_ge(gates.sem, gates.next())
                for l in range(2):
                    v.tensor_tensor(m.wo[l], m.wo[l], m.gates[:, 2 * l], ALU.mult).then_inc(weights_ready, 1)


def reciprocal_root(v, act_done, count, a, root, y, t):
    v.wait_ge(act_done[0], act_done[1])
    v.reciprocal(y, root).then_inc(count.sem, 1)
    v.wait_ge(count.sem, count.next())
    v.tensor_tensor(t, y, y, ALU.mult).then_inc(count.sem, 1)
    v.wait_ge(count.sem, count.next())
    v.tensor_tensor(t, t, a, ALU.mult).then_inc(count.sem, 1)
    v.wait_ge(count.sem, count.next())
    v.tensor_scalar(t, t, -.5, 1.5, ALU.mult, ALU.add).then_inc(count.sem, 1)
    v.wait_ge(count.sem, count.next())
    v.tensor_tensor(y, y, t, ALU.mult).then_inc(count.sem, 1)
    v.wait_ge(count.sem, count.next())


class LayerNorm:

    def __init__(self, nc, ctx, m, n):
        sb = lambda name, s: ctx.enter_context(nc.sbuf_tensor(f"{name}_ln{n}", s, F32))
        self.m, self.base = m, n * NC4
        self.st, self.mv = sb("st", [P, TILES, 6]), sb("mv", [P, TILES, 2])
        self.a, self.root, self.y, self.t = (sb(k, [P, TILES]) for k in "a root y t".split())
        self.chain, self.var_ready, self.root_done, self.xn_ready = m.ln_chain, m.sem("ln_var"), m.sem("ln_root"), m.sem("ln_xn")

    def stats(self, v, c):
        m, k = self.m, self.chain
        for b in range(c * TPC, (c + 1) * TPC):
            v.bn_stats(self.st[:, b], m.x[:, b]).then_inc(k.sem, 1)
        v.wait_ge(k.sem, k.next(TPC))
        for b in range(c * TPC, (c + 1) * TPC):
            v.bn_aggr(self.mv[:, b], self.st[:, b]).then_inc(k.sem, 1)
        v.wait_ge(k.sem, k.next(TPC))
        v.tensor_scalar(self.a[:, c * TPC:(c + 1) * TPC], self.mv[:, c * TPC:(c + 1) * TPC, 1], EPS, None, ALU.add).then_inc(self.var_ready, 1)
        v.wait_ge(self.var_ready, self.base + c + 1)

    def take_root(self, act, c):
        act.wait_ge(self.var_ready, self.base + c + 1)
        act.activation(self.root[:, c * TPC:(c + 1) * TPC], self.a[:, c * TPC:(c + 1) * TPC], ACT.Sqrt).then_inc(self.root_done, 1)

    def normalise(self, v, c):
        m, cs = self.m, slice(c * TPC, (c + 1) * TPC)
        reciprocal_root(v, (self.root_done, self.base + c + 1), self.chain, self.a[:, cs], self.root[:, cs], self.y[:, cs], self.t[:, cs])
        for b in range(c * TPC, (c + 1) * TPC):
            v.tensor_scalar(m.xn[:, b], m.x[:, b], self.mv[:, b, 0:1], self.y[:, b:b + 1], ALU.subtract, ALU.mult).then_inc(self.xn_ready, 1)

    def wait_chunk(self, pe, c):
        pe.wait_ge(self.xn_ready, TPC * (self.base + c + 1))


def project(nc, m, L, dram):
    with ExitStack() as ctx:
        sb = lambda name, s, d=F32: ctx.enter_context(nc.sbuf_tensor(f"{name}_pj{L}", s, d))
        hT = sb("hT", [P, T])
        qf, res = [sb(f"qf{i}", [P, CH]) for i in range(2)], [sb(f"res{i}", [P, CH]) for i in range(2)]
        parts = [[sb(f"part{i}{a}", [P, T], BF) for a in range(3)] for i in range(2)]
        ln = LayerNorm(nc, ctx, m, 2 * L)
        if L == 0:
            tmp = [sb(f"tmp{i}", [P, CH]) for i in range(2)]
            cen, sq, latn = (sb(k, [P, TILES, LAT]) for k in ("cen", "sq", "latn"))
            latT = sb("latT", [LAT, T])
            mean, a, root, y, t = (sb(k, [P, TILES]) for k in ("mean", "a", "root", "y", "t"))
            steps = [(i, c) for i in range(2) for c in range(NC4)]
        else:
            got = sb("got", [P, 2, TILES, D])
            steps = [(i, c) for c in range(NC4) for i in range(2)]
        names = "turned ht_ready lat_ready lat_var lat_root latn_ready latT_turned latT_ready v_ready v_out proj_ready proj_used qf_ready hi_done r_done mid_done lo_done stored".split()
        (turned, ht_ready, lat_ready, lat_var, lat_root, latn_ready, latT_turned, latT_ready, v_ready, v_out, proj_ready,
         proj_used, qf_ready, hi_done, r_done, mid_done, lo_done, stored) = (m.sem("pj_" + k) for k in names)
        chain = m.pj_chain
        bank = m.bank
        NS = len(steps)
        s8, s4 = NS * L, NC4 * L
        product = (lambda n: (bank[5], bank[7])[n % 2]) if L == 0 else (lambda n: bank[4 + n % 4])
        rotated = lambda n: (bank[6], bank[0])[n % 2]
        v_bank = lambda c: bank[1 + c] if L == 0 else bank[c]
        ident = m.consts[:, C_ID:C_ID + P]
        cols = lambda c: slice(c * CH, (c + 1) * CH)

        with nc.Block() as block:
            @block.sync
            def _(sp):
                if L == 0:
                    sp.wait_ge(m.sem("pool_set"), 8)
                    for p in range(2):
                        for j in range(GH):
                            sp.dma_start(m.KS[p][SHIFT0:SHIFT0 + 2 * GH, j, :], dram["zo"][j]).then_inc(m.sem("ones_in"), 16)
                    sp.wait_ge(m.sem("ones_in"), 16 * 2 * GH)
                for n, (i, c) in enumerate(steps):
                    if c % 2 == 0:
                        continue
                    sp.wait_ge(lo_done, s8 + n + 1)
                    half = (c - 1) * CH
                    for a3 in range(3):
                        dst = bass.AP(dram[f"{('q_parts', 'k_parts')[i]}{L}"].tensor, a3 * HD * T + half, [[3 * HD * T, H], [T, HD], [1, 2 * CH]])
                        sp.dma_start(dst, parts[i][a3][:, half:half + 2 * CH]).then_inc(stored, 16)
                sp.wait_ge(stored, 12 * 16 * (L + 1))

            @block.tensor
            def _(pe):
                def heads(n):
                    i, c = steps[n]
                    rhs = (latT if i and L == 0 else hT)[:, cols(c)]
                    if L == 0:
                        if n >= 2:
                            pe.wait_ge(proj_used, n - 1)
                        pe.matmul(rotated(n), (m.wqr, m.wukr)[i][:], rhs, start=True, stop=True)
                        mm = pe.matmul(product(n), (m.wq, m.wuk)[i], rhs, start=True, stop=True)
                    else:
                        if n >= 4:
                            pe.wait_ge(r_done, s8 + n - 3)
                        mm = pe.matmul(product(n), m.w1bd[:, i], rhs, start=True, stop=True)
                    mm.then_inc(proj_ready, 1)

                def values(c):
                    for t4 in range(TPC):
                        b = c * TPC + t4
                        mm = pe.matmul(v_bank(c)[:, t4 * P:(t4 + 1) * P], (latT if L == 0 else hT)[:, b * P:(b + 1) * P],
                                       m.wuv if L == 0 else m.w1bd[:, 2], start=True, stop=True)
                    mm.then_inc(v_ready, 1)

                for c in range(NC4):
                    ln.wait_chunk(pe, c)
                    for t4 in range(TPC):
                        mm = pe.transpose(bank[c][:, t4 * P:(t4 + 1) * P], m.xn[:, c * TPC + t4], ident)
                    mm.then_inc(turned, 1)
                    pe.wait_ge(ht_ready, s4 + c + 1)
                    if L == 0:
                        for b in range(c * TPC, (c + 1) * TPC):
                            mm = pe.matmul(bank[4][:, b * LAT:(b + 1) * LAT], hT[:, b * P:(b + 1) * P], m.wdkv, start=True, stop=True)
                        mm.then_inc(lat_ready, 1)
                        heads(c)
                    else:
                        heads(2 * c)
                        heads(2 * c + 1)
                        values(c)
                if L == 0:
                    pe.wait_ge(latn_ready, 1)
                    for c in range(NC4):
                        for t4 in range(TPC):
                            mm = pe.transpose(bank[1 + c][0:LAT, t4 * P:(t4 + 1) * P], latn[:, c * TPC + t4], ident)
                        mm.then_inc(latT_turned, 1)
                    for c in range(NC4):
                        pe.wait_ge(latT_ready, c + 1)
                        values(c)
                    for n in range(NC4, NS):
                        heads(n)

            @block.scalar
            def _(act):
                def hi(n):
                    i, c = steps[n]
                    if L == 0:
                        act.wait_ge(qf_ready, n + 1)
                    else:
                        act.wait_ge(proj_ready, s8 + n + 1)
                    act.copy(parts[i][0][:, cols(c)], qf[n % 2][:] if L == 0 else product(n)).then_inc(hi_done, 1)

                def mid(n):
                    i, c = steps[n]
                    act.wait_ge(r_done, s8 + n + 1)
                    act.copy(parts[i][1][:, cols(c)], res[n % 2][:]).then_inc(mid_done, 1)

                def split(n):
                    hi(n)
                    if n:
                        mid(n - 1)

                def v_rows(c):
                    act.wait_ge(v_ready, s4 + c + 1)
                    act.copy(m.vall[:, c * TPC:(c + 1) * TPC], v_bank(c).rearrange("p (b d) -> p b d", d=D)).then_inc(v_out, 1)

                ln.take_root(act, 0)
                for c in range(NC4):
                    if c + 1 < NC4:
                        ln.take_root(act, c + 1)
                    act.wait_ge(turned, s4 + c + 1)
                    act.activation(hT[:, cols(c)], bank[c], ACT.Identity, bias=m.modc[:, 4 * L:4 * L + 1],
                                   scale=m.modc[:, 4 * L + 1:4 * L + 2]).then_inc(ht_ready, 1)
                    if L == 0:
                        if c:
                            split(c - 1)
                    else:
                        split(2 * c)
                        split(2 * c + 1)
                        v_rows(c)
                if L == 0:
                    split(NC4 - 1)
                    act.wait_ge(lat_var, 1)
                    act.activation(root[:], a[:], ACT.Sqrt).then_inc(lat_root, 1)
                    for c in range(NC4):
                        act.wait_ge(latT_turned, c + 1)
                        act.activation(latT[:, cols(c)], bank[1 + c][0:LAT], ACT.Identity, bias=m.lngb[:, 1:2],
                                       scale=m.lngb[:, 0:1]).then_inc(latT_ready, 1)
                    for c in range(NC4):
                        v_rows(c)
                    for n in range(NC4, NS):
                        split(n)
                mid(NS - 1)

            @block.vector
            def _(v):
                def rope(n):
                    i, c = steps[n]
                    if n >= 2:
                        v.wait_ge(r_done, n - 1)
                    v.wait_ge(proj_ready, n + 1)
                    v.tensor_tensor(tmp[0][:], product(n), m.cosT[:, cols(c)], ALU.mult).then_inc(chain.sem, 1)
                    v.tensor_tensor(tmp[1][:], rotated(n), m.sinT[:, cols(c)], ALU.mult).then_inc(proj_used, 1)
                    v.wait_ge(chain.sem, chain.next())
                    v.wait_ge(proj_used, n + 1)
                    v.tensor_tensor(qf[n % 2][:], tmp[0][:], tmp[1][:], ALU.add).then_inc(qf_ready, 1)

                def residue(n):
                    i, c = steps[n]
                    if n >= 2:
                        v.wait_ge(lo_done, s8 + n - 1)
                    v.wait_ge(hi_done, s8 + n + 1)
                    v.tensor_tensor(res[n % 2][:], qf[n % 2][:] if L == 0 else product(n), parts[i][0][:, cols(c)], ALU.subtract).then_inc(r_done, 1)

                def step(n):
                    if L == 0:
                        rope(n)
                        if n:
                            residue(n - 1)
                    else:
                        residue(n)

                def chunk_in(c):
                    if L == 1:
                        add_rows(v, m, 0, c, got)
                    ln.stats(v, c)

                if L == 0:
                    v.wait_ge(m.sem("tables"), 32)
                chunk_in(0)
                if L == 0:
                    for c in range(NC4):
                        if c + 1 < NC4:
                            chunk_in(c + 1)
                        ln.normalise(v, c)
                        if c:
                            step(c - 1)
                    step(NC4 - 1)
                    lat = bank[4].rearrange("p (b l) -> p b l", l=LAT)
                    v.wait_ge(lat_ready, NC4)
                    v.tensor_reduce(mean[:], lat, AX.X, ALU.add).then_inc(chain.sem, 1)
                    v.wait_ge(chain.sem, chain.next())
                    v.tensor_scalar(mean[:], mean[:], 1 / LAT, None, ALU.mult).then_inc(chain.sem, 1)
                    v.wait_ge(chain.sem, chain.next())
                    v.tensor_tensor(cen[:], lat, mean[:].unsqueeze(2).to_broadcast([P, TILES, LAT]), ALU.subtract).then_inc(chain.sem, 1)
                    v.wait_ge(chain.sem, chain.next())
                    v.tensor_tensor(sq[:], cen[:], cen[:], ALU.mult).then_inc(chain.sem, 1)
                    v.wait_ge(chain.sem, chain.next())
                    v.tensor_reduce(a[:], sq[:], AX.X, ALU.add).then_inc(chain.sem, 1)
                    v.wait_ge(chain.sem, chain.next())
                    v.tensor_scalar(a[:], a[:], 1 / LAT, EPS, ALU.mult, ALU.add).then_inc(lat_var, 1)
                    v.wait_ge(lat_var, 1)
                    reciprocal_root(v, (lat_root, 1), chain, a[:], root[:], y[:], t[:])
                    v.tensor_tensor(latn[:], cen[:], y[:].unsqueeze(2).to_broadcast([P, TILES, LAT]), ALU.mult).then_inc(latn_ready, 1)
                    for n in range(NC4, NS):
                        step(n)
                    residue(NS - 1)
                else:
                    for c in range(NC4):
                        ln.normalise(v, c)
                        if c:
                            step(2 * c - 2)
                            step(2 * c - 1)
                        if c + 1 < NC4:
                            chunk_in(c + 1)
                    step(NS - 2)
                    step(NS - 1)

            @block.gpsimd
            def _(g):
                if L == 1:
                    gather_rows(g, m, 0, dram, got)
                else:
                    for z, rows in enumerate(m.QS + m.KS):
                        g.memset(rows[64:P].bitcast(F32), 0.).then_inc(m.sem("pool_set"), 1)
                        g.wait_ge(m.sem("pool_set"), 4 + z + 1)
                for n, (i, c) in enumerate(steps):
                    g.wait_ge(mid_done, s8 + n + 1)
                    g.tensor_tensor(parts[i][2][:, cols(c)], res[n % 2][:], parts[i][1][:, cols(c)], ALU.subtract).then_inc(lo_done, 1)


def gather_rows(g, m, L, dram, got):
    for c in range(NC4):
        for b in range(c * TPC, (c + 1) * TPC):
            for i in range(2):
                g.indirect_dma_start(out=got[:, i, b], out_offset=None, in_=dram[f"eo{L}"],
                                     in_offset=bass.IndirectOffsetOnAxis(ap=m.pos[:, i, b:b + 1], axis=0)).then_inc(m.sem(f"cb_gathered{c}"), 16)


def add_rows(v, m, L, c, got):
    added = m.sem("cb_added")
    v.wait_ge(m.sem(f"cb_gathered{c}"), 128 * (L + 1))
    for i in range(2):
        for b in range(c * TPC, (c + 1) * TPC):
            v.scalar_tensor_tensor(m.x[:, b], got[:, i, b], m.wt[:, i, b:b + 1], m.x[:, b], ALU.mult, ALU.add).then_inc(added, 1)
        v.wait_ge(added, (L * NC4 + c) * 2 * TPC + (i + 1) * TPC)


def attention(nc, m, L, dram, weight_loads):
    with ExitStack() as ctx:
        sb = lambda name, s, d=F32: ctx.enter_context(nc.sbuf_tensor(f"{name}_at{L}", s, d))
        QS, KS = m.QS, m.KS
        VS = m.VS
        probs = sb("probs", [P, 2, GH, CH])
        avs = sb("avs", [P, 2, CH])
        mxp = sb("mxp", [P, 4, GH * TPC, NC4])
        mx = sb("mx", [P, 4, GH * TPC])
        nsh = sb("nsh", [P, 4, TPC, 2 * GH], BF)
        shrow = sb("shrow", [2 * GH, 4, CH], BF)
        junk = sb("junk", [P, MXBUF, CH])
        st, mxb, avb = m.st, m.mxb, m.avb
        s_ = m.sem
        q_d, k_d = dram[f"q_parts{L}"], dram[f"k_parts{L}"]
        weights_in = s_("weights_in")
        kq_loaded = [s_(f"kq_loaded{p}") for p in range(2)]
        v_copied = [s_(f"v_copied{p}") for p in range(2)]
        st_ready = [s_(f"st_ready{i}") for i in range(2)]
        exp_done = [s_(f"exp_done{i}") for i in range(2)]
        shift_set = [s_(f"shift_set{u}") for u in range(4)]
        (av_done, av_free, max_final, hi_split, mx_ready, mx_free, shift_split, shift_row) = (s_(n) for n in (
            "av_done", "av_free", "max_final", "hi_split", "mx_ready", "mx_free", "shift_split", "shift_row"))
        RB, SB, UB = L * NROT, L * NST, L * NU
        GB = L * NG // 2

        with nc.Block() as block:
            @block.sync
            def _(sp):
                def load_group(g):
                    p = g % 2
                    sp.dma_start(QS[p][SHIFT0:SHIFT0 + 2 * GH], bass.AP(dram["zrow"].tensor, 0, [[T, 2 * GH], [0, GH], [1, T]])).then_inc(kq_loaded[p], 16)
                    for j in range(GH):
                        base = (g * GH + j) * 3 * HD * T
                        for a in range(3):
                            sp.dma_start(QS[p][24 * a:24 * a + 24, j, :],
                                         bass.AP(q_d.tensor, base + a * HD * T, [[0, 3], [T, HD], [1, T]])).then_inc(kq_loaded[p], 16)
                        sp.dma_start(KS[p][0:72, j, :], bass.AP(k_d.tensor, base, [[0, 3], [T, 3 * HD], [1, T]])).then_inc(kq_loaded[p], 16)

                load_group(0)
                loads = list(weight_loads)
                for item in ORDER:
                    if item[0] == "rot" and ROT[item[1]][0] == "turn":
                        u = ROT[item[1]][1]
                        g, Q = UNITS[u]
                        sp.wait_ge(shift_row, UB + u + 1)
                        sp.dma_start(QS[g % 2][SHIFT0:SHIFT0 + 2 * GH, :, Q * CH:(Q + 1) * CH],
                                     shrow[:, u % 4, :].unsqueeze(1).to_broadcast([2 * GH, GH, CH])).then_inc(shift_set[u % 4], 16)
                        if u == 0:
                            load_group(1)
                        elif u > 1:
                            for dst, src in loads[:2]:
                                sp.dma_start(dst, src).then_inc(weights_in, 16)
                            del loads[:2]
                    if item[0] == "av" and item[1] in LAST[:NG - 2]:
                        sp.wait_ge(av_done, 2 + SB + item[1] + 1)
                        load_group(LAST.index(item[1]) + 2)
                sp.wait_ge(weights_in, 16 * m.weights_total)

            @block.gpsimd
            def _(g):
                for gg in range(NG):
                    p, i = gg % 2, gg // 2
                    if i:
                        g.wait_ge(av_done, 2 + SB + LAST[gg - 2] + 1)
                    g.tensor_copy(VS[p][:, :, :, 0:HD], m.vall[:, :, gg * GH * HD:(gg + 1) * GH * HD].rearrange(
                        "p b (h d) -> p b h d", d=HD)).then_inc(v_copied[p], 1)
                    g.wait_ge(v_copied[p], GB + i + 1)

            @block.tensor
            def _(pe):
                if L == 0:
                    pe.sem_inc(av_done, 2)

                def rotate(k):
                    kind, x = ROT[k]
                    buf = mxb[k % MXBUF]
                    pe.wait_ge(mx_free, RB + k + 1)
                    if kind == "max":
                        gg, Q, j, qb, c = x
                        p, w = gg % 2, max_width(x)
                        if (qb, j, c) == (0, 0, 0) and UNITS.index((gg, Q)) == FIRST_UNIT[gg]:
                            pe.wait_ge(kq_loaded[p], (GB + gg // 2 + 1) * 16 * (4 * GH + 1))
                        pe.matmul(buf[:, 0:w], QS[p][:, j, (4 * Q + qb) * P:(4 * Q + qb + 1) * P],
                                  KS[p][:, j, c * CH:c * CH + w], start=True, stop=True).then_inc(mx_ready, 1)
                    elif kind == "turn":
                        pe.wait_ge(shift_split, UB + x + 1)
                        for qb in range(TPC):
                            mm = pe.transpose(buf[:].bitcast(BF)[0:2 * GH, qb * P:(qb + 1) * P], nsh[:, x % 4, qb, :], m.identb[:])
                        mm.then_inc(mx_ready, 1)
                    else:
                        pe.wait_ge(av_free, UB + x + 1)
                        for qb in range(TPC):
                            mm = pe.transpose(buf[:, qb * P:(qb + 1) * P], avs[:, x % 2, qb * P:(qb + 1) * P], m.consts[:, C_ID:C_ID + P])
                        mm.then_inc(mx_ready, 1)

                def scores(s, half):
                    gg, Q, kb = STEPS[s]
                    p, off, diag = gg % 2, step_off(s), kb >= TPC * Q
                    if s:
                        pe.wait_ge(exp_done[half], SB + s)
                    for y in range(2):
                        j = 2 * half + y
                        mm = pe.matmul(st[half][:, y, off:CH], KS[p][:, j, kb * P:(kb + 1) * P], QS[p][:, j, Q * CH + off:(Q + 1) * CH],
                                       start=True, stop=True, skip_group_check=diag)
                        if diag:
                            mm = pe.matmul(st[half][:, y, off:off + P], m.identb[:], m.maskTb[:], start=False, stop=True, skip_group_check=True)
                    mm.then_inc(st_ready[half], 1)

                def values(s):
                    gg, Q, kb = STEPS[s]
                    u, p, off = UNIT[s], gg % 2, step_off(s)
                    if kb == 0:
                        pe.wait_ge(v_copied[p], GB + gg // 2 + 1)
                        if u:
                            pe.wait_ge(av_free, UB + u)
                    for half in range(2):
                        pe.wait_ge(exp_done[half], SB + s + 1)
                    for j in range(GH):
                        mm = pe.matmul(avb[32 * j:32 * j + 32, off:CH], VS[p][:, kb, j, :], probs[:, s % 2, j, off:CH],
                                       start=kb == 0, stop=kb == TPC * Q + 3, tile_position=(0, 32 * j), skip_group_check=True)
                    mm.then_inc(av_done, 1)

                for item in ORDER:
                    if item[0] == "rot":
                        rotate(item[1])
                    elif item[0] == "av":
                        values(item[1])
                    else:
                        _, s, half = item
                        if STEPS[s][2] == 0 and half == 0:
                            u = UNIT[s]
                            pe.wait_ge(shift_set[u % 4], 16 * (L * (NU // 4) + u // 4 + 1))
                        scores(s, half)

            @block.scalar
            def _(act):
                def evacuate(u):
                    act.wait_ge(av_done, 2 + SB + FIRST[u + 1])
                    if u >= 2:
                        act.wait_ge(mx_ready, RB + NORM_AT[u - 2] + 1)
                    act.copy(avs[:, u % 2, :], avb[:]).then_inc(av_free, 1)

                for s, (g, Q, kb) in enumerate(STEPS):
                    off = step_off(s)
                    act.wait_ge(av_done, SB + s + 1)
                    for half in range(2):
                        act.wait_ge(st_ready[half], SB + s + 1)
                        act.activation(probs[:, s % 2, 2 * half:2 * half + 2, off:CH], st[half][:, :, off:CH], ACT.Exp,
                                       scale=SCALE).then_inc(exp_done[half], 1)
                    if kb == 0 and s:
                        evacuate(UNIT[s] - 1)
                evacuate(NU - 1)

            @block.vector
            def _(v):
                if L == 0:
                    v.sem_inc(mx_free, MXBUF)
                for k, (kind, x) in enumerate(ROT):
                    buf = mxb[k % MXBUF]
                    v.wait_ge(mx_ready, RB + k + 1)
                    if kind == "max":
                        g, Q, j, qb, c = x
                        u, w = UNITS.index((g, Q)), max_width(x)
                        dst = mxp[:, u % 4, qb * GH + j, c:c + 1]
                        if c < Q:
                            ins = v.tensor_reduce(dst, buf[:, 0:w], AX.X, ALU.max)
                        else:
                            ins = v.tensor_tensor_reduce(junk[:, k % MXBUF, 0:w], buf[:, 0:w], m.maskN[:, CH - w:], 1.0, -3e38,
                                                         ALU.add, ALU.max, dst)
                        ins.then_inc(mx_free, 1)
                        if (j, qb, c) == (GH - 1, TPC - 1, Q):
                            v.wait_ge(mx_free, RB + k + 1 + MXBUF)
                            v.tensor_reduce(mx[:, u % 4, :], mxp[:, u % 4, :, 0:Q + 1], AX.X, ALU.max, negate=True).then_inc(max_final, 1)
                            v.wait_ge(max_final, UB + u + 1)
                            ns = nsh[:, u % 4].rearrange("p q (j s) -> p (q j) s", s=2)
                            v.tensor_copy(ns[:, :, 0], mx[:, u % 4, :]).then_inc(hi_split, 1)
                            v.wait_ge(hi_split, UB + u + 1)
                            v.tensor_tensor(ns[:, :, 1], mx[:, u % 4, :], ns[:, :, 0], ALU.subtract).then_inc(shift_split, 1)
                    elif kind == "turn":
                        if x >= 4:
                            v.wait_ge(shift_set[x % 4], 16 * (L * (NU // 4) + x // 4))
                        v.tensor_copy(shrow[:, x % 4, :], buf[:].bitcast(BF)[0:2 * GH, 0:CH]).then_inc(shift_row, 1)
                        v.wait_ge(shift_row, UB + x + 1)
                        v.sem_inc(mx_free, 1)
                    else:
                        g, Q = UNITS[x]
                        v.tensor_copy(m.araw[:, TPC * Q:TPC * Q + TPC, GH * g:GH * g + GH, :],
                                      buf[:].rearrange("p (q j c) -> p q j c", j=GH, c=32)[:, :, :, 0:HD + 1]).then_inc(mx_free, 1)


def route(nc, m, L, dram):
    with ExitStack() as ctx:
        sb = lambda name, s, d=F32: ctx.enter_context(nc.sbuf_tensor(f"{name}_rt{L}", s, d))
        hT = m.hT
        S3 = [P, TILES, E8]
        val, eq, cand, sel2, oh1, oh2, both = (sb(k, S3) for k in "val eq cand sel2 oh1 oh2 both".split())
        m1, m2, ix, sm, dif, ex, pf = (sb(k, [P, TILES]) for k in "m1 m2 ix sm dif ex pf".split())
        tot, run = sb("tot", [P, E8, TILES]), sb("run", [P, E8, TILES])
        rank = sb("rank", S3)
        npad, cmp, endt, texp = sb("npad", [P, E8]), sb("cmp", [P, E8, TILES]), sb("endt", [P, E8]), sb("texp", [P, 40])
        zero8, ones = sb("zero8", [P, P]), sb("ones", [P, P])
        rec, att, attT = sb("rec", [P, TILES, H]), sb("att", [P, TILES, D]), sb("attT", [P, T])
        ln = LayerNorm(nc, ctx, m, 2 * L + 1)
        inv_done, att_ready, att_turned, attT_ready, o_ready, x_done = (m.sem("op_" + n) for n in "inv att turned attT o x".split())
        grid = sb("grid", [P, 40, E8])
        turned, ht_ready, logits_ready, counted = (m.sem("rt_" + n) for n in "turned ht logits counted".split())
        both_ready, exp_in, exp_out, pos_ready = (m.sem("rt_" + n) for n in "both exp_in exp_out pos".split())
        k = m.rt_chain
        s4 = L * NC4
        C = m.consts
        iota = C[:, C_I8:C_I8 + E8].unsqueeze(1).to_broadcast(S3)
        bc = lambda a: a.unsqueeze(2).to_broadcast(S3)
        f2 = lambda a: a.rearrange("p b e -> p (b e)")
        with nc.Block() as block:
            @block.tensor
            def _(pe):
                def project_out(c):
                    pe.wait_ge(attT_ready, s4 + c + 1)
                    for t4 in range(TPC):
                        b = c * TPC + t4
                        mm = pe.matmul(m.bank[4 + c][:, t4 * P:(t4 + 1) * P], attT[:, b * P:(b + 1) * P], m.wo[L], start=True, stop=True)
                    mm.then_inc(o_ready, 1)

                for c in range(NC4):
                    pe.wait_ge(att_ready, TPC * (s4 + c + 1))
                    for t4 in range(TPC):
                        mm = pe.transpose(m.bank[c][:, t4 * P:(t4 + 1) * P], att[:, c * TPC + t4], C[:, C_ID:C_ID + P])
                    mm.then_inc(att_turned, 1)
                    if c:
                        project_out(c - 1)
                project_out(NC4 - 1)
                for c in range(NC4):
                    ln.wait_chunk(pe, c)
                    for t4 in range(TPC):
                        mm = pe.transpose(m.bank[c][:, t4 * P:(t4 + 1) * P], m.xn[:, c * TPC + t4], C[:, C_ID:C_ID + P])
                    mm.then_inc(turned, 1)
                    pe.wait_ge(ht_ready, s4 + c + 1)
                    for b in range(c * TPC, (c + 1) * TPC):
                        mm = pe.matmul(m.bank[4][:, b * E8:(b + 1) * E8], hT[:, b * P:(b + 1) * P], m.wr[L], start=True, stop=True)
                mm.then_inc(logits_ready, 1)
                pe.wait_ge(both_ready, 2 * L + 2)
                pe.matmul(m.bank[5][:, 0:P], C[:, C_UP:C_UP + P], f2(both[:]), start=True, stop=True)
                pe.matmul(m.bank[6][:, 0:P], ones[:], f2(both[:]), start=True, stop=True).then_inc(counted, 1)

            @block.scalar
            def _(act):
                for c in range(NC4):
                    act.wait_ge(att_turned, s4 + c + 1)
                    act.copy(attT[:, c * CH:(c + 1) * CH], m.bank[c]).then_inc(attT_ready, 1)
                ln.take_root(act, 0)
                for c in range(NC4):
                    if c + 1 < NC4:
                        ln.take_root(act, c + 1)
                    act.wait_ge(turned, s4 + c + 1)
                    act.activation(hT[:, c * CH:(c + 1) * CH], m.bank[c][:], ACT.Identity, bias=m.modc[:, 4 * L + 2:4 * L + 3],
                                   scale=m.modc[:, 4 * L + 3:4 * L + 4]).then_inc(ht_ready, 1)
                act.wait_ge(exp_in, L + 1)
                if L == 0:
                    act.activation(ex[:], dif[:], ACT.Exp).then_inc(exp_out, 1)
                else:
                    act.activation(f2(val[:]), f2(val[:]), ACT.Exp).then_inc(exp_out, 1)

            @block.vector
            def _(v):
                def chunk_in(c):
                    v.wait_ge(o_ready, s4 + c + 1)
                    xs = m.x[:, c * TPC:(c + 1) * TPC].rearrange("p b d -> p (b d)")
                    v.tensor_tensor(xs, xs, m.bank[4 + c], ALU.add).then_inc(x_done, 1)
                    v.wait_ge(x_done, s4 + c + 1)
                    ln.stats(v, c)

                v.reciprocal(rec[:], m.araw[:, :, :, HD]).then_inc(inv_done, 1)
                v.wait_ge(inv_done, L + 1)
                for b in range(TILES):
                    v.tensor_tensor(att[:, b].rearrange("p (h d) -> p h d", d=HD), m.araw[:, b, :, 0:HD],
                                    rec[:, b].unsqueeze(2).to_broadcast([P, H, HD]), ALU.mult).then_inc(att_ready, 1)
                chunk_in(0)
                for c in range(NC4):
                    if c + 1 < NC4:
                        chunk_in(c + 1)
                    ln.normalise(v, c)
                v.memset(ones[:], 1.).then_inc(both_ready, 1)
                v.memset(zero8[:], 0.).then_inc(k.sem, 1)
                v.wait_ge(logits_ready, L + 1)
                v.tensor_copy(f2(val[:]), m.bank[4][:, 0:P]).then_inc(k.sem, 1)
                v.wait_ge(k.sem, k.next(2))
                if L == 1:
                    v.tensor_reduce(m1[:], val[:], AX.X, ALU.max).then_inc(k.sem, 1)
                    v.wait_ge(k.sem, k.next())
                    v.tensor_tensor(val[:], val[:], bc(m1[:]), ALU.subtract).then_inc(exp_in, 2 - L)
                    v.wait_ge(exp_out, L + 1)
                    v.tensor_reduce(sm[:], val[:], AX.X, ALU.add).then_inc(k.sem, 1)
                    v.wait_ge(k.sem, k.next())
                    v.reciprocal(sm[:], sm[:]).then_inc(k.sem, 1)
                    v.wait_ge(k.sem, k.next())
                    v.tensor_tensor(val[:], val[:], bc(sm[:]), ALU.mult).then_inc(k.sem, 1)
                    v.wait_ge(k.sem, k.next())

                for src, top, oh in ((val, m1, oh1), (sel2, m2, oh2)):
                    v.tensor_reduce(top[:], src[:], AX.X, ALU.max).then_inc(k.sem, 1)
                    v.wait_ge(k.sem, k.next())
                    v.tensor_tensor(eq[:], src[:], bc(top[:]), ALU.is_ge).then_inc(k.sem, 1)
                    v.wait_ge(k.sem, k.next())
                    v.tensor_tensor(cand[:], eq[:], iota, ALU.mult).then_inc(k.sem, 1)
                    v.wait_ge(k.sem, k.next())
                    v.tensor_reduce(ix[:], cand[:], AX.X, ALU.min).then_inc(k.sem, 1)
                    v.wait_ge(k.sem, k.next())
                    v.tensor_tensor(oh[:], iota, bc(ix[:]), ALU.is_equal).then_inc(k.sem, 1)
                    v.wait_ge(k.sem, k.next())
                    if src is val:
                        v.scalar_tensor_tensor(f2(sel2[:]), f2(oh1[:]), NEG, f2(val[:]), ALU.mult, ALU.add).then_inc(k.sem, 1)
                        v.wait_ge(k.sem, k.next())
                v.tensor_tensor(both[:], oh1[:], oh2[:], ALU.add).then_inc(both_ready, 1)
                if L == 0:
                    v.tensor_tensor(dif[:], m2[:], m1[:], ALU.subtract).then_inc(exp_in, 1)
                    v.wait_ge(exp_out, 1)
                    v.tensor_scalar(sm[:], ex[:], 1., None, ALU.add).then_inc(k.sem, 1)
                    v.wait_ge(k.sem, k.next())
                    v.reciprocal(m.wt[:, 0], sm[:]).then_inc(k.sem, 1)
                    v.wait_ge(k.sem, k.next())
                    v.tensor_tensor(m.wt[:, 1], ex[:], m.wt[:, 0], ALU.mult).then_inc(k.sem, 1)
                else:
                    v.tensor_tensor(sm[:], m1[:], m2[:], ALU.add).then_inc(k.sem, 1)
                    v.wait_ge(k.sem, k.next())
                    v.tensor_scalar(sm[:], sm[:], 1e-20, None, ALU.add).then_inc(k.sem, 1)
                    v.wait_ge(k.sem, k.next())
                    v.reciprocal(sm[:], sm[:]).then_inc(k.sem, 1)
                    v.wait_ge(k.sem, k.next())
                    v.tensor_tensor(m.wt[:, 0], m1[:], sm[:], ALU.mult).then_inc(k.sem, 1)
                    v.wait_ge(k.sem, k.next())
                    v.tensor_tensor(m.wt[:, 1], m2[:], sm[:], ALU.mult).then_inc(k.sem, 1)
                v.wait_ge(k.sem, k.next())
                v.wait_ge(counted, L + 1)
                v.tensor_copy(tot[:], m.bank[6][:, 0:P].rearrange("p (b e) -> p e b", e=E8)).then_inc(k.sem, 1)
                v.wait_ge(k.sem, k.next())
                v.tensor_tensor_scan(f2(run[:]), f2(tot[:]), zero8[:], 0., ALU.add, ALU.add).then_inc(k.sem, 1)
                v.wait_ge(k.sem, k.next())
                if L == 1:
                    v.tensor_reduce(npad[:], tot[:], AX.X, ALU.add).then_inc(k.sem, 1)
                    v.wait_ge(k.sem, k.next())
                    v.tensor_tensor(cmp[:], npad[:].unsqueeze(2).to_broadcast([P, E8, TILES]),
                                    C[:, C_TH:C_TH + TILES].unsqueeze(1).to_broadcast([P, E8, TILES]), ALU.is_gt).then_inc(k.sem, 1)
                    v.wait_ge(k.sem, k.next())
                    v.tensor_reduce(endt[:], cmp[:], AX.X, ALU.add).then_inc(k.sem, 1)
                    v.wait_ge(k.sem, k.next())
                    v.tensor_tensor_scan(texp[:, 0:E8], endt[:], zero8[:, 0:E8], 0., ALU.add, ALU.add).then_inc(k.sem, 1)
                    v.wait_ge(k.sem, k.next())
                    v.tensor_tensor(npad[:], texp[:, 0:E8], endt[:], ALU.subtract).then_inc(k.sem, 1)
                    v.tensor_tensor(grid[:], C[:, C_IT:C_IT + 40].unsqueeze(2).to_broadcast([P, 40, E8]),
                                    texp[:, 0:E8].unsqueeze(1).to_broadcast([P, 40, E8]), ALU.is_ge).then_inc(k.sem, 1)
                    v.wait_ge(k.sem, k.next(2))
                    v.tensor_scalar(npad[:], npad[:], float(P), None, ALU.mult).then_inc(k.sem, 1)
                    v.tensor_reduce(texp[:], grid[:], AX.X, ALU.add).then_inc(k.sem, 1)
                    v.wait_ge(k.sem, k.next(2))
                    v.tensor_scalar(m.tile_expert[:], texp[:], float(E8 - 1), None, ALU.min).then_inc(k.sem, 1)
                    v.tensor_tensor(endt[:], run[:, :, 0], tot[:, :, 0], ALU.subtract).then_inc(k.sem, 1)
                    v.wait_ge(k.sem, k.next(2))
                    v.tensor_tensor(npad[:], npad[:], endt[:], ALU.subtract).then_inc(k.sem, 1)
                    v.wait_ge(k.sem, k.next())
                    v.tensor_tensor(run[:], run[:], npad[:].unsqueeze(2).to_broadcast([P, E8, TILES]), ALU.add).then_inc(k.sem, 1)
                    v.wait_ge(k.sem, k.next())
                v.tensor_tensor(run[:], run[:], tot[:], ALU.subtract).then_inc(k.sem, 1)
                v.wait_ge(k.sem, k.next())
                v.tensor_tensor(rank[:], run[:].rearrange("p e b -> p b e"), m.bank[5][:, 0:P].rearrange("p (b e) -> p b e", e=E8),
                                ALU.add).then_inc(k.sem, 1)
                v.wait_ge(k.sem, k.next())
                for i, oh in enumerate((oh1, oh2)):
                    v.tensor_tensor(cand[:], oh[:], rank[:], ALU.mult).then_inc(k.sem, 1)
                    v.wait_ge(k.sem, k.next())
                    v.tensor_reduce(pf[:], cand[:], AX.X, ALU.add).then_inc(k.sem, 1)
                    v.wait_ge(k.sem, k.next())
                    v.tensor_copy(m.pos[:, i], pf[:]).then_inc(pos_ready, 1)
                    v.wait_ge(pos_ready, 2 * L + i + 1)

            if L == 0:
                @block.gpsimd
                def _(g):
                    scatter_rows(g, m, L, dram)


def scatter_rows(g, m, L, dram):
    pos_ready, scattered = m.sem("rt_pos"), m.sem("rt_scattered")
    for i in range(2):
        g.wait_ge(pos_ready, 2 * L + i + 1)
        for b in range(TILES):
            g.indirect_dma_start(out=dram[f"perm{L}"], out_offset=bass.IndirectOffsetOnAxis(ap=m.pos[:, i, b:b + 1], axis=0),
                                 in_=m.xn[:, b], in_offset=None).then_inc(scattered, 16)
    g.wait_ge(scattered, (L + 1) * 32 * 16)


def experts0(nc, m, dram, w1, w2):
    with ExitStack() as ctx:
        sb = lambda name, s, d=F32: ctx.enter_context(nc.sbuf_tensor(f"{name}_f0", s, d))
        rows = [sb(f"rows{i}", [P, TPC, D]) for i in range(3)]
        hT = [sb(f"hTf{i}", [P, CH]) for i in range(2)]
        hid = [sb(f"hid{i}", [P, TPC, CH]) for i in range(2)]
        eo = [sb(f"eo{i}", [P, TPC, D]) for i in range(2)]
        loaded, stored = [m.sem(f"f0_loaded{i}") for i in range(3)], [m.sem(f"f0_stored{i}") for i in range(2)]
        turned, ht_ready, up_ready, hid_ready, down_ready, eo_ready = (m.sem("f0_" + n) for n in "turned ht up hid down eo".split())
        FB = FF0 // P
        bank = m.bank
        view = lambda t, e: t.rearrange("(b p) d -> p b d", p=P)[:, e * TPC:(e + 1) * TPC]
        with nc.Block() as block:
            @block.sync
            def _(sp):
                for e in range(E8 + 2):
                    if e < E8:
                        if e >= 3:
                            sp.wait_ge(turned, e - 2)
                        sp.dma_start(rows[e % 3][:], view(dram["perm0"], e)).then_inc(loaded[e % 3], 16)
                    if e >= 2:
                        sp.wait_ge(eo_ready, e - 1)
                        sp.dma_start(view(dram["eo0"], e - 2), eo[e % 2][:]).then_inc(stored[e % 2], 16)
                for i in range(2):
                    sp.wait_ge(stored[i], 16 * E8 // 2)

            @block.tensor
            def _(pe):
                def turn(e):
                    pe.wait_ge(loaded[e % 3], 16 * (e // 3 + 1))
                    for t4 in range(TPC):
                        mm = pe.transpose(bank[e % 2][:, t4 * P:(t4 + 1) * P], rows[e % 3][:, t4], m.consts[:, C_ID:C_ID + P])
                    mm.then_inc(turned, 1)

                turn(0)
                for e in range(E8):
                    pe.wait_ge(ht_ready, e + 1)
                    for f in range(FB):
                        if e:
                            pe.wait_ge(hid_ready, (e - 1) * FB + f + 1)
                        pe.matmul(bank[2 + f][:], w1[:, e, f * P:(f + 1) * P], hT[e % 2][:], start=True, stop=True).then_inc(up_ready, 1)
                    if e + 1 < E8:
                        turn(e + 1)
                    if e >= 2:
                        pe.wait_ge(eo_ready, e - 1)
                    for t4 in range(TPC):
                        for f in range(FB):
                            if t4 == 0:
                                pe.wait_ge(hid_ready, e * FB + f + 1)
                            mm = pe.matmul(bank[6 + e % 2][:, t4 * P:(t4 + 1) * P], hid[e % 2][:, f, t4 * P:(t4 + 1) * P], w2[:, e * FB + f],
                                           start=f == 0, stop=f == FB - 1)
                    mm.then_inc(down_ready, 1)

            @block.scalar
            def _(act):
                def modulate(e):
                    act.wait_ge(turned, e + 1)
                    act.activation(hT[e % 2][:], bank[e % 2][:], ACT.Identity, bias=m.modc[:, 2:3], scale=m.modc[:, 3:4]).then_inc(ht_ready, 1)

                modulate(0)
                for e in range(E8):
                    for f in range(FB):
                        if e >= 2 and f == 0:
                            act.wait_ge(down_ready, e - 1)
                        act.wait_ge(up_ready, e * FB + f + 1)
                        act.activation(hid[e % 2][:, f], bank[2 + f][:], ACT.Gelu).then_inc(hid_ready, 1)
                    if e + 1 < E8:
                        modulate(e + 1)

            @block.vector
            def _(v):
                for e in range(E8):
                    if e >= 2:
                        v.wait_ge(stored[e % 2], 16 * (e // 2))
                    v.wait_ge(down_ready, e + 1)
                    v.tensor_tensor(eo[e % 2][:], bank[6 + e % 2][:].rearrange("p (b d) -> p b d", d=D),
                                    m.gates[:, 1:2, :].to_broadcast([P, TPC, D]), ALU.mult).then_inc(eo_ready, 1)


BLOCKS1 = [(0, P), (P, P), (2 * P, FF1 - 2 * P)]


def shared_expert(nc, m, dram, gw, uw, dw):
    with ExitStack() as ctx:
        sb = lambda name, s, d=F32: ctx.enter_context(nc.sbuf_tensor(f"{name}_sh", s, d))
        sg = [sb(f"sg{i}", [P, CH]) for i in range(2)]
        hid = [sb(f"hid{i}", [P, 3, CH]) for i in range(2)]
        tmp = [sb(f"tmp{i}", [P, TPC, D]) for i in range(2)]
        gu_ready, silu_done, hid_ready, down_ready, tmp_ready, x_done = (m.sem("sh_" + n) for n in "gu silu hid down tmp x".split())
        bank, S = m.bank, E8
        with nc.Block() as block:
            @block.gpsimd
            def _(g):
                scatter_rows(g, m, 1, dram)

            @block.tensor
            def _(pe):
                def down(c):
                    if c >= 2:
                        pe.wait_ge(tmp_ready, c - 1)
                    pe.wait_ge(hid_ready, 3 * c + 3)
                    for t4 in range(TPC):
                        for f, (o, w) in enumerate(BLOCKS1):
                            mm = pe.matmul(bank[4 + c % 2][:, t4 * P:(t4 + 1) * P], hid[c % 2][0:w, f, t4 * P:(t4 + 1) * P],
                                           dw[0:w, S, f], start=f == 0, stop=f == 2)
                    mm.then_inc(down_ready, 1)

                for c in range(NC4):
                    for f, (o, w) in enumerate(BLOCKS1):
                        n = 3 * c + f
                        if n >= 2:
                            pe.wait_ge(hid_ready, n - 1)
                        for z, wt in enumerate((gw, uw)):
                            mm = pe.matmul(bank[2 * (n % 2) + z][0:w], wt[:, S, o:o + w], m.hT[:, c * CH:(c + 1) * CH], start=True, stop=True)
                        mm.then_inc(gu_ready, 1)
                    if c:
                        down(c - 1)
                down(NC4 - 1)

            @block.scalar
            def _(act):
                for n in range(3 * NC4):
                    w = BLOCKS1[n % 3][1]
                    if n >= 2:
                        act.wait_ge(hid_ready, n - 1)
                    act.wait_ge(gu_ready, n + 1)
                    act.activation(sg[n % 2][0:w], bank[2 * (n % 2)][0:w], ACT.Silu).then_inc(silu_done, 1)

            @block.vector
            def _(v):
                def finish(c):
                    v.wait_ge(down_ready, c + 1)
                    v.tensor_tensor(tmp[c % 2][:], bank[4 + c % 2][:].rearrange("p (b d) -> p b d", d=D),
                                    m.gates[:, 3:4, :].to_broadcast([P, TPC, D]), ALU.mult).then_inc(tmp_ready, 1)
                    v.wait_ge(tmp_ready, c + 1)
                    xs = m.x[:, c * TPC:(c + 1) * TPC]
                    v.tensor_tensor(xs, xs, tmp[c % 2][:], ALU.add).then_inc(x_done, 1)
                    v.wait_ge(x_done, c + 1)

                for n in range(3 * NC4):
                    c, f = divmod(n, 3)
                    w = BLOCKS1[f][1]
                    if c >= 2 and f == 0:
                        v.wait_ge(down_ready, c - 1)
                    v.wait_ge(silu_done, n + 1)
                    v.tensor_tensor(hid[c % 2][0:w, f], bank[2 * (n % 2) + 1][0:w], sg[n % 2][0:w], ALU.mult).then_inc(hid_ready, 1)
                    if f == 2 and c:
                        finish(c - 1)
                finish(NC4 - 1)


def experts1(nc, m, dram, gw, uw, dw):
    with ExitStack() as ctx:
        sb = lambda name, s, d=F32: ctx.enter_context(nc.sbuf_tensor(f"{name}_f1", s, d))
        rows = [sb(f"rows{i}", [P, D]) for i in range(4)]
        hT = [sb(f"hTt{i}", [P, P]) for i in range(2)]
        sg = [sb(f"sg{i}", [P, FF1]) for i in range(2)]
        hid = [sb(f"hid{i}", [P, FF1]) for i in range(2)]
        hidT = [sb(f"hidT{i}", [P, 3, P]) for i in range(2)]
        eo = [sb(f"eo{i}", [P, D]) for i in range(4)]
        loaded, stored = [m.sem(f"f1_loaded{i}") for i in range(4)], [m.sem(f"f1_stored{i}") for i in range(4)]
        (turned, ht_ready, gu_ready, silu_done, hid_ready, hid_turned, hidT_ready, down_ready, eo_ready) = (
            m.sem("f1_" + n) for n in "turned ht gu silu hid hid_turned hidT down eo".split())
        G, U, X, O = m.bank[0:2], m.bank[2:4], m.bank[4:6], m.bank[6:8]
        N, ident = RTILES1, m.consts[:, C_ID:C_ID + P]
        with nc.Block() as block:
            @block.sync
            def _(sp):
                def load(n, z, q):
                    sp.dma_start(rows[z][:], dram["perm1"][bass.ds(n * P, P)]).then_inc(loaded[z], 16)

                def store(n, z):
                    sp.wait_ge(eo_ready, n + 1)
                    sp.dma_start(dram["eo1"][bass.ds(n * P, P)], eo[z][:]).then_inc(stored[z], 16)

                for n in range(4):
                    load(n, n, 0)
                for n in range(4):
                    sp.wait_ge(turned, n + 1)
                    load(n + 4, n, 1)
                    if n >= 2:
                        store(n - 2, n - 2)
                with sp.Fori(1, N // 4 - 1) as i:
                    for z in range(4):
                        sp.wait_ge(turned, 4 * i + z + 1)
                        load(4 * i + 4 + z, z, i + 1)
                        store(4 * i + z - 2, (z - 2) % 4)
                for n in range(N - 6, N):
                    store(n, n % 4)
                for z in range(4):
                    sp.wait_ge(stored[z], 16 * (N // 4))

            @block.tensor
            def _(pe):
                expert = lambda n: pe.value_load(m.tile_expert[0:1, bass.ds(n, 1)], min_val=0, max_val=E8 - 1)

                def turn(z, q):
                    pe.wait_ge(loaded[z], 16 * (q + 1))
                    pe.transpose(X[z % 2][:, 0:P], rows[z][:], ident).then_inc(turned, 1)

                def gate_up(n, z):
                    e = expert(n)
                    pe.wait_ge(ht_ready, n + 1)
                    pe.matmul(G[z % 2][:, 0:FF1], hT[z % 2][:], gw[:, bass.ds(e, 1), :], start=True, stop=True)
                    pe.matmul(U[z % 2][:, 0:FF1], hT[z % 2][:], uw[:, bass.ds(e, 1), :], start=True, stop=True).then_inc(gu_ready, 1)

                def turn_hidden(n, z, later=True):
                    if later:
                        pe.wait_ge(ht_ready, n + 3)
                    pe.wait_ge(hid_ready, n + 1)
                    for f, (o, w) in enumerate(BLOCKS1):
                        mm = pe.transpose(X[z % 2][0:w, (f + 1) * P:(f + 2) * P], hid[z % 2][:, o:o + w], ident)
                    mm.then_inc(hid_turned, 1)

                def down(n, z, reused=True):
                    e = expert(n)
                    if reused:
                        pe.wait_ge(eo_ready, n - 1)
                    pe.wait_ge(hidT_ready, n + 1)
                    for f, (o, w) in enumerate(BLOCKS1):
                        mm = pe.matmul(O[z % 2][:, 0:P], hidT[z % 2][0:w, f], dw[0:w, bass.ds(e, 1), f], start=f == 0, stop=f == 2)
                    mm.then_inc(down_ready, 1)

                turn(0, 0)
                turn(1, 0)
                gate_up(0, 0)
                for n in range(1, 5):
                    turn((n + 1) % 4, (n + 1) // 4)
                    gate_up(n, n % 4)
                    turn_hidden(n - 1, (n - 1) % 4)
                    if n >= 2:
                        down(n - 2, (n - 2) % 4, n >= 4)
                with pe.Fori(1, N // 4 - 1) as i:
                    for z in range(1, 5):
                        turn((z + 1) % 4, i + (z + 1) // 4)
                        gate_up(4 * i + z, z % 4)
                        turn_hidden(4 * i + z - 1, (z - 1) % 4)
                        down(4 * i + z - 2, (z - 2) % 4)
                for n in range(N - 3, N):
                    if n + 1 < N:
                        turn((n + 1) % 4, (n + 1) // 4)
                    gate_up(n, n % 4)
                    turn_hidden(n - 1, (n - 1) % 4, n + 1 < N)
                    down(n - 2, (n - 2) % 4)
                turn_hidden(N - 1, 3, False)
                down(N - 2, 2)
                down(N - 1, 3)

            @block.scalar
            def _(act):
                def modulate(n, z):
                    act.wait_ge(turned, n + 1)
                    act.activation(hT[z % 2][:], X[z % 2][:, 0:P], ACT.Identity, bias=m.modc[:, 6:7], scale=m.modc[:, 7:8]).then_inc(ht_ready, 1)

                def silu(n, z, reused=True):
                    if reused:
                        act.wait_ge(hid_ready, n - 1)
                    act.wait_ge(gu_ready, n + 1)
                    act.activation(sg[z % 2][:], G[z % 2][:, 0:FF1], ACT.Silu).then_inc(silu_done, 1)

                modulate(0, 0)
                for n in range(4):
                    modulate(n + 1, n + 1)
                    silu(n, n, n >= 2)
                with act.Fori(1, N // 4 - 1) as i:
                    for z in range(4):
                        modulate(4 * i + z + 1, z + 1)
                        silu(4 * i + z, z)
                for n in range(N - 4, N):
                    if n + 1 < N:
                        modulate(n + 1, n + 1)
                    silu(n, n)

            @block.vector
            def _(v):
                def hidden(n, z):
                    v.wait_ge(silu_done, n + 1)
                    v.tensor_tensor(hid[z % 2][:], U[z % 2][:, 0:FF1], sg[z % 2][:], ALU.mult).then_inc(hid_ready, 1)

                def hidden_turned(n, z):
                    v.wait_ge(hid_turned, n + 1)
                    v.tensor_copy(hidT[z % 2][:], X[z % 2][:, P:4 * P].rearrange("p (f t) -> p f t", t=P)).then_inc(hidT_ready, 1)

                def finish(n, z, q, reused=True):
                    if reused:
                        v.wait_ge(stored[z % 4], 16 * q)
                    v.wait_ge(down_ready, n + 1)
                    v.tensor_tensor(eo[z % 4][:], O[z % 2][:, 0:P], m.gates[:, 3], ALU.mult).then_inc(eo_ready, 1)

                hidden(0, 0)
                for n in range(1, 6):
                    hidden(n, n)
                    hidden_turned(n - 1, n - 1)
                    if n >= 2:
                        finish(n - 2, n - 2, 0, False)
                with v.Fori(1, N // 4 - 1) as i:
                    for z in range(2, 6):
                        hidden(4 * i + z, z)
                        hidden_turned(4 * i + z - 1, z - 1)
                        finish(4 * i + z - 2, z - 2, i)
                for n in range(N - 2, N):
                    hidden(n, n)
                    hidden_turned(n - 1, n - 1)
                    finish(n - 2, n - 2, (n - 2) // 4)
                hidden_turned(N - 1, N - 1)
                finish(N - 2, 2, (N - 2) // 4)
                finish(N - 1, 3, (N - 1) // 4)


def combine(nc, m, dram, out):
    with ExitStack() as ctx:
        got = ctx.enter_context(nc.sbuf_tensor("got_cb", [P, 2, TILES, D], F32))
        added, written = m.sem("cb_added"), m.sem("cb_written")
        with nc.Block() as block:
            @block.gpsimd
            def _(g):
                gather_rows(g, m, 1, dram, got)

            @block.vector
            def _(v):
                for c in range(NC4):
                    add_rows(v, m, 1, c, got)

            @block.sync
            def _(sp):
                for c in range(NC4):
                    sp.wait_ge(added, (NC4 + c + 1) * 2 * TPC)
                    sp.dma_start(out[0].rearrange("(b p) d -> p b d", p=P)[:, c * TPC:(c + 1) * TPC], m.x[:, c * TPC:(c + 1) * TPC]).then_inc(written, 16)
                sp.wait_ge(written, 16 * NC4)


class Memory:

    def __init__(self, nc, ctx):
        sb = lambda n, s, d=F32: ctx.enter_context(nc.sbuf_tensor(n, s, d))
        self.sems = {}
        self.new_sem = lambda n: ctx.enter_context(nc.semaphore(n))
        self.x, self.xn, self.vall = sb("x", [P, TILES, D]), sb("xn", [P, TILES, D]), sb("vall", [P, TILES, D])
        self.QS = [sb(f"qs{p}", [P, GH, T], BF) for p in range(2)]
        self.KS = [sb(f"ks{p}", [P, GH, T], BF) for p in range(2)]
        self.araw = sb("araw", [P, TILES, H, HD + 1])
        self.VS = [sb(f"vs{p}", [P, TILES, GH, 32]) for p in range(2)]
        self.pack, self.lpack = sb("pack_sb", [P, W_PACK]), sb("lpack_sb", [LAT, 2 * D + 2])
        at = {}
        o = 0
        for name, w in PACK:
            at[name], o = self.pack[:, o:o + w], o + w
        self.consts, self.wq, self.wdkv = at["consts"], at["wq0"], at["wdkv"]
        self.wo, self.wr = [at["wo0"], at["wo1"]], [at["wr0"], at["wr1"]]
        self.w1small = at["w1small"].rearrange("p (i e) -> p i e", e=HD)
        self.wuk, self.wuv, self.lngb = self.lpack[:, 0:D], self.lpack[:, D:2 * D], self.lpack[:, 2 * D:2 * D + 2]
        self.identb, self.maskTb, self.maskN = sb("identb", [P, P], BF), sb("maskTb", [P, P], BF), sb("maskN", [P, CH])
        self.wqr, self.wukr, self.w1bd = sb("wqr", [P, D]), sb("wukr", [LAT, D]), sb("w1bd", [P, 3, D])
        self.modc, self.gates = sb("modc", [P, 8]), sb("gates", [P, 4, D])
        self.wt, self.pos = sb("wt", [P, 2, TILES]), sb("pos", [P, 2, TILES], U32)
        self.tile_expert = sb("tile_expert", [P, 40], I32)
        self.st = [ctx.enter_context(nc.psum_tensor(f"st{i}", [P, 2, CH], F32)) for i in range(2)]
        self.mxb = [ctx.enter_context(nc.psum_tensor(f"mx{i}", [P, CH], F32)) for i in range(MXBUF)]
        self.avb = ctx.enter_context(nc.psum_tensor("av", [P, CH], F32))
        self.bank = [self.st[0][:, 0], self.st[0][:, 1], self.st[1][:, 0], self.st[1][:, 1]] + [b[:] for b in self.mxb] + [self.avb[:]]
        self.ln_chain, self.pj_chain, self.rt_chain = (Count(self.sem(n)) for n in ("ln_chain", "pj_chain", "rt_chain"))
        self.weights_total = 0

    def sem(self, name):
        if name not in self.sems:
            self.sems[name] = self.new_sem(name)
        return self.sems[name]


def adaln_two_layers(nc, *aps):
    dram = dict(zip(INPUTS, aps))
    out = aps[-1]
    for L in range(2):
        for key in ("q_parts", "k_parts"):
            dram[f"{key}{L}"] = nc.dram_tensor(f"{key}{L}", [H * 3 * HD, T], BF).ap()
        for key, n in (("perm", (ROWS0, ROWS1)), ("eo", (ROWS0, ROWS1))):
            dram[f"{key}{L}"] = nc.dram_tensor(f"{key}{L}", [n[L], D], F32).ap()
    with ExitStack() as ctx:
        m = Memory(nc, ctx)
        with ExitStack() as tables:
            m.cosT, m.sinT = (tables.enter_context(nc.sbuf_tensor(n, [P, T], F32)) for n in ("cosT", "sinT"))
            setup(nc, m, dram)
            project(nc, m, 0, dram)
        for L in range(2):
            if L:
                project(nc, m, 1, dram)
            with ExitStack() as wctx:
                sb = lambda n, s: wctx.enter_context(nc.sbuf_tensor(n, s, F32))
                if L == 0:
                    w1, w2 = sb("w1_sb", [P, E8, FF0]), sb("w2_sb", [P, E8 * FF0 // P, D])
                    weight_loads = [(w1[:, e], dram["w1"][e]) for e in range(E8)] + [
                        (w2[:, 4 * e:4 * e + 4], dram["w2"][e].rearrange("(k p) d -> p k d", p=P)) for e in range(E8)] + [
                        (dram["perm1"].rearrange("(p r) d -> p (r d)", p=P), bass.AP(dram["zeros"].tensor, 0, [[0, P], [1, ROWS1 // P * D]]))]
                else:
                    gw, uw, dw = sb("gw_sb", [P, E8 + 1, FF1]), sb("uw_sb", [P, E8 + 1, FF1]), sb("dw_sb", [P, E8 + 1, 3, D])
                    weight_loads = [(dst[:, 3 * z:3 * z + 3], dram[key][:, 3 * z:3 * z + 3])
                                    for z in range(3) for dst, key in ((gw, "gw"), (uw, "uw"), (dw, "dw"))]
                m.weights_total += len(weight_loads)
                attention(nc, m, L, dram, weight_loads)
                m.hT = wctx.enter_context(nc.sbuf_tensor(f"hT{L}", [P, T], F32))
                route(nc, m, L, dram)
                if L == 0:
                    experts0(nc, m, dram, w1, w2)
                else:
                    shared_expert(nc, m, dram, gw, uw, dw)
                    experts1(nc, m, dram, gw, uw, dw)
        combine(nc, m, dram, out)


INPUTS = ["x", "mod", "pack", "lpack", "cos", "sin", "zo", "zrow", "zeros", "w1", "w2", "gw", "uw", "dw"]


def layout(i):
    a = {k: np.asarray(v) for k, v in i.items()}
    q = np.arange(P)
    consts = np.zeros((P, C_W), np.float32)
    consts[:, C_ID:C_ID + P] = np.eye(P)
    consts[:, C_MN:C_MN + P] = np.where(q[None, :] <= q[:, None], 0, NEG)
    consts[:, C_MT:C_MT + P] = np.where(q[:, None] <= q[None, :], 0, NEG)
    consts[:, C_UP:C_UP + P] = q[:, None] < q[None, :]
    consts[:, C_BD:C_BD + P] = q[:, None] // HD == q[None, :] // HD
    consts[:, C_I8:C_I8 + E8] = np.arange(E8) - E8
    consts[:, C_IT:C_IT + 40] = np.arange(40)
    consts[:, C_TH:C_TH + TILES] = P * np.arange(TILES)
    half = HD // 2
    inv = (np.float32(1.0) / np.float32(10000.0) ** (np.arange(half, dtype=np.float32) / np.float32(half))).astype(np.float32)
    ang = (np.arange(T, dtype=np.float32)[None, :] * inv[:, None]).astype(np.float32)
    ones = np.zeros((GH, 2 * GH, T), np.dtype("bfloat16"))
    for j in range(GH):
        ones[j, 2 * j:2 * j + 2] = 1
    dw = np.zeros((E8 + 1, 3 * P, D), np.float32)
    dw[:E8, :FF1] = a["L1_ffn_expert_down"].transpose(0, 2, 1)
    dw[E8, :FF1] = a["L1_ffn_shared_down"].T
    both = lambda e, s: np.concatenate([a[e], a[s][None]]).transpose(2, 0, 1)
    heads = [a[f"L1_attn_{n}"].reshape(P, HD) for n in ("Wq", "Wk", "Wv")]
    return {
        "x": a["L0_attn_x"][0], "cos": np.cos(ang).astype(np.float32), "sin": np.sin(ang).astype(np.float32),
        "zo": ones, "zrow": np.zeros((2 * GH, T), np.dtype("bfloat16")), "zeros": np.zeros((1, ROWS1 // P * D), np.float32),
        "mod": np.concatenate([a["L0_c"].T, a["L1_c"].T, a["L0_wmod"], a["L1_wmod"]], 1),
        "pack": np.concatenate([consts, a["L0_attn_W_q"], a["L0_attn_W_dkv"], a["L0_attn_W_o"], a["L1_attn_Wo"],
                                a["L0_ffn_Wr"].T, a["L1_ffn_gate_w"].T] + heads, 1),
        "lpack": np.concatenate([a["L0_attn_W_uk"], a["L0_attn_W_uv"], a["L0_attn_ln_gamma"][:, None], a["L0_attn_ln_beta"][:, None]], 1),
        "w1": a["L0_ffn_W1"], "w2": a["L0_ffn_W2"],
        "gw": both("L1_ffn_expert_gate", "L1_ffn_shared_gate"), "uw": both("L1_ffn_expert_up", "L1_ffn_shared_up"),
        "dw": dw.reshape(E8 + 1, 3, P, D).transpose(2, 0, 1, 3)}


def kernel(**inputs):
    import concourse.bacc as bacc
    from concourse.bass_utils import run_bass_kernel_spmd

    nc = bacc.Bacc("TRN2", target_bir_lowering=False, num_devices=1)
    arrays, args = {}, []
    laid = layout(inputs)
    for name in INPUTS:
        a = np.ascontiguousarray(laid[name])
        arrays[f"in_{name}_dram"] = a
        args.append(nc.dram_tensor(f"in_{name}_dram", a.shape, mybir.dt.from_np(a.dtype), kind="ExternalInput").ap())
    args.append(nc.dram_tensor("out_0_dram", (1, T, D), F32, kind="ExternalOutput").ap())
    adaln_two_layers(nc, *args)
    r = run_bass_kernel_spmd(nc, [arrays], core_ids=[0])
    return r.results[0]["out_0_dram"]
```

```python
import numpy as np
import concourse.bass as bass
from concourse import mybir
from concourse.alu_op_type import AluOpType as ALU
from contextlib import ExitStack

F32 = mybir.dt.float32
BF = mybir.dt.bfloat16
U32 = mybir.dt.uint32
I32 = mybir.dt.int32
ACT = mybir.ActivationFunctionType
AX = mybir.AxisListType

P = 128
T = 2048
D = 128
H, HD = 16, 8
TILES = T // P
CH = 512
NC4 = T // CH
TPC = CH // P
LAT = 32
E8 = 8
FF0, FF1 = 512, 352
EPS = 1e-5
NEG = -1e30
SCALE = float(1 / np.sqrt(np.float32(HD)))
GH = 4
NG = H // GH
SHIFT0 = 96
MXBUF = 3

ROWS0 = 2 * T
RTILES1 = 2 * T // P + E8 - 1
ROWS1 = (RTILES1 + 1) * P

C_ID, C_MN, C_MT, C_UP, C_BD, C_I8, C_IT, C_TH, C_SL, C_W = 0, 128, 256, 384, 512, 640, 648, 688, 704, 736
ROW = D + 2
PACK = [("consts", C_W), ("wq0", D), ("wdkv", LAT), ("wo0", D), ("wo1", D), ("wr0", E8), ("wr1", E8), ("w1small", 3 * HD)]
W_PACK = sum(w for _, w in PACK)
W_MOD = 2 + 12 * D

UNITS = [(0, 0), (0, 1), (0, 2), (1, 1), (0, 3), (1, 2), (1, 3), (1, 0),
         (2, 2), (2, 3), (3, 3), (2, 1), (3, 1), (2, 0), (3, 0), (3, 2)]
STEPS = [(g, Q, kb) for g, Q in UNITS for kb in range(TPC * (Q + 1))]
NU, NST = len(UNITS), len(STEPS)
UNIT = [UNITS.index(s[:2]) for s in STEPS]
FIRST = [UNIT.index(u) for u in range(NU)] + [NST]
FIRST_UNIT = [min(u for u, x in enumerate(UNITS) if x[0] == g) for g in range(NG)]
LAST = [max(s for s, x in enumerate(STEPS) if x[0] == g) for g in range(NG)]
TURN_LAG = 3


def max_tiles(g, Q):
    return [(g, Q, j, qb, c) for qb in range(TPC) for j in range(GH) for c in range(Q + 1)]


def max_width(m):
    return CH if m[4] < m[1] else (m[3] + 1) * P


def step_off(s):
    return max(0, STEPS[s][2] * P - STEPS[s][1] * CH)


def schedule():
    base, due = [], []
    for u, (g, Q) in enumerate(UNITS):
        for m in max_tiles(g, Q):
            base.append(("max", m))
            if due and due[0][0] <= len(base):
                base.append(("turn", due.pop(0)[1]))
        due.append((len(base) + TURN_LAG, u))
    base += [("turn", u) for _, u in due]
    pe = dve = act = 0.0
    out, rot = [], []
    k = s = half = 0
    lat = 0.1
    ready = [1e9] * NU
    free = [0.0] * MXBUF
    last_max, exp_done = {}, [0.0, 0.0]
    loaded = [0.0, 22.0] + [1e9] * NG
    norms = []
    normed = [0] * NC4
    while k < len(base) or s < NST or norms:
        b = len(rot) % MXBUF
        if norms and norms[0][0] <= pe or (k == len(base) and s == NST):
            _, kind, x = norms.pop(0)
            pe = max(pe, free[b] + lat) + (.9 if kind == "out" else .4)
            dve = max(dve, pe + lat) + {"norm": .5, "attT": .6, "out": 2.5}[kind]
            free[b] = dve
            out.append(("rot", len(rot)))
            rot.append((kind, x))
            if kind == "norm":
                Q = UNITS[x][1]
                normed[Q] += 1
                if normed[Q] == NG:
                    norms.append((dve + 4, "attT", Q))
            elif kind == "attT":
                norms.append((dve + 4, "out", x))
            continue
        t_step = max(pe, ready[UNIT[s]], exp_done[half] + lat) if s < NST and ready[UNIT[s]] < 1e8 else 1e9
        t_max = 1e9
        if k < len(base):
            kind, x = base[k]
            t_max = max(pe, free[b] + lat)
            if kind == "max":
                t_max = max(t_max, loaded[x[0]] if x[0] or x[1] < NC4 // 2 else 8.0)
            else:
                t_max = max(t_max, last_max[x] + .6)
        if t_max <= t_step + 0.2 and k < len(base):
            pe = t_max
            if kind == "max":
                w = max_width(x)
                pe += w / 2400 + .003
                dve = max(dve, pe + lat + .1) + .075 + w * .00104
                last_max[UNITS.index(x[:2])] = dve
            else:
                pe += .22
                dve = max(dve, pe + lat) + .6
                ready[x] = dve + 2.4
            free[b] = dve
            out.append(("rot", len(rot)))
            rot.append((kind, x))
            k += 1
        else:
            pe = t_step
            w = CH - step_off(s)
            pe += 2 * w / 2400 + (.11 if STEPS[s][2] >= TPC * STEPS[s][1] else 0)
            act = max(act, pe + lat + .1) + .19 + 2 * w * .000833
            exp_done[half] = act
            out.append(("scores", s, half))
            if half == 1:
                if s:
                    out.append(("av", s - 1))
                    pe += 4 * (CH - step_off(s - 1)) / 2400
                    if s - 1 in LAST:
                        loaded[LAST.index(s - 1) + 2] = pe + 9
                    if s in FIRST:
                        norms.append((pe + 3, "norm", UNIT[s] - 1))
                s += 1
                if s == NST:
                    out.append(("av", NST - 1))
                    norms.append((pe + 3, "norm", NU - 1))
            half ^= 1
    return out, rot, pe


ORDER, ROT, _ = schedule()
NROT = len(ROT)
ATTT_AT = {x: k for k, (kind, x) in enumerate(ROT) if kind == "attT"}
NORM_AT = {x: k for k, (kind, x) in enumerate(ROT) if kind == "norm"}


class Count:

    def __init__(self, sem):
        self.sem, self.value = sem, 0

    def next(self, n=1):
        self.value += n
        return self.value


def setup(nc, m, dram):
    with ExitStack() as ctx:
        sb = lambda n, s, d=F32: ctx.enter_context(nc.sbuf_tensor(n, s, d))
        mod = sb("mod", [P, W_MOD])
        scol, sbc = sb("scol", [P, 2]), sb("sbc", [P, 2, P])
        gate, sign = sb("gate", [P, 4, D]), sb("sign", [P, 4, D])
        wmod = lambda l, part: mod[:, 2 + (6 * l + part) * D:2 + (6 * l + part + 1) * D]
        mod_loaded, pack_loaded = m.sem("mod_loaded"), m.sem("pack_loaded")
        silu_done, bc_done, cols_ready, rows_ready = (m.sem(n) for n in ("silu_done", "bc_done", "cols_ready", "rows_ready"))
        gates, weights_ready, pool_set = Count(m.sem("gates_chain")), m.sem("weights_ready"), m.sem("pool_set")

        with nc.Block() as block:
            @block.sync
            def _(sp):
                sp.dma_start(mod[:], dram["mod"]).then_inc(mod_loaded, 16)
                for z in range(NC4):
                    sp.dma_start(m.x[:, 4 * z:4 * z + 4], dram["x"].rearrange("(b p) d -> p b d", p=P)[:, 4 * z:4 * z + 4]).then_inc(m.sem("x_loaded"), 16)
                sp.dma_start(m.pack[:], dram["pack"]).then_inc(pack_loaded, 16)
                sp.dma_start(m.lpack[:], dram["lpack"]).then_inc(pack_loaded, 16)
                for dst, key in ((m.cosT, "cos"), (m.sinT, "sin")):
                    sp.dma_start(dst[:], bass.AP(dram[key].tensor, 0, [[0, 2 * H], [T, HD // 2], [1, T]])).then_inc(m.sem("tables"), 16)
                sp.wait_ge(m.sem("x_loaded"), 16 * NC4)

            @block.scalar
            def _(act):
                act.wait_ge(mod_loaded, 16)
                act.activation(scol[:], mod[:, 0:2], ACT.Silu).then_inc(silu_done, 1)

            @block.tensor
            def _(pe):
                pe.wait_ge(bc_done, 2)
                for l in range(2):
                    for i, part in enumerate((0, 1, 3, 4)):
                        mm = pe.matmul(m.bank[0][:, 4 * l + i:4 * l + i + 1], wmod(l, part), scol[:, l:l + 1], start=True, stop=True)
                mm.then_inc(cols_ready, 1)
                for l in range(2):
                    for i, part in enumerate((2, 5)):
                        mm = pe.matmul(m.bank[1][:, (2 * l + i) * D:(2 * l + i + 1) * D], sbc[:, l, :], wmod(l, part), start=True, stop=True)
                mm.then_inc(rows_ready, 1)

            @block.gpsimd
            def _(g):
                for p in range(2):
                    g.memset(m.VS[p][:], 0.).then_inc(pool_set, 1)
                g.wait_ge(pool_set, 2)
                for p in range(2):
                    g.memset(m.VS[p][:, :, :, HD:HD + 1], 1.).then_inc(pool_set, 1)

            @block.vector
            def _(v):
                v.wait_ge(silu_done, 1)
                for l in range(2):
                    v.tensor_copy(sbc[:, l, :], scol[:, l:l + 1].to_broadcast([P, P])).then_inc(bc_done, 1)
                v.wait_ge(pack_loaded, 32)
                for src, dst in ((m.wq, m.wqr), (m.wuk, m.wukr)):
                    a = src.rearrange("p (h u d) -> p h u d", u=2, d=HD // 2)
                    b = dst[:].rearrange("p (h u d) -> p h u d", u=2, d=HD // 2)
                    v.tensor_scalar(b[:, :, 0], a[:, :, 1], -1., None, ALU.mult).then_inc(weights_ready, 1)
                    v.tensor_copy(b[:, :, 1], a[:, :, 0]).then_inc(weights_ready, 1)
                for i in range(3):
                    v.tensor_tensor(m.w1bd[:, i].rearrange("p (h e) -> p h e", e=HD),
                                    m.consts[:, C_BD:C_BD + P].rearrange("p (h e) -> p h e", e=HD),
                                    m.w1small[:, i:i + 1, :].to_broadcast([P, H, HD]), ALU.mult).then_inc(weights_ready, 1)
                v.tensor_copy(m.identb[:], m.consts[:, C_ID:C_ID + P]).then_inc(weights_ready, 1)
                v.tensor_copy(m.maskTb[:], m.consts[:, C_MT:C_MT + P]).then_inc(weights_ready, 1)
                v.memset(m.maskN[:, 0:CH - P], 0.).then_inc(weights_ready, 1)
                v.tensor_copy(m.maskN[:, CH - P:], m.consts[:, C_MN:C_MN + P]).then_inc(weights_ready, 1)
                v.wait_ge(cols_ready, 1)
                v.tensor_copy(m.modc[:], m.bank[0][:, 0:8]).then_inc(gates.sem, 1)
                v.wait_ge(gates.sem, gates.next())
                for i in (1, 3, 5, 7):
                    v.tensor_scalar(m.modc[:, i:i + 1], m.modc[:, i:i + 1], 1.0, None, ALU.add).then_inc(gates.sem, 1)
                v.wait_ge(rows_ready, 1)
                g2, s2 = gate[:].rearrange("p a d -> p (a d)"), sign[:].rearrange("p a d -> p (a d)")
                v.tensor_scalar(s2, m.bank[1][:], 0., 2., ALU.is_ge, ALU.mult).then_inc(gates.sem, 1)
                v.wait_ge(gates.sem, gates.next(5))
                v.tensor_scalar(s2, s2, -1., None, ALU.add).then_inc(gates.sem, 1)
                v.wait_ge(gates.sem, gates.next())
                v.tensor_tensor(g2, m.bank[1][:], s2, ALU.mult).then_inc(gates.sem, 1)
                v.wait_ge(gates.sem, gates.next())
                v.tensor_scalar(g2, g2, .25, None, ALU.max).then_inc(gates.sem, 1)
                v.wait_ge(gates.sem, gates.next())
                v.tensor_tensor(m.gates[:].rearrange("p a d -> p (a d)"), g2, s2, ALU.mult).then_inc(gates.sem, 1)
                v.wait_ge(gates.sem, gates.next())
                for l in range(2):
                    v.tensor_tensor(m.wo[l], m.wo[l], m.gates[:, 2 * l], ALU.mult).then_inc(weights_ready, 1)


def reciprocal_root(v, act_done, count, a, root, y, t):
    v.wait_ge(act_done[0], act_done[1])
    v.reciprocal(y, root).then_inc(count.sem, 1)
    v.wait_ge(count.sem, count.next())
    v.tensor_tensor(t, y, y, ALU.mult).then_inc(count.sem, 1)
    v.wait_ge(count.sem, count.next())
    v.tensor_tensor(t, t, a, ALU.mult).then_inc(count.sem, 1)
    v.wait_ge(count.sem, count.next())
    v.tensor_scalar(t, t, -.5, 1.5, ALU.mult, ALU.add).then_inc(count.sem, 1)
    v.wait_ge(count.sem, count.next())
    v.tensor_tensor(y, y, t, ALU.mult).then_inc(count.sem, 1)
    v.wait_ge(count.sem, count.next())


class LayerNorm:

    def __init__(self, nc, ctx, m, n, xn):
        self.xn, self.taken = xn, 0
        self.roots = (0, NC4, NC4 + 1, 2 * NC4 + 1)[n]
        sb = lambda name, s: ctx.enter_context(nc.sbuf_tensor(f"{name}_ln{n}", s, F32))
        self.m, self.base = m, n * NC4
        self.st, self.mv = sb("st", [P, TILES, 6]), sb("mv", [P, TILES, 2])
        self.a, self.root, self.y, self.t = (sb(k, [P, TILES]) for k in "a root y t".split())
        self.chain, self.var_ready, self.root_done, self.xn_ready = m.ln_chain, m.sem("ln_var"), m.sem("ln_root"), m.sem("ln_xn")

    def stats(self, v, c):
        m, k = self.m, self.chain
        for b in range(c * TPC, (c + 1) * TPC):
            v.bn_stats(self.st[:, b], m.x[:, b]).then_inc(k.sem, 1)
        v.wait_ge(k.sem, k.next(TPC))
        for b in range(c * TPC, (c + 1) * TPC):
            v.bn_aggr(self.mv[:, b], self.st[:, b]).then_inc(k.sem, 1)
        v.wait_ge(k.sem, k.next(TPC))
        v.tensor_scalar(self.a[:, c * TPC:(c + 1) * TPC], self.mv[:, c * TPC:(c + 1) * TPC, 1], EPS, None, ALU.add).then_inc(self.var_ready, 1)
        self.taken += 1
        v.wait_ge(self.var_ready, self.base + self.taken)

    def take_root(self, act, c=None):
        n, cs = (NC4, slice(0, TILES)) if c is None else (c + 1, slice(c * TPC, (c + 1) * TPC))
        act.wait_ge(self.var_ready, self.base + n)
        act.activation(self.root[:, cs], self.a[:, cs], ACT.Sqrt).then_inc(self.root_done, 1)

    def invert(self, v, c=None):
        cs = slice(0, TILES) if c is None else slice(c * TPC, (c + 1) * TPC)
        self.roots += 1
        reciprocal_root(v, (self.root_done, self.roots), self.chain, self.a[:, cs], self.root[:, cs], self.y[:, cs], self.t[:, cs])

    def normalise(self, v, c):
        m = self.m
        for b in range(c * TPC, (c + 1) * TPC):
            v.tensor_scalar(self.xn[:, b], m.x[:, b], self.mv[:, b, 0:1], self.y[:, b:b + 1], ALU.subtract, ALU.mult).then_inc(self.xn_ready, 1)

    def wait_chunk(self, pe, c):
        pe.wait_ge(self.xn_ready, TPC * (self.base + c + 1))


def project(nc, m, L, dram):
    with ExitStack() as ctx:
        sb = lambda name, s, d=F32: ctx.enter_context(nc.sbuf_tensor(f"{name}_pj{L}", s, d))
        hT = sb("hT", [P, T])
        qf, res = [sb(f"qf{i}", [P, CH]) for i in range(2)], [sb(f"res{i}", [P, CH]) for i in range(2)]
        parts = [[sb(f"part{i}{a}", [P, T], BF) for a in range(3)] for i in range(2)]
        xn = sb("xn", [P, TILES, D])
        ln = LayerNorm(nc, ctx, m, 2 * L, xn)
        if L == 0:
            tmp = [sb(f"tmp{i}", [P, CH]) for i in range(2)]
            cen, sq, latn = (sb(k, [P, TILES, LAT]) for k in ("cen", "sq", "latn"))
            latT = sb("latT", [LAT, T])
            mean, a, root, y, t = (sb(k, [P, TILES]) for k in ("mean", "a", "root", "y", "t"))
            steps = [(i, c) for i in range(2) for c in range(NC4)]
        else:
            got = sb("got", [P, TILES, 2, D])
            steps = [(i, c) for c in range(NC4) for i in range(2)]
        names = "turned ht_ready lat_ready lat_var lat_root latn_ready latT_turned latT_ready v_ready v_out proj_ready proj_used qf_ready hi_done r_done mid_done lo_done stored".split()
        (turned, ht_ready, lat_ready, lat_var, lat_root, latn_ready, latT_turned, latT_ready, v_ready, v_out, proj_ready,
         proj_used, qf_ready, hi_done, r_done, mid_done, lo_done, stored) = (m.sem("pj_" + k) for k in names)
        chain = m.pj_chain
        bank = m.bank
        NS = len(steps)
        s8, s4 = NS * L, NC4 * L
        product = (lambda n: (bank[5], bank[7])[n % 2]) if L == 0 else (lambda n: bank[4 + n % 4])
        rotated = lambda n: (bank[6], bank[0])[n % 2]
        v_bank = lambda c: bank[1 + c] if L == 0 else bank[c]
        ident = m.consts[:, C_ID:C_ID + P]
        cols = lambda c: slice(c * CH, (c + 1) * CH)

        with nc.Block() as block:
            @block.sync
            def _(sp):
                if L == 0:
                    sp.wait_ge(m.sem("pool_set"), 8)
                    for p in range(2):
                        for j in range(GH):
                            sp.dma_start(m.KS[p][SHIFT0:SHIFT0 + 2 * GH, j, :], dram["zo"][j]).then_inc(m.sem("ones_in"), 16)
                    sp.wait_ge(m.sem("ones_in"), 16 * 2 * GH)
                else:
                    load_rows(sp, m, 0, dram, got)
                issued = 12 * L
                for n, (i, c) in enumerate(steps):
                    if c % 2 == 0:
                        continue
                    sp.wait_ge(lo_done, s8 + n + 1)
                    half = (c - 1) * CH
                    for a3 in range(3):
                        dst = bass.AP(dram[f"{('q_parts', 'k_parts')[i]}{L}"].tensor, a3 * HD * T + half, [[3 * HD * T, H], [T, HD], [1, 2 * CH]])
                        sp.dma_start(dst, parts[i][a3][:, half:half + 2 * CH]).then_inc(stored, 16)
                        issued += 1
                    if L == 0 and n in (3, 5) or L == 1 and n == 3:
                        sp.wait_ge(stored, 16 * issued)
                    if L == 0 and n == 3:
                        load_q(sp, m, L, dram, 0, slice(0, T), m.sem("first_half"))
                    if L == 0 and n == 5:
                        load_k(sp, m, L, dram, 0, slice(0, T // 2), m.sem("first_half"))
                    if L == 1 and n == 3:
                        load_q(sp, m, L, dram, 0, slice(0, T // 2), m.sem("first_half"))
                        load_k(sp, m, L, dram, 0, slice(0, T // 2), m.sem("first_half"))
                sp.wait_ge(stored, 12 * 16 * (L + 1))

            @block.tensor
            def _(pe):
                def heads(n):
                    i, c = steps[n]
                    rhs = (latT if i and L == 0 else hT)[:, cols(c)]
                    if L == 0:
                        if n >= 2:
                            pe.wait_ge(proj_used, n - 1)
                        pe.matmul(rotated(n), (m.wqr, m.wukr)[i][:], rhs, start=True, stop=True)
                        mm = pe.matmul(product(n), (m.wq, m.wuk)[i], rhs, start=True, stop=True)
                    else:
                        if n >= 4:
                            pe.wait_ge(r_done, s8 + n - 3)
                        mm = pe.matmul(product(n), m.w1bd[:, i], rhs, start=True, stop=True)
                    mm.then_inc(proj_ready, 1)

                def values(c):
                    for t4 in range(TPC):
                        b = c * TPC + t4
                        mm = pe.matmul(v_bank(c)[:, t4 * P:(t4 + 1) * P], (latT if L == 0 else hT)[:, b * P:(b + 1) * P],
                                       m.wuv if L == 0 else m.w1bd[:, 2], start=True, stop=True)
                    mm.then_inc(v_ready, 1)

                for c in range(NC4):
                    ln.wait_chunk(pe, c)
                    for t4 in range(TPC):
                        mm = pe.transpose(bank[c][:, t4 * P:(t4 + 1) * P], xn[:, c * TPC + t4], ident)
                    mm.then_inc(turned, 1)
                    pe.wait_ge(ht_ready, s4 + c + 1)
                    if L == 0:
                        for b in range(c * TPC, (c + 1) * TPC):
                            mm = pe.matmul(bank[4][:, b * LAT:(b + 1) * LAT], hT[:, b * P:(b + 1) * P], m.wdkv, start=True, stop=True)
                        mm.then_inc(lat_ready, 1)
                    else:
                        heads(2 * c)
                        heads(2 * c + 1)
                        values(c)
                if L == 0:
                    heads(0)
                    heads(1)
                    pe.wait_ge(latn_ready, 1)
                    for c in range(NC4):
                        for t4 in range(TPC):
                            mm = pe.transpose(bank[1 + c][0:LAT, t4 * P:(t4 + 1) * P], latn[:, c * TPC + t4], ident)
                        mm.then_inc(latT_turned, 1)
                    for c in range(NC4):
                        pe.wait_ge(latT_ready, c + 1)
                        values(c)
                    for n in range(2, NS):
                        heads(n)

            @block.scalar
            def _(act):
                def hi(n):
                    i, c = steps[n]
                    if L == 0:
                        act.wait_ge(qf_ready, n + 1)
                    else:
                        act.wait_ge(proj_ready, s8 + n + 1)
                    act.copy(parts[i][0][:, cols(c)], qf[n % 2][:] if L == 0 else product(n)).then_inc(hi_done, 1)

                def mid(n):
                    i, c = steps[n]
                    act.wait_ge(r_done, s8 + n + 1)
                    act.copy(parts[i][1][:, cols(c)], res[n % 2][:]).then_inc(mid_done, 1)

                def split(n):
                    hi(n)
                    if n:
                        mid(n - 1)

                def v_rows(c):
                    act.wait_ge(v_ready, s4 + c + 1)
                    act.copy(m.vall[:, c * TPC:(c + 1) * TPC], v_bank(c).rearrange("p (b d) -> p b d", d=D)).then_inc(v_out, 1)

                ln.take_root(act, 0)
                for c in range(NC4):
                    if c + 1 < NC4:
                        ln.take_root(act, c + 1)
                    act.wait_ge(turned, s4 + c + 1)
                    act.activation(hT[:, cols(c)], bank[c], ACT.Identity, bias=m.modc[:, 4 * L:4 * L + 1],
                                   scale=m.modc[:, 4 * L + 1:4 * L + 2]).then_inc(ht_ready, 1)
                    if L == 1:
                        split(2 * c)
                        split(2 * c + 1)
                        v_rows(c)
                if L == 0:
                    act.wait_ge(lat_var, 1)
                    act.activation(root[:], a[:], ACT.Sqrt).then_inc(lat_root, 1)
                    for c in range(NC4):
                        act.wait_ge(latT_turned, c + 1)
                        act.activation(latT[:, cols(c)], bank[1 + c][0:LAT], ACT.Identity, bias=m.lngb[:, 1:2],
                                       scale=m.lngb[:, 0:1]).then_inc(latT_ready, 1)
                    for c in range(NC4):
                        split(c)
                        v_rows(c)
                    for n in range(NC4, NS):
                        split(n)
                mid(NS - 1)

            @block.vector
            def _(v):
                def rope(n):
                    i, c = steps[n]
                    if n:
                        v.wait_ge(qf_ready, n)
                    if n >= 2:
                        v.wait_ge(r_done, n - 1)
                    v.wait_ge(proj_ready, n + 1)
                    v.tensor_tensor(tmp[0][:], product(n), m.cosT[:, cols(c)], ALU.mult).then_inc(chain.sem, 1)
                    v.tensor_tensor(tmp[1][:], rotated(n), m.sinT[:, cols(c)], ALU.mult).then_inc(proj_used, 1)
                    v.wait_ge(chain.sem, chain.next())
                    v.wait_ge(proj_used, n + 1)
                    v.tensor_tensor(qf[n % 2][:], tmp[0][:], tmp[1][:], ALU.add).then_inc(qf_ready, 1)

                def residue(n):
                    i, c = steps[n]
                    if n >= 2:
                        v.wait_ge(lo_done, s8 + n - 1)
                    v.wait_ge(hi_done, s8 + n + 1)
                    v.tensor_tensor(res[n % 2][:], qf[n % 2][:] if L == 0 else product(n), parts[i][0][:, cols(c)], ALU.subtract).then_inc(r_done, 1)

                def step(n):
                    if L == 0:
                        rope(n)
                        if n:
                            residue(n - 1)
                    else:
                        residue(n)

                def chunk_in(c):
                    if L == 1:
                        add_rows(v, m, 0, c, got)
                    ln.stats(v, c)

                chunk_in(0)
                if L == 0:
                    for c in range(NC4):
                        if c + 1 < NC4:
                            chunk_in(c + 1)
                        ln.invert(v, c)
                        ln.normalise(v, c)
                    lat = bank[4].rearrange("p (b l) -> p b l", l=LAT)
                    v.wait_ge(lat_ready, NC4)
                    v.tensor_reduce(mean[:], lat, AX.X, ALU.add).then_inc(chain.sem, 1)
                    v.wait_ge(chain.sem, chain.next())
                    v.tensor_scalar(mean[:], mean[:], 1 / LAT, None, ALU.mult).then_inc(chain.sem, 1)
                    v.wait_ge(chain.sem, chain.next())
                    v.tensor_tensor(cen[:], lat, mean[:].unsqueeze(2).to_broadcast([P, TILES, LAT]), ALU.subtract).then_inc(chain.sem, 1)
                    v.wait_ge(chain.sem, chain.next())
                    v.tensor_tensor(sq[:], cen[:], cen[:], ALU.mult).then_inc(chain.sem, 1)
                    v.wait_ge(chain.sem, chain.next())
                    v.tensor_reduce(a[:], sq[:], AX.X, ALU.add).then_inc(chain.sem, 1)
                    v.wait_ge(chain.sem, chain.next())
                    v.tensor_scalar(a[:], a[:], 1 / LAT, EPS, ALU.mult, ALU.add).then_inc(lat_var, 1)
                    v.wait_ge(lat_var, 1)
                    reciprocal_root(v, (lat_root, 1), chain, a[:], root[:], y[:], t[:])
                    v.tensor_tensor(latn[:], cen[:], y[:].unsqueeze(2).to_broadcast([P, TILES, LAT]), ALU.mult).then_inc(latn_ready, 1)
                    v.wait_ge(m.sem("tables"), 32)
                    for n in range(NS):
                        step(n)
                    residue(NS - 1)
                else:
                    for c in range(NC4):
                        ln.invert(v, c)
                        ln.normalise(v, c)
                        if c:
                            step(2 * c - 2)
                            step(2 * c - 1)
                        if c + 1 < NC4:
                            chunk_in(c + 1)
                    step(NS - 2)
                    step(NS - 1)

            @block.gpsimd
            def _(g):
                if L == 0:
                    for z, rows in enumerate(m.QS + m.KS):
                        g.memset(rows[64:P].bitcast(F32), 0.).then_inc(m.sem("pool_set"), 1)
                        g.wait_ge(m.sem("pool_set"), 4 + z + 1)
                for n, (i, c) in enumerate(steps):
                    g.wait_ge(mid_done, s8 + n + 1)
                    g.tensor_tensor(parts[i][2][:, cols(c)], res[n % 2][:], parts[i][1][:, cols(c)], ALU.subtract).then_inc(lo_done, 1)


Q_LOADS, K_LOADS = 9 + 1, 3


def load_q(sp, m, L, dram, g, cols, done):
    p, n = g % 2, cols.stop - cols.start
    if cols.start == 0:
        sp.dma_start(m.QS[p][SHIFT0:SHIFT0 + 2 * GH], bass.AP(dram["zrow"].tensor, 0, [[T, 2 * GH], [0, GH], [1, T]])).then_inc(done, 16)
    for a in range(3):
        for b in range(3):
            r = (3 * a + b) * HD
            sp.dma_start(m.QS[p][r:r + HD, :, cols], bass.AP(
                dram[f"q_parts{L}"].tensor, (g * GH * 3 + a) * HD * T + cols.start, [[T, HD], [3 * HD * T, GH], [1, n]])).then_inc(done, 16)


def load_k(sp, m, L, dram, g, cols, done):
    p, n = g % 2, cols.stop - cols.start
    for a in range(3):
        r = 3 * a * HD
        sp.dma_start(m.KS[p][r:r + 3 * HD, :, cols], bass.AP(
            dram[f"k_parts{L}"].tensor, g * GH * 3 * HD * T + cols.start, [[T, 3 * HD], [3 * HD * T, GH], [1, n]])).then_inc(done, 16)


def load_rest(sp, m, L, dram, done):
    if L == 1:
        load_q(sp, m, L, dram, 0, slice(T // 2, T), done)
    load_k(sp, m, L, dram, 0, slice(T // 2, T), done)


def load_rows(sp, m, L, dram, got):
    for c in range(NC4):
        sp.dma_start(got[:, c * TPC:(c + 1) * TPC].rearrange("p b i d -> p b (i d)"),
                     dram[f"eo{L}"][0:2 * T].rearrange("(b p i) d -> p b (i d)", p=P, i=2)[:, c * TPC:(c + 1) * TPC]).then_inc(m.sem(f"rows_back{c}"), 16)


def add_rows(v, m, L, c, got):
    added = m.sem("cb_added")
    v.wait_ge(m.sem(f"rows_back{c}"), 16 * (L + 1))
    for i in range(2):
        xs = m.x[:, c * TPC:(c + 1) * TPC]
        v.tensor_tensor(xs, xs, got[:, c * TPC:(c + 1) * TPC, i], ALU.add).then_inc(added, 1)
        v.wait_ge(added, 2 * (L * NC4 + c) + i + 1)


def attention(nc, m, L, dram, weight_loads, ln):
    with ExitStack() as ctx:
        sb = lambda name, s, d=F32: ctx.enter_context(nc.sbuf_tensor(f"{name}_at{L}", s, d))
        QS, KS = m.QS, m.KS
        VS = m.VS
        probs = sb("probs", [P, 2, GH, CH])
        avs = sb("avs", [P, 2, CH])
        mxp = sb("mxp", [P, 4, GH * TPC, NC4])
        mx = sb("mx", [P, 4, GH * TPC])
        nsh = sb("nsh", [P, 4, TPC, 2 * GH], BF)
        shrow = sb("shrow", [2 * GH, 4, CH], BF)
        junk = sb("junk", [P, MXBUF, CH])
        att, attT, rec = sb("att", [P, TILES, H, HD]), sb("attT", [P, CH]), sb("rec", [P, 2, TPC, GH])
        st, mxb, avb = m.st, m.mxb, m.avb
        s_ = m.sem
        weights_in = s_("weights_in")
        kq_loaded = [s_(f"kq_loaded{p}") for p in range(2)]
        v_copied = [s_(f"v_copied{p}") for p in range(2)]
        st_ready = [s_(f"st_ready{i}") for i in range(2)]
        exp_done = [s_(f"exp_done{i}") for i in range(2)]
        shift_set = [s_(f"shift_set{u}") for u in range(4)]
        (av_done, av_free, max_final, hi_split, mx_ready, mx_free, shift_split, shift_row) = (s_(n) for n in (
            "av_done", "av_free", "max_final", "hi_split", "mx_ready", "mx_free", "shift_split", "shift_row"))
        rec_ready = s_("rec_ready")
        RB, SB, UB = L * NROT, L * NST, L * NU
        GB = L * NG // 2
        group, rest = Q_LOADS + K_LOADS, (K_LOADS, K_LOADS + Q_LOADS - 1)
        before = (L * (rest[0] + group), L * 2 * group)
        loaded_at = [rest[L], group, rest[L] + group, 2 * group]
        late_half = min(u for u, x in enumerate(UNITS) if x[0] == 0 and x[1] >= NC4 // 2)

        with nc.Block() as block:
            @block.sync
            def _(sp):
                load_rest(sp, m, L, dram, kq_loaded[0])
                loads = list(weight_loads)
                for item in ORDER:
                    if item[0] == "rot" and ROT[item[1]][0] == "turn":
                        u = ROT[item[1]][1]
                        g, Q = UNITS[u]
                        sp.wait_ge(shift_row, UB + u + 1)
                        sp.dma_start(QS[g % 2][SHIFT0:SHIFT0 + 2 * GH, :, Q * CH:(Q + 1) * CH],
                                     shrow[:, u % 4, :].unsqueeze(1).to_broadcast([2 * GH, GH, CH])).then_inc(shift_set[u % 4], 16)
                        if u == 0:
                            load_q(sp, m, L, dram, 1, slice(0, T), kq_loaded[1])
                            load_k(sp, m, L, dram, 1, slice(0, T), kq_loaded[1])
                        elif u > 1:
                            for dst, src in loads[:2]:
                                sp.dma_start(dst, src).then_inc(weights_in, 16)
                            del loads[:2]
                    if item[0] == "av" and item[1] in LAST[:NG - 2]:
                        sp.wait_ge(av_done, 2 + SB + item[1] + 1)
                        g = LAST.index(item[1]) + 2
                        load_q(sp, m, L, dram, g, slice(0, T), kq_loaded[g % 2])
                        load_k(sp, m, L, dram, g, slice(0, T), kq_loaded[g % 2])
                sp.wait_ge(weights_in, 16 * m.weights_total)

            @block.gpsimd
            def _(g):
                for gg in range(NG):
                    p, i = gg % 2, gg // 2
                    if i:
                        g.wait_ge(av_done, 2 + SB + LAST[gg - 2] + 1)
                    g.tensor_copy(VS[p][:, :, :, 0:HD], m.vall[:, :, gg * GH * HD:(gg + 1) * GH * HD].rearrange(
                        "p b (h d) -> p b h d", d=HD)).then_inc(v_copied[p], 1)
                    g.wait_ge(v_copied[p], GB + i + 1)

            @block.tensor
            def _(pe):
                if L == 0:
                    pe.sem_inc(av_done, 2)

                def rotate(k):
                    kind, x = ROT[k]
                    buf = mxb[k % MXBUF]
                    pe.wait_ge(mx_free, RB + k + 1)
                    if kind == "max":
                        gg, Q, j, qb, c = x
                        p, w = gg % 2, max_width(x)
                        if (qb, j, c) == (0, 0, 0):
                            u = UNITS.index((gg, Q))
                            if u == 0:
                                pe.wait_ge(s_("first_half"), 16 * group * (L + 1))
                            elif u == (FIRST_UNIT[gg] if gg else late_half):
                                pe.wait_ge(kq_loaded[p], 16 * (before[p] + loaded_at[gg]))
                        pe.matmul(buf[:, 0:w], QS[p][:, j, (4 * Q + qb) * P:(4 * Q + qb + 1) * P],
                                  KS[p][:, j, c * CH:c * CH + w], start=True, stop=True).then_inc(mx_ready, 1)
                    elif kind == "turn":
                        pe.wait_ge(shift_split, UB + x + 1)
                        for qb in range(TPC):
                            mm = pe.transpose(buf[:].bitcast(BF)[0:2 * GH, qb * P:(qb + 1) * P], nsh[:, x % 4, qb, :], m.identb[:])
                        mm.then_inc(mx_ready, 1)
                    elif kind == "attT":
                        pe.wait_ge(mx_free, RB + max(NORM_AT[u] for u in range(NU) if UNITS[u][1] == x) + 1 + MXBUF)
                        for qb in range(TPC):
                            mm = pe.transpose(buf[:, qb * P:(qb + 1) * P], att[:, x * TPC + qb].rearrange("p h d -> p (h d)"),
                                              m.consts[:, C_ID:C_ID + P])
                        mm.then_inc(mx_ready, 1)
                    elif kind == "out":
                        pe.wait_ge(mx_free, RB + ATTT_AT[x] + 1 + MXBUF)
                        for qb in range(TPC):
                            mm = pe.matmul(buf[:, qb * P:(qb + 1) * P], attT[:, qb * P:(qb + 1) * P], m.wo[L], start=True, stop=True)
                        mm.then_inc(mx_ready, 1)
                    else:
                        pe.wait_ge(av_free, UB + x + 1)
                        for qb in range(TPC):
                            mm = pe.transpose(buf[:, qb * P:(qb + 1) * P], avs[:, x % 2, qb * P:(qb + 1) * P], m.consts[:, C_ID:C_ID + P])
                        mm.then_inc(mx_ready, 1)

                def scores(s, half):
                    gg, Q, kb = STEPS[s]
                    p, off, diag = gg % 2, step_off(s), kb >= TPC * Q
                    if s:
                        pe.wait_ge(exp_done[half], SB + s)
                    for y in range(2):
                        j = 2 * half + y
                        mm = pe.matmul(st[half][:, y, off:CH], KS[p][:, j, kb * P:(kb + 1) * P], QS[p][:, j, Q * CH + off:(Q + 1) * CH],
                                       start=True, stop=True, skip_group_check=diag)
                        if diag:
                            mm = pe.matmul(st[half][:, y, off:off + P], m.identb[:], m.maskTb[:], start=False, stop=True, skip_group_check=True)
                    mm.then_inc(st_ready[half], 1)

                def values(s):
                    gg, Q, kb = STEPS[s]
                    u, p, off = UNIT[s], gg % 2, step_off(s)
                    if kb == 0:
                        pe.wait_ge(v_copied[p], GB + gg // 2 + 1)
                        if u:
                            pe.wait_ge(av_free, UB + u)
                    for half in range(2):
                        pe.wait_ge(exp_done[half], SB + s + 1)
                    for j in range(GH):
                        mm = pe.matmul(avb[32 * j:32 * j + 32, off:CH], VS[p][:, kb, j, :], probs[:, s % 2, j, off:CH],
                                       start=kb == 0, stop=kb == TPC * Q + 3, tile_position=(0, 32 * j), skip_group_check=True)
                    mm.then_inc(av_done, 1)

                for item in ORDER:
                    if item[0] == "rot":
                        rotate(item[1])
                    elif item[0] == "av":
                        values(item[1])
                    else:
                        _, s, half = item
                        if STEPS[s][2] == 0 and half == 0:
                            u = UNIT[s]
                            pe.wait_ge(shift_set[u % 4], 16 * (L * (NU // 4) + u // 4 + 1))
                        scores(s, half)

            @block.scalar
            def _(act):
                def evacuate(u):
                    act.wait_ge(av_done, 2 + SB + FIRST[u + 1])
                    if u >= 2:
                        act.wait_ge(mx_ready, RB + NORM_AT[u - 2] + 1)
                    act.copy(avs[:, u % 2, :], avb[:]).then_inc(av_free, 1)

                for s, (g, Q, kb) in enumerate(STEPS):
                    off = step_off(s)
                    act.wait_ge(av_done, SB + s + 1)
                    for half in range(2):
                        act.wait_ge(st_ready[half], SB + s + 1)
                        act.activation(probs[:, s % 2, 2 * half:2 * half + 2, off:CH], st[half][:, :, off:CH], ACT.Exp,
                                       scale=SCALE).then_inc(exp_done[half], 1)
                    if kb == 0 and s:
                        evacuate(UNIT[s] - 1)
                evacuate(NU - 1)

            @block.vector
            def _(v):
                if L == 0:
                    v.sem_inc(mx_free, MXBUF)
                for k, (kind, x) in enumerate(ROT):
                    buf = mxb[k % MXBUF]
                    v.wait_ge(mx_ready, RB + k + 1)
                    if kind == "max":
                        g, Q, j, qb, c = x
                        u, w = UNITS.index((g, Q)), max_width(x)
                        dst = mxp[:, u % 4, qb * GH + j, c:c + 1]
                        if c < Q:
                            ins = v.tensor_reduce(dst, buf[:, 0:w], AX.X, ALU.max)
                        else:
                            ins = v.tensor_tensor_reduce(junk[:, k % MXBUF, 0:w], buf[:, 0:w], m.maskN[:, CH - w:], 1.0, -3e38,
                                                         ALU.add, ALU.max, dst)
                        ins.then_inc(mx_free, 1)
                        if (j, qb, c) == (GH - 1, TPC - 1, Q):
                            v.wait_ge(mx_free, RB + k + 1 + MXBUF)
                            v.tensor_reduce(mx[:, u % 4, :], mxp[:, u % 4, :, 0:Q + 1], AX.X, ALU.max, negate=True).then_inc(max_final, 1)
                            v.wait_ge(max_final, UB + u + 1)
                            ns = nsh[:, u % 4].rearrange("p q (j s) -> p (q j) s", s=2)
                            v.tensor_copy(ns[:, :, 0], mx[:, u % 4, :]).then_inc(hi_split, 1)
                            v.wait_ge(hi_split, UB + u + 1)
                            v.tensor_tensor(ns[:, :, 1], mx[:, u % 4, :], ns[:, :, 0], ALU.subtract).then_inc(shift_split, 1)
                    elif kind == "turn":
                        if x >= 4:
                            v.wait_ge(shift_set[x % 4], 16 * (L * (NU // 4) + x // 4))
                        v.tensor_copy(shrow[:, x % 4, :], buf[:].bitcast(BF)[0:2 * GH, 0:CH]).then_inc(shift_row, 1)
                        v.wait_ge(shift_row, UB + x + 1)
                        v.sem_inc(mx_free, 1)
                    elif kind == "attT":
                        v.tensor_copy(attT[:], buf[:]).then_inc(mx_free, 1)
                    elif kind == "out":
                        xs = m.x[:, x * TPC:(x + 1) * TPC].rearrange("p b d -> p (b d)")
                        v.tensor_tensor(xs, xs, buf[:], ALU.add).then_inc(mx_free, 1)
                        v.wait_ge(mx_free, RB + k + 1 + MXBUF)
                        ln.stats(v, x)
                    else:
                        g, Q = UNITS[x]
                        sums = buf[:].rearrange("p (q j c) -> p q j c", j=GH, c=32)
                        v.reciprocal(rec[:, x % 2], sums[:, :, :, HD]).then_inc(rec_ready, 1)
                        v.wait_ge(rec_ready, UB + x + 1)
                        v.tensor_tensor(att[:, TPC * Q:TPC * Q + TPC, GH * g:GH * g + GH], sums[:, :, :, 0:HD],
                                        rec[:, x % 2].unsqueeze(3).to_broadcast([P, TPC, GH, HD]), ALU.mult).then_inc(mx_free, 1)


def route(nc, m, L, dram, ln):
    with ExitStack() as ctx:
        sb = lambda name, s, d=F32: ctx.enter_context(nc.sbuf_tensor(f"{name}_rt{L}", s, d))
        hT = m.hT
        S3 = [P, TILES, E8]
        val, eq, cand, sel2, oh1, oh2, both = (sb(k, S3) for k in "val eq cand sel2 oh1 oh2 both".split())
        m1, m2, ix, sm, dif, ex, pf = (sb(k, [P, TILES]) for k in "m1 m2 ix sm dif ex pf".split())
        tot, run = sb("tot", [P, E8, TILES]), sb("run", [P, E8, TILES])
        rank = sb("rank", S3)
        npad, cmp, endt, texp = sb("npad", [P, E8]), sb("cmp", [P, E8, TILES]), sb("endt", [P, E8]), sb("texp", [P, 40])
        zero8, ones = sb("zero8", [P, P]), sb("ones", [P, P])
        xn = m.rows[:, 0, :, 0:D]
        ln.xn = xn
        second_copied = m.sem("rt_second")
        grid = sb("grid", [P, 40, E8])
        turned, ht_ready, logits_ready, counted = (m.sem("rt_" + n) for n in "turned ht logits counted".split())
        both_ready, exp_in, exp_out, pos_ready = (m.sem("rt_" + n) for n in "both exp_in exp_out pos".split())
        k = m.rt_chain
        s4 = L * NC4
        C = m.consts
        iota = C[:, C_I8:C_I8 + E8].unsqueeze(1).to_broadcast(S3)
        bc = lambda a: a.unsqueeze(2).to_broadcast(S3)
        f2 = lambda a: a.rearrange("p b e -> p (b e)")
        with nc.Block() as block:
            @block.tensor
            def _(pe):
                def turn(c):
                    ln.wait_chunk(pe, c)
                    for t4 in range(TPC):
                        mm = pe.transpose(m.bank[c][:, t4 * P:(t4 + 1) * P], xn[:, c * TPC + t4], C[:, C_ID:C_ID + P])
                    mm.then_inc(turned, 1)

                turn(0)
                for c in range(NC4):
                    if c + 1 < NC4:
                        turn(c + 1)
                    pe.wait_ge(ht_ready, s4 + c + 1)
                    for b in range(c * TPC, (c + 1) * TPC):
                        mm = pe.matmul(m.bank[4][:, b * E8:(b + 1) * E8], hT[:, b * P:(b + 1) * P], m.wr[L], start=True, stop=True)
                mm.then_inc(logits_ready, 1)
                pe.wait_ge(both_ready, 2 * L + 2)
                pe.matmul(m.bank[5][:, 0:P], C[:, C_UP:C_UP + P], f2(both[:]), start=True, stop=True)
                pe.matmul(m.bank[6][:, 0:P], ones[:], f2(both[:]), start=True, stop=True).then_inc(counted, 1)

            @block.scalar
            def _(act):
                ln.take_root(act)
                for c in range(NC4):
                    act.wait_ge(turned, s4 + c + 1)
                    act.activation(hT[:, c * CH:(c + 1) * CH], m.bank[c][:], ACT.Identity, bias=m.modc[:, 4 * L + 2:4 * L + 3],
                                   scale=m.modc[:, 4 * L + 3:4 * L + 4]).then_inc(ht_ready, 1)
                act.wait_ge(exp_in, L + 1)
                if L == 0:
                    act.activation(ex[:], dif[:], ACT.Exp).then_inc(exp_out, 1)
                else:
                    act.activation(f2(val[:]), f2(val[:]), ACT.Exp).then_inc(exp_out, 1)
                for c in range(NC4):
                    ln.wait_chunk(act, c)
                    act.copy(m.rows[:, 1, c * TPC:(c + 1) * TPC, 0:D], xn[:, c * TPC:(c + 1) * TPC]).then_inc(second_copied, 1)

            @block.vector
            def _(v):
                v.tensor_copy(m.rows[:, :, :, D], C[:, C_SL:C_SL + 2 * TILES].rearrange("p (i b) -> p i b", i=2)).then_inc(m.sem("rt_slots"), 1)
                ln.invert(v)
                for c in range(NC4):
                    ln.normalise(v, c)
                v.memset(ones[:], 1.).then_inc(both_ready, 1)
                v.memset(zero8[:], 0.).then_inc(k.sem, 1)
                v.wait_ge(logits_ready, L + 1)
                v.tensor_copy(f2(val[:]), m.bank[4][:, 0:P]).then_inc(k.sem, 1)
                v.wait_ge(k.sem, k.next(2))
                if L == 1:
                    v.tensor_reduce(m1[:], val[:], AX.X, ALU.max).then_inc(k.sem, 1)
                    v.wait_ge(k.sem, k.next())
                    v.tensor_tensor(val[:], val[:], bc(m1[:]), ALU.subtract).then_inc(exp_in, 2 - L)
                    v.wait_ge(exp_out, L + 1)
                    v.tensor_reduce(sm[:], val[:], AX.X, ALU.add).then_inc(k.sem, 1)
                    v.wait_ge(k.sem, k.next())
                    v.reciprocal(sm[:], sm[:]).then_inc(k.sem, 1)
                    v.wait_ge(k.sem, k.next())
                    v.tensor_tensor(val[:], val[:], bc(sm[:]), ALU.mult).then_inc(k.sem, 1)
                    v.wait_ge(k.sem, k.next())

                for src, top, oh in ((val, m1, oh1), (sel2, m2, oh2)):
                    v.tensor_reduce(top[:], src[:], AX.X, ALU.max).then_inc(k.sem, 1)
                    v.wait_ge(k.sem, k.next())
                    v.tensor_tensor(eq[:], src[:], bc(top[:]), ALU.is_ge).then_inc(k.sem, 1)
                    v.wait_ge(k.sem, k.next())
                    v.tensor_tensor(cand[:], eq[:], iota, ALU.mult).then_inc(k.sem, 1)
                    v.wait_ge(k.sem, k.next())
                    v.tensor_reduce(ix[:], cand[:], AX.X, ALU.min).then_inc(k.sem, 1)
                    v.wait_ge(k.sem, k.next())
                    v.tensor_tensor(oh[:], iota, bc(ix[:]), ALU.is_equal).then_inc(k.sem, 1)
                    v.wait_ge(k.sem, k.next())
                    if src is val:
                        v.scalar_tensor_tensor(f2(sel2[:]), f2(oh1[:]), NEG, f2(val[:]), ALU.mult, ALU.add).then_inc(k.sem, 1)
                        v.wait_ge(k.sem, k.next())
                v.tensor_tensor(both[:], oh1[:], oh2[:], ALU.add).then_inc(both_ready, 1)
                if L == 0:
                    v.tensor_tensor(dif[:], m2[:], m1[:], ALU.subtract).then_inc(exp_in, 1)
                    v.wait_ge(exp_out, 1)
                    v.tensor_scalar(sm[:], ex[:], 1., None, ALU.add).then_inc(k.sem, 1)
                    v.wait_ge(k.sem, k.next())
                    v.reciprocal(m.rows[:, 0, :, D + 1], sm[:]).then_inc(k.sem, 1)
                    v.wait_ge(k.sem, k.next())
                    v.tensor_tensor(m.rows[:, 1, :, D + 1], ex[:], m.rows[:, 0, :, D + 1], ALU.mult).then_inc(k.sem, 1)
                else:
                    v.tensor_tensor(sm[:], m1[:], m2[:], ALU.add).then_inc(k.sem, 1)
                    v.wait_ge(k.sem, k.next())
                    v.tensor_scalar(sm[:], sm[:], 1e-20, None, ALU.add).then_inc(k.sem, 1)
                    v.wait_ge(k.sem, k.next())
                    v.reciprocal(sm[:], sm[:]).then_inc(k.sem, 1)
                    v.wait_ge(k.sem, k.next())
                    v.tensor_tensor(m.rows[:, 0, :, D + 1], m1[:], sm[:], ALU.mult).then_inc(k.sem, 1)
                    v.wait_ge(k.sem, k.next())
                    v.tensor_tensor(m.rows[:, 1, :, D + 1], m2[:], sm[:], ALU.mult).then_inc(k.sem, 1)
                v.wait_ge(k.sem, k.next())
                v.wait_ge(counted, L + 1)
                v.tensor_copy(tot[:], m.bank[6][:, 0:P].rearrange("p (b e) -> p e b", e=E8)).then_inc(k.sem, 1)
                v.wait_ge(k.sem, k.next())
                v.tensor_tensor_scan(f2(run[:]), f2(tot[:]), zero8[:], 0., ALU.add, ALU.add).then_inc(k.sem, 1)
                v.wait_ge(k.sem, k.next())
                if L == 1:
                    v.tensor_reduce(npad[:], tot[:], AX.X, ALU.add).then_inc(k.sem, 1)
                    v.wait_ge(k.sem, k.next())
                    v.tensor_tensor(cmp[:], npad[:].unsqueeze(2).to_broadcast([P, E8, TILES]),
                                    C[:, C_TH:C_TH + TILES].unsqueeze(1).to_broadcast([P, E8, TILES]), ALU.is_gt).then_inc(k.sem, 1)
                    v.wait_ge(k.sem, k.next())
                    v.tensor_reduce(endt[:], cmp[:], AX.X, ALU.add).then_inc(k.sem, 1)
                    v.wait_ge(k.sem, k.next())
                    v.tensor_tensor_scan(texp[:, 0:E8], endt[:], zero8[:, 0:E8], 0., ALU.add, ALU.add).then_inc(k.sem, 1)
                    v.wait_ge(k.sem, k.next())
                    v.tensor_tensor(npad[:], texp[:, 0:E8], endt[:], ALU.subtract).then_inc(k.sem, 1)
                    v.tensor_tensor(grid[:], C[:, C_IT:C_IT + 40].unsqueeze(2).to_broadcast([P, 40, E8]),
                                    texp[:, 0:E8].unsqueeze(1).to_broadcast([P, 40, E8]), ALU.is_ge).then_inc(k.sem, 1)
                    v.wait_ge(k.sem, k.next(2))
                    v.tensor_scalar(npad[:], npad[:], float(P), None, ALU.mult).then_inc(k.sem, 1)
                    v.tensor_reduce(texp[:], grid[:], AX.X, ALU.add).then_inc(k.sem, 1)
                    v.wait_ge(k.sem, k.next(2))
                    v.tensor_scalar(m.tile_expert[:], texp[:], float(E8 - 1), None, ALU.min).then_inc(k.sem, 1)
                    v.tensor_tensor(endt[:], run[:, :, 0], tot[:, :, 0], ALU.subtract).then_inc(k.sem, 1)
                    v.wait_ge(k.sem, k.next(2))
                    v.tensor_tensor(npad[:], npad[:], endt[:], ALU.subtract).then_inc(k.sem, 1)
                    v.wait_ge(k.sem, k.next())
                    v.tensor_tensor(run[:], run[:], npad[:].unsqueeze(2).to_broadcast([P, E8, TILES]), ALU.add).then_inc(k.sem, 1)
                    v.wait_ge(k.sem, k.next())
                v.tensor_tensor(run[:], run[:], tot[:], ALU.subtract).then_inc(k.sem, 1)
                v.wait_ge(k.sem, k.next())
                v.tensor_tensor(rank[:], run[:].rearrange("p e b -> p b e"), m.bank[5][:, 0:P].rearrange("p (b e) -> p b e", e=E8),
                                ALU.add).then_inc(k.sem, 1)
                v.wait_ge(k.sem, k.next())
                for i, oh in enumerate((oh1, oh2)):
                    v.tensor_tensor(cand[:], oh[:], rank[:], ALU.mult).then_inc(k.sem, 1)
                    v.wait_ge(k.sem, k.next())
                    v.tensor_reduce(pf[:], cand[:], AX.X, ALU.add).then_inc(k.sem, 1)
                    v.wait_ge(k.sem, k.next())
                    v.tensor_copy(m.pos[:, i], pf[:]).then_inc(pos_ready, 1)
                    v.wait_ge(pos_ready, 2 * L + i + 1)

            if L == 0:
                @block.gpsimd
                def _(g):
                    scatter_rows(g, m, L, dram)


def scatter_rows(g, m, L, dram):
    pos_ready, scattered = m.sem("rt_pos"), m.sem("rt_scattered")
    for i in range(2):
        if i:
            g.wait_ge(m.sem("rt_second"), NC4 * (L + 1))
        g.wait_ge(pos_ready, 2 * L + i + 1)
        for b in range(TILES):
            g.indirect_dma_start(out=dram[f"perm{L}"], out_offset=bass.IndirectOffsetOnAxis(ap=m.pos[:, i, b:b + 1], axis=0),
                                 in_=m.rows[:, i, b], in_offset=None).then_inc(scattered, 16)
    g.wait_ge(scattered, (L + 1) * 32 * 16)


def experts0(nc, m, dram, w1, w2):
    with ExitStack() as ctx:
        sb = lambda name, s, d=F32: ctx.enter_context(nc.sbuf_tensor(f"{name}_f0", s, d))
        rows = [sb(f"rows{i}", [P, TPC, ROW]) for i in range(4)]
        slot = [sb(f"slot{i}", [P, TPC], U32) for i in range(2)]
        hT = [sb(f"hTf{i}", [P, CH]) for i in range(2)]
        hid = [sb(f"hid{i}", [P, TPC, CH]) for i in range(2)]
        eo = [sb(f"eo{i}", [P, TPC, D]) for i in range(2)]
        loaded, slot_ready, stored = [m.sem(f"f0_loaded{i}") for i in range(4)], m.sem("f0_slot"), [m.sem(f"f0_stored{i}") for i in range(2)]
        turned, ht_ready, up_ready, hid_ready, down_ready, eo_ready = (m.sem("f0_" + n) for n in "turned ht up hid down eo".split())
        FB = FF0 // P
        bank = m.bank
        view = lambda t, e: t.rearrange("(b p) d -> p b d", p=P)[:, e * TPC:(e + 1) * TPC]
        with nc.Block() as block:
            @block.sync
            def _(sp):
                for e in range(E8):
                    if e >= 4:
                        sp.wait_ge(eo_ready, (e - 3) * TPC)
                        sp.wait_ge(slot_ready, e - 3)
                    sp.dma_start(rows[e % 4][:], view(dram["perm0"], e)).then_inc(loaded[e % 4], 16)

            @block.gpsimd
            def _(g):
                for e in range(E8):
                    g.wait_ge(loaded[e % 4], 16 * (e // 4 + 1))
                    if e >= 2:
                        g.wait_ge(stored[e % 2], 16 * TPC * (e // 2))
                    g.tensor_copy(slot[e % 2][:], rows[e % 4][:, :, D]).then_inc(slot_ready, 1)
                    g.wait_ge(slot_ready, e + 1)
                    for t4 in range(TPC):
                        g.wait_ge(eo_ready, e * TPC + t4 + 1)
                        g.indirect_dma_start(out=dram["eo0"], out_offset=bass.IndirectOffsetOnAxis(ap=slot[e % 2][:, t4:t4 + 1], axis=0),
                                             in_=eo[e % 2][:, t4], in_offset=None).then_inc(stored[e % 2], 16)
                for i in range(2):
                    g.wait_ge(stored[i], 16 * TPC * E8 // 2)

            @block.tensor
            def _(pe):
                def turn(e):
                    pe.wait_ge(loaded[e % 4], 16 * (e // 4 + 1))
                    for t4 in range(TPC):
                        mm = pe.transpose(bank[e % 2][:, t4 * P:(t4 + 1) * P], rows[e % 4][:, t4, 0:D], m.consts[:, C_ID:C_ID + P])
                    mm.then_inc(turned, 1)

                turn(0)
                for e in range(E8):
                    pe.wait_ge(ht_ready, e + 1)
                    for f in range(FB):
                        if e:
                            pe.wait_ge(hid_ready, (e - 1) * FB + f + 1)
                        pe.matmul(bank[2 + f][:], w1[:, e, f * P:(f + 1) * P], hT[e % 2][:], start=True, stop=True).then_inc(up_ready, 1)
                    if e + 1 < E8:
                        turn(e + 1)
                    if e >= 2:
                        pe.wait_ge(eo_ready, (e - 1) * TPC)
                    for t4 in range(TPC):
                        for f in range(FB):
                            if t4 == 0:
                                pe.wait_ge(hid_ready, e * FB + f + 1)
                            mm = pe.matmul(bank[6 + e % 2][:, t4 * P:(t4 + 1) * P], hid[e % 2][:, f, t4 * P:(t4 + 1) * P], w2[:, e * FB + f],
                                           start=f == 0, stop=f == FB - 1)
                    mm.then_inc(down_ready, 1)

            @block.scalar
            def _(act):
                def modulate(e):
                    act.wait_ge(turned, e + 1)
                    act.activation(hT[e % 2][:], bank[e % 2][:], ACT.Identity, bias=m.modc[:, 2:3], scale=m.modc[:, 3:4]).then_inc(ht_ready, 1)

                modulate(0)
                for e in range(E8):
                    for f in range(FB):
                        if e >= 2 and f == 0:
                            act.wait_ge(down_ready, e - 1)
                        act.wait_ge(up_ready, e * FB + f + 1)
                        act.activation(hid[e % 2][:, f], bank[2 + f][:], ACT.Gelu).then_inc(hid_ready, 1)
                    if e + 1 < E8:
                        modulate(e + 1)

            @block.vector
            def _(v):
                for e in range(E8):
                    if e >= 2:
                        v.wait_ge(stored[e % 2], 16 * TPC * (e // 2))
                    v.wait_ge(down_ready, e + 1)
                    for t4 in range(TPC):
                        v.scalar_tensor_tensor(eo[e % 2][:, t4], bank[6 + e % 2][:, t4 * P:(t4 + 1) * P], rows[e % 4][:, t4, D + 1:D + 2],
                                               m.gates[:, 1], ALU.mult, ALU.mult).then_inc(eo_ready, 1)


BLOCKS1 = [(0, P), (P, P), (2 * P, FF1 - 2 * P)]


def shared_expert(nc, m, dram, gw, uw, dw):
    with ExitStack() as ctx:
        sb = lambda name, s, d=F32: ctx.enter_context(nc.sbuf_tensor(f"{name}_sh", s, d))
        sg = [sb(f"sg{i}", [P, CH]) for i in range(2)]
        hid = [sb(f"hid{i}", [P, 3, CH]) for i in range(2)]
        tmp = [sb(f"tmp{i}", [P, TPC, D]) for i in range(2)]
        gu_ready, silu_done, hid_ready, down_ready, tmp_ready, x_done = (m.sem("sh_" + n) for n in "gu silu hid down tmp x".split())
        bank, S = m.bank, E8
        with nc.Block() as block:
            @block.gpsimd
            def _(g):
                scatter_rows(g, m, 1, dram)

            @block.tensor
            def _(pe):
                def down(c):
                    if c >= 2:
                        pe.wait_ge(tmp_ready, c - 1)
                    pe.wait_ge(hid_ready, 3 * c + 3)
                    for t4 in range(TPC):
                        for f, (o, w) in enumerate(BLOCKS1):
                            mm = pe.matmul(bank[4 + c % 2][:, t4 * P:(t4 + 1) * P], hid[c % 2][0:w, f, t4 * P:(t4 + 1) * P],
                                           dw[0:w, S, f], start=f == 0, stop=f == 2)
                    mm.then_inc(down_ready, 1)

                for c in range(NC4):
                    for f, (o, w) in enumerate(BLOCKS1):
                        n = 3 * c + f
                        if n >= 2:
                            pe.wait_ge(hid_ready, n - 1)
                        for z, wt in enumerate((gw, uw)):
                            mm = pe.matmul(bank[2 * (n % 2) + z][0:w], wt[:, S, o:o + w], m.hT[:, c * CH:(c + 1) * CH], start=True, stop=True)
                        mm.then_inc(gu_ready, 1)
                    if c:
                        down(c - 1)
                down(NC4 - 1)

            @block.scalar
            def _(act):
                for n in range(3 * NC4):
                    w = BLOCKS1[n % 3][1]
                    if n >= 2:
                        act.wait_ge(hid_ready, n - 1)
                    act.wait_ge(gu_ready, n + 1)
                    act.activation(sg[n % 2][0:w], bank[2 * (n % 2)][0:w], ACT.Silu).then_inc(silu_done, 1)

            @block.vector
            def _(v):
                def finish(c):
                    v.wait_ge(down_ready, c + 1)
                    v.tensor_tensor(tmp[c % 2][:], bank[4 + c % 2][:].rearrange("p (b d) -> p b d", d=D),
                                    m.gates[:, 3:4, :].to_broadcast([P, TPC, D]), ALU.mult).then_inc(tmp_ready, 1)
                    v.wait_ge(tmp_ready, c + 1)
                    xs = m.x[:, c * TPC:(c + 1) * TPC]
                    v.tensor_tensor(xs, xs, tmp[c % 2][:], ALU.add).then_inc(x_done, 1)
                    v.wait_ge(x_done, c + 1)

                for n in range(3 * NC4):
                    c, f = divmod(n, 3)
                    w = BLOCKS1[f][1]
                    if c >= 2 and f == 0:
                        v.wait_ge(down_ready, c - 1)
                    v.wait_ge(silu_done, n + 1)
                    v.tensor_tensor(hid[c % 2][0:w, f], bank[2 * (n % 2) + 1][0:w], sg[n % 2][0:w], ALU.mult).then_inc(hid_ready, 1)
                    if f == 2 and c:
                        finish(c - 1)
                finish(NC4 - 1)


def experts1(nc, m, dram, gw, uw, dw):
    with ExitStack() as ctx:
        sb = lambda name, s, d=F32: ctx.enter_context(nc.sbuf_tensor(f"{name}_f1", s, d))
        rows = [sb(f"rows{i}", [P, ROW]) for i in range(4)]
        slot, weight = [sb(f"slot{i}", [P, 1], U32) for i in range(4)], [sb(f"weight{i}", [P, 1]) for i in range(4)]
        slot_ready, weight_ready, passed = m.sem("f1_slot"), m.sem("f1_weight"), m.sem("f1_passed")
        hT = [sb(f"hTt{i}", [P, P]) for i in range(2)]
        sg = [sb(f"sg{i}", [P, FF1]) for i in range(2)]
        hid = [sb(f"hid{i}", [P, FF1]) for i in range(2)]
        hidT = [sb(f"hidT{i}", [P, 3, P]) for i in range(2)]
        eo = [sb(f"eo{i}", [P, D]) for i in range(4)]
        loaded, stored = [m.sem(f"f1_loaded{i}") for i in range(4)], [m.sem(f"f1_stored{i}") for i in range(4)]
        (turned, ht_ready, gu_ready, silu_done, hid_ready, hid_turned, hidT_ready, down_ready, eo_ready) = (
            m.sem("f1_" + n) for n in "turned ht gu silu hid hid_turned hidT down eo".split())
        G, U, X, O = m.bank[0:2], m.bank[2:4], m.bank[4:6], m.bank[6:8]
        N, ident = RTILES1, m.consts[:, C_ID:C_ID + P]
        Q4 = ROWS1 // P // 4
        with nc.Block() as block:
            @block.sync
            def _(sp):
                def load(n, z, q):
                    sp.dma_start(rows[z][:], dram["perm1"][bass.ds(n * P, P)]).then_inc(loaded[z], 16)

                for n in range(4):
                    load(n, n, 0)
                for n in range(4):
                    sp.wait_ge(turned, n + 1)
                    sp.wait_ge(slot_ready, n + 1)
                    sp.wait_ge(weight_ready, n + 1)
                    load(n + 4, n, 1)
                with sp.Fori(1, Q4 - 2) as i:
                    for z in range(4):
                        sp.wait_ge(turned, 4 * i + z + 1)
                        sp.wait_ge(slot_ready, 4 * i + z + 1)
                        sp.wait_ge(weight_ready, 4 * i + z + 1)
                        load(4 * i + 4 + z, z, i + 1)
                for n in range(4 * Q4 - 8, N - 4):
                    sp.wait_ge(turned, n + 1)
                    sp.wait_ge(slot_ready, n + 1)
                    sp.wait_ge(weight_ready, n + 1)
                    load(n + 4, n % 4, n // 4 + 1)

            @block.gpsimd
            def _(g):
                def meta(z, q, reused=True):
                    if reused:
                        g.wait_ge(stored[z], 16 * q)
                    g.wait_ge(loaded[z], 16 * (q + 1))
                    g.sem_inc(passed, 1)
                    g.tensor_copy(slot[z][:], rows[z][:, D:D + 1]).then_inc(slot_ready, 1)
                    g.tensor_copy(weight[z][:], rows[z][:, D + 1:D + 2]).then_inc(weight_ready, 1)

                def store(n, z):
                    g.wait_ge(slot_ready, n + 1)
                    g.wait_ge(eo_ready, n + 1)
                    g.sem_inc(passed, 1)
                    g.indirect_dma_start(out=dram["eo1"], out_offset=bass.IndirectOffsetOnAxis(ap=slot[z][:, 0:1], axis=0),
                                         in_=eo[z][:], in_offset=None).then_inc(stored[z], 16)

                for z in range(2):
                    meta(z, 0, False)
                for n in range(4):
                    if n < 2:
                        meta(n + 2, 0, False)
                    else:
                        meta(n - 2, 1)
                    store(n, n)
                with g.Fori(1, Q4 - 1) as i:
                    for z in range(4):
                        meta((z + 2) % 4, i + (z + 2) // 4)
                        store(4 * i + z, z)
                for n in range(4 * Q4 - 4, N):
                    if n + 2 < N:
                        meta((n + 2) % 4, (n + 2) // 4)
                    store(n, n % 4)
                for z in range(4):
                    g.wait_ge(stored[z], 16 * (Q4 - (z >= N % 4)))

            @block.tensor
            def _(pe):
                expert = lambda n: pe.value_load(m.tile_expert[0:1, bass.ds(n, 1)], min_val=0, max_val=E8 - 1)

                def turn(z, q):
                    pe.wait_ge(loaded[z], 16 * (q + 1))
                    pe.transpose(X[z % 2][:, 0:P], rows[z][:, 0:D], ident).then_inc(turned, 1)

                def gate_up(n, z):
                    e = expert(n)
                    pe.wait_ge(ht_ready, n + 1)
                    pe.matmul(G[z % 2][:, 0:FF1], hT[z % 2][:], gw[:, bass.ds(e, 1), :], start=True, stop=True)
                    pe.matmul(U[z % 2][:, 0:FF1], hT[z % 2][:], uw[:, bass.ds(e, 1), :], start=True, stop=True).then_inc(gu_ready, 1)

                def turn_hidden(n, z, later=True):
                    if later:
                        pe.wait_ge(ht_ready, n + 3)
                    pe.wait_ge(hid_ready, n + 1)
                    for f, (o, w) in enumerate(BLOCKS1):
                        mm = pe.transpose(X[z % 2][0:w, (f + 1) * P:(f + 2) * P], hid[z % 2][:, o:o + w], ident)
                    mm.then_inc(hid_turned, 1)

                def down(n, z, reused=True):
                    e = expert(n)
                    if reused:
                        pe.wait_ge(eo_ready, n - 1)
                    pe.wait_ge(hidT_ready, n + 1)
                    for f, (o, w) in enumerate(BLOCKS1):
                        mm = pe.matmul(O[z % 2][:, 0:P], hidT[z % 2][0:w, f], dw[0:w, bass.ds(e, 1), f], start=f == 0, stop=f == 2)
                    mm.then_inc(down_ready, 1)

                turn(0, 0)
                turn(1, 0)
                gate_up(0, 0)
                for n in range(1, 5):
                    turn((n + 1) % 4, (n + 1) // 4)
                    gate_up(n, n % 4)
                    turn_hidden(n - 1, (n - 1) % 4)
                    if n >= 2:
                        down(n - 2, (n - 2) % 4, n >= 4)
                with pe.Fori(1, Q4 - 1) as i:
                    for z in range(1, 5):
                        turn((z + 1) % 4, i + (z + 1) // 4)
                        gate_up(4 * i + z, z % 4)
                        turn_hidden(4 * i + z - 1, (z - 1) % 4)
                        down(4 * i + z - 2, (z - 2) % 4)
                for n in range(4 * Q4 - 3, N):
                    if n + 1 < N:
                        turn((n + 1) % 4, (n + 1) // 4)
                    gate_up(n, n % 4)
                    turn_hidden(n - 1, (n - 1) % 4, n + 1 < N)
                    down(n - 2, (n - 2) % 4)
                turn_hidden(N - 1, (N - 1) % 4, False)
                down(N - 2, (N - 2) % 4)
                down(N - 1, (N - 1) % 4)

            @block.scalar
            def _(act):
                def modulate(n, z):
                    act.wait_ge(turned, n + 1)
                    act.activation(hT[z % 2][:], X[z % 2][:, 0:P], ACT.Identity, bias=m.modc[:, 6:7], scale=m.modc[:, 7:8]).then_inc(ht_ready, 1)

                def silu(n, z, reused=True):
                    if reused:
                        act.wait_ge(hid_ready, n - 1)
                    act.wait_ge(gu_ready, n + 1)
                    act.activation(sg[z % 2][:], G[z % 2][:, 0:FF1], ACT.Silu).then_inc(silu_done, 1)

                modulate(0, 0)
                for n in range(4):
                    modulate(n + 1, n + 1)
                    silu(n, n, n >= 2)
                with act.Fori(1, Q4 - 1) as i:
                    for z in range(4):
                        modulate(4 * i + z + 1, z + 1)
                        silu(4 * i + z, z)
                for n in range(4 * Q4 - 4, N):
                    if n + 1 < N:
                        modulate(n + 1, n + 1)
                    silu(n, n)

            @block.vector
            def _(v):
                def hidden(n, z):
                    v.wait_ge(silu_done, n + 1)
                    v.tensor_tensor(hid[z % 2][:], U[z % 2][:, 0:FF1], sg[z % 2][:], ALU.mult).then_inc(hid_ready, 1)

                def hidden_turned(n, z):
                    v.wait_ge(hid_turned, n + 1)
                    v.tensor_copy(hidT[z % 2][:], X[z % 2][:, P:4 * P].rearrange("p (f t) -> p f t", t=P)).then_inc(hidT_ready, 1)

                def finish(n, z, q, reused=True):
                    if reused:
                        v.wait_ge(stored[z % 4], 16 * q)
                    v.wait_ge(down_ready, n + 1)
                    v.wait_ge(weight_ready, n + 1)
                    v.scalar_tensor_tensor(eo[z % 4][:], O[z % 2][:, 0:P], weight[z % 4][:, 0:1], m.gates[:, 3], ALU.mult, ALU.mult).then_inc(eo_ready, 1)

                hidden(0, 0)
                for n in range(1, 6):
                    hidden(n, n)
                    hidden_turned(n - 1, n - 1)
                    if n >= 2:
                        finish(n - 2, n - 2, 0, False)
                with v.Fori(1, Q4 - 1) as i:
                    for z in range(2, 6):
                        hidden(4 * i + z, z)
                        hidden_turned(4 * i + z - 1, z - 1)
                        finish(4 * i + z - 2, z - 2, i)
                for n in range(4 * Q4 - 2, N):
                    hidden(n, n)
                    hidden_turned(n - 1, n - 1)
                    finish(n - 2, n - 2, (n - 2) // 4)
                hidden_turned(N - 1, N - 1)
                finish(N - 2, N - 2, (N - 2) // 4)
                finish(N - 1, N - 1, (N - 1) // 4)


def combine(nc, m, dram, out):
    with ExitStack() as ctx:
        got = ctx.enter_context(nc.sbuf_tensor("got_cb", [P, TILES, 2, D], F32))
        added, written = m.sem("cb_added"), m.sem("cb_written")
        with nc.Block() as block:
            @block.vector
            def _(v):
                for c in range(NC4):
                    add_rows(v, m, 1, c, got)

            @block.sync
            def _(sp):
                load_rows(sp, m, 1, dram, got)
                for c in range(NC4):
                    sp.wait_ge(added, (NC4 + c + 1) * 2)
                    sp.dma_start(out[0].rearrange("(b p) d -> p b d", p=P)[:, c * TPC:(c + 1) * TPC], m.x[:, c * TPC:(c + 1) * TPC]).then_inc(written, 16)
                sp.wait_ge(written, 16 * NC4)


class Memory:

    def __init__(self, nc, ctx):
        sb = lambda n, s, d=F32: ctx.enter_context(nc.sbuf_tensor(n, s, d))
        self.sems = {}
        self.new_sem = lambda n: ctx.enter_context(nc.semaphore(n))
        self.x, self.vall = sb("x", [P, TILES, D]), sb("vall", [P, TILES, D])
        self.QS = [sb(f"qs{p}", [P, GH, T], BF) for p in range(2)]
        self.KS = [sb(f"ks{p}", [P, GH, T], BF) for p in range(2)]
        self.VS = [sb(f"vs{p}", [P, TILES, GH, 32]) for p in range(2)]
        self.pack, self.lpack = sb("pack_sb", [P, W_PACK]), sb("lpack_sb", [LAT, 2 * D + 2])
        at = {}
        o = 0
        for name, w in PACK:
            at[name], o = self.pack[:, o:o + w], o + w
        self.consts, self.wq, self.wdkv = at["consts"], at["wq0"], at["wdkv"]
        self.wo, self.wr = [at["wo0"], at["wo1"]], [at["wr0"], at["wr1"]]
        self.w1small = at["w1small"].rearrange("p (i e) -> p i e", e=HD)
        self.wuk, self.wuv, self.lngb = self.lpack[:, 0:D], self.lpack[:, D:2 * D], self.lpack[:, 2 * D:2 * D + 2]
        self.identb, self.maskTb, self.maskN = sb("identb", [P, P], BF), sb("maskTb", [P, P], BF), sb("maskN", [P, CH])
        self.wqr, self.wukr, self.w1bd = sb("wqr", [P, D]), sb("wukr", [LAT, D]), sb("w1bd", [P, 3, D])
        self.modc, self.gates = sb("modc", [P, 8]), sb("gates", [P, 4, D])
        self.pos = sb("pos", [P, 2, TILES], U32)
        self.tile_expert = sb("tile_expert", [P, 40], I32)
        self.st = [ctx.enter_context(nc.psum_tensor(f"st{i}", [P, 2, CH], F32)) for i in range(2)]
        self.mxb = [ctx.enter_context(nc.psum_tensor(f"mx{i}", [P, CH], F32)) for i in range(MXBUF)]
        self.avb = ctx.enter_context(nc.psum_tensor("av", [P, CH], F32))
        self.bank = [self.st[0][:, 0], self.st[0][:, 1], self.st[1][:, 0], self.st[1][:, 1]] + [b[:] for b in self.mxb] + [self.avb[:]]
        self.ln_chain, self.pj_chain, self.rt_chain = (Count(self.sem(n)) for n in ("ln_chain", "pj_chain", "rt_chain"))
        self.weights_total = 0

    def sem(self, name):
        if name not in self.sems:
            self.sems[name] = self.new_sem(name)
        return self.sems[name]


def adaln_two_layers(nc, *aps):
    dram = dict(zip(INPUTS, aps))
    out = aps[-1]
    for L in range(2):
        for key in ("q_parts", "k_parts"):
            dram[f"{key}{L}"] = nc.dram_tensor(f"{key}{L}", [H * 3 * HD, T], BF).ap()
        dram[f"perm{L}"] = nc.dram_tensor(f"perm{L}", [(ROWS0, ROWS1)[L], ROW], F32).ap()
        dram[f"eo{L}"] = nc.dram_tensor(f"eo{L}", [2 * T + (0, ROWS1)[L], D], F32).ap()
    with ExitStack() as ctx:
        m = Memory(nc, ctx)
        with ExitStack() as tables:
            m.cosT, m.sinT = (tables.enter_context(nc.sbuf_tensor(n, [P, T], F32)) for n in ("cosT", "sinT"))
            setup(nc, m, dram)
            project(nc, m, 0, dram)
        for L in range(2):
            if L:
                project(nc, m, 1, dram)
            with ExitStack() as wctx:
                sb = lambda n, s: wctx.enter_context(nc.sbuf_tensor(n, s, F32))
                if L == 0:
                    w1, w2 = sb("w1_sb", [P, E8, FF0]), sb("w2_sb", [P, E8 * FF0 // P, D])
                    weight_loads = [(w1[:, e], dram["w1"][e]) for e in range(E8)] + [
                        (w2[:, 4 * e:4 * e + 4], dram["w2"][e].rearrange("(k p) d -> p k d", p=P)) for e in range(E8)] + [
                        (dram["perm1"].rearrange("(p r) d -> p (r d)", p=P), dram["pad"].rearrange("(p r) d -> p (r d)", p=P))]
                else:
                    gw, uw, dw = sb("gw_sb", [P, E8 + 1, FF1]), sb("uw_sb", [P, E8 + 1, FF1]), sb("dw_sb", [P, E8 + 1, 3, D])
                    weight_loads = [(dst[:, 3 * z:3 * z + 3], dram[key][:, 3 * z:3 * z + 3])
                                    for z in range(3) for dst, key in ((gw, "gw"), (uw, "uw"), (dw, "dw"))]
                m.weights_total += len(weight_loads)
                ln = LayerNorm(nc, wctx, m, 2 * L + 1, None)
                attention(nc, m, L, dram, weight_loads, ln)
                m.hT = wctx.enter_context(nc.sbuf_tensor(f"hT{L}", [P, T], F32))
                m.rows = wctx.enter_context(nc.sbuf_tensor(f"rows{L}", [P, 2, TILES, ROW], F32))
                route(nc, m, L, dram, ln)
                if L == 0:
                    experts0(nc, m, dram, w1, w2)
                else:
                    shared_expert(nc, m, dram, gw, uw, dw)
                    experts1(nc, m, dram, gw, uw, dw)
        combine(nc, m, dram, out)


INPUTS = ["x", "mod", "pack", "lpack", "cos", "sin", "zo", "zrow", "pad", "w1", "w2", "gw", "uw", "dw"]


def layout(i):
    a = {k: np.asarray(v) for k, v in i.items()}
    q = np.arange(P)
    consts = np.zeros((P, C_W), np.float32)
    consts[:, C_ID:C_ID + P] = np.eye(P)
    consts[:, C_MN:C_MN + P] = np.where(q[None, :] <= q[:, None], 0, NEG)
    consts[:, C_MT:C_MT + P] = np.where(q[:, None] <= q[None, :], 0, NEG)
    consts[:, C_UP:C_UP + P] = q[:, None] < q[None, :]
    consts[:, C_BD:C_BD + P] = q[:, None] // HD == q[None, :] // HD
    consts[:, C_I8:C_I8 + E8] = np.arange(E8) - E8
    consts[:, C_IT:C_IT + 40] = np.arange(40)
    consts[:, C_TH:C_TH + TILES] = P * np.arange(TILES)
    consts[:, C_SL:C_SL + 2 * TILES] = (2 * (P * np.arange(TILES)[None, None, :] + q[:, None, None]) + np.arange(2)[None, :, None]).reshape(P, -1)
    pad = np.zeros((ROWS1, ROW), np.float32)
    pad[:, D] = 2 * T + np.arange(ROWS1)
    half = HD // 2
    inv = (np.float32(1.0) / np.float32(10000.0) ** (np.arange(half, dtype=np.float32) / np.float32(half))).astype(np.float32)
    ang = (np.arange(T, dtype=np.float32)[None, :] * inv[:, None]).astype(np.float32)
    ones = np.zeros((GH, 2 * GH, T), np.dtype("bfloat16"))
    for j in range(GH):
        ones[j, 2 * j:2 * j + 2] = 1
    dw = np.zeros((E8 + 1, 3 * P, D), np.float32)
    dw[:E8, :FF1] = a["L1_ffn_expert_down"].transpose(0, 2, 1)
    dw[E8, :FF1] = a["L1_ffn_shared_down"].T
    both = lambda e, s: np.concatenate([a[e], a[s][None]]).transpose(2, 0, 1)
    heads = [a[f"L1_attn_{n}"].reshape(P, HD) for n in ("Wq", "Wk", "Wv")]
    return {
        "x": a["L0_attn_x"][0], "cos": np.cos(ang).astype(np.float32), "sin": np.sin(ang).astype(np.float32),
        "zo": ones, "zrow": np.zeros((2 * GH, T), np.dtype("bfloat16")), "pad": pad,
        "mod": np.concatenate([a["L0_c"].T, a["L1_c"].T, a["L0_wmod"], a["L1_wmod"]], 1),
        "pack": np.concatenate([consts, a["L0_attn_W_q"], a["L0_attn_W_dkv"], a["L0_attn_W_o"], a["L1_attn_Wo"],
                                a["L0_ffn_Wr"].T, a["L1_ffn_gate_w"].T] + heads, 1),
        "lpack": np.concatenate([a["L0_attn_W_uk"], a["L0_attn_W_uv"], a["L0_attn_ln_gamma"][:, None], a["L0_attn_ln_beta"][:, None]], 1),
        "w1": a["L0_ffn_W1"], "w2": a["L0_ffn_W2"],
        "gw": both("L1_ffn_expert_gate", "L1_ffn_shared_gate"), "uw": both("L1_ffn_expert_up", "L1_ffn_shared_up"),
        "dw": dw.reshape(E8 + 1, 3, P, D).transpose(2, 0, 1, 3)}


def kernel(**inputs):
    import concourse.bacc as bacc
    from concourse.bass_utils import run_bass_kernel_spmd

    nc = bacc.Bacc("TRN2", target_bir_lowering=False, num_devices=1)
    arrays, args = {}, []
    laid = layout(inputs)
    for name in INPUTS:
        a = np.ascontiguousarray(laid[name])
        arrays[f"in_{name}_dram"] = a
        args.append(nc.dram_tensor(f"in_{name}_dram", a.shape, mybir.dt.from_np(a.dtype), kind="ExternalInput").ap())
    args.append(nc.dram_tensor("out_0_dram", (1, T, D), F32, kind="ExternalOutput").ap())
    adaln_two_layers(nc, *args)
    r = run_bass_kernel_spmd(nc, [arrays], core_ids=[0])
    return r.results[0]["out_0_dram"]
```
